# Optimizing a Trainium2 kernel written in Bass

```python
import numpy as np
import jax
import jax.numpy as jnp

def _softmax(x, axis=-1):
    return jax.nn.softmax(x, axis=axis)

def _gelu(x):
    return jax.nn.gelu(x, approximate=True)

def _silu(x):
    return jax.nn.silu(x)

def _sigmoid(x):
    return jax.nn.sigmoid(x)

def _layernorm(x, axis=-1, eps=1e-05):
    m = jnp.mean(x, axis=axis, keepdims=True)
    v = jnp.var(x, axis=axis, keepdims=True)
    return (x - m) / jnp.sqrt(v + eps)

def _scatter_add(tgt, idx, src, axis=0):
    return tgt.at[idx].add(src)

def _segment_sum(src, seg, n):
    return jax.ops.segment_sum(src, seg, n)
kernel_name = 'mk_gnn_ffn_d1_gnn_r8_256db6'

def setup_inputs(seed: int=0):
    np.random.seed(seed)
    _w = jnp.asarray

    def _rec_inputs():
        import jax
        import jax.numpy as jnp
        _gk = jax.random.key(seed)
        x = -8.776e-05 + 1 * jax.random.normal(jax.random.fold_in(_gk, 1), (2500, 256), jnp.float32)
        src = jax.random.randint(jax.random.fold_in(_gk, 2), (80000,), 0, 2500, jnp.int32)
        dst = jax.random.randint(jax.random.fold_in(_gk, 3), (80000,), 0, 2500, jnp.int32)
        _o = jnp.argsort(dst, stable=True)
        src = src[_o]
        dst = dst[_o]
        return (x, src, dst)
    x, src, dst = _rec_inputs()

    def _L0_gnn_setup():
        import jax, jax.numpy as jnp
        import numpy as np
        N = 2500
        E = 80000
        F_IN = 256
        H = 4
        F_OUT = 64
        NEG_SLOPE = 0.2
        key = jax.random.key(seed)
        k = jax.random.split(key, 6)
        x = jax.random.normal(k[0], (N, F_IN), jnp.float32)
        edge_src = jax.random.randint(k[1], (E,), 0, N, jnp.int32)
        edge_dst = jax.random.randint(k[2], (E,), 0, N, jnp.int32)
        W = jax.random.normal(k[3], (H, F_IN, F_OUT), jnp.float32) * (1.0 / np.sqrt(F_IN))
        a_src = jax.random.normal(k[4], (H, F_OUT), jnp.float32) * 0.1
        a_dst = jax.random.normal(k[5], (H, F_OUT), jnp.float32) * 0.1
        return {'x': x, 'edge_src': edge_src, 'edge_dst': edge_dst, 'W': W, 'a_src': a_src, 'a_dst': a_dst}
    _L0_gnn_all = _L0_gnn_setup()
    _L0_gnn_in = {k: v for k, v in _L0_gnn_all.items() if k in ('W', 'a_src', 'a_dst')}
    del _L0_gnn_all

    def _L0_ffn_setup():
        import jax, jax.numpy as jnp
        import numpy as np
        E = 8
        K = 2
        D = 256
        H = 512
        DOUT = 256
        EPS = 1e-05
        key = jax.random.key(seed)
        ks = jax.random.split(key, 9)
        s = 0.02
        return {'x': jax.random.normal(ks[0], (4, 1024, D), jnp.float32), 'gamma': 1.0 + 0.05 * jax.random.normal(ks[1], (D,), jnp.float32), 'beta': 0.05 * jax.random.normal(ks[2], (D,), jnp.float32), 'Wr': 0.01 * jax.random.normal(ks[3], (D, E), jnp.float32), 'br': jnp.zeros((E,), jnp.float32), 'W1': s * jax.random.normal(ks[4], (E, D, H), jnp.float32), 'b1': s * jax.random.normal(ks[5], (E, H), jnp.float32), 'W2': s * jax.random.normal(ks[6], (E, H, DOUT), jnp.float32), 'b2': s * jax.random.normal(ks[7], (E, DOUT), jnp.float32)}
    _L0_ffn_all = _L0_ffn_setup()
    _L0_ffn_in = {k: v for k, v in _L0_ffn_all.items() if k in ('gamma', 'beta', 'Wr', 'br', 'W1', 'b1', 'W2', 'b2')}
    del _L0_ffn_all
    return {'x': x, 'src': src, 'dst': dst, 'L0_gnn_W': _L0_gnn_in['W'], 'L0_gnn_a_src': _L0_gnn_in['a_src'], 'L0_gnn_a_dst': _L0_gnn_in['a_dst'], 'L0_ffn_gamma': _L0_ffn_in['gamma'], 'L0_ffn_beta': _L0_ffn_in['beta'], 'L0_ffn_Wr': _L0_ffn_in['Wr'], 'L0_ffn_br': _L0_ffn_in['br'], 'L0_ffn_W1': _L0_ffn_in['W1'], 'L0_ffn_b1': _L0_ffn_in['b1'], 'L0_ffn_W2': _L0_ffn_in['W2'], 'L0_ffn_b2': _L0_ffn_in['b2']}

def reference(x, src, dst, L0_gnn_W, L0_gnn_a_src, L0_gnn_a_dst, L0_ffn_gamma, L0_ffn_beta, L0_ffn_Wr, L0_ffn_br, L0_ffn_W1, L0_ffn_b1, L0_ffn_W2, L0_ffn_b2):
    import jax
    import jax.numpy as jnp

    def _L0_gnn_ref(x, edge_src, edge_dst, W, a_src, a_dst):
        import jax, jax.numpy as jnp
        import numpy as np
        N = 2500
        E = 80000
        F_IN = 256
        H = 4
        F_OUT = 64
        NEG_SLOPE = 0.2
        h = jnp.einsum('nf,hfo->nho', x, W)
        e_s = jnp.einsum('nho,ho->nh', h, a_src)
        e_d = jnp.einsum('nho,ho->nh', h, a_dst)
        scores = jax.nn.leaky_relu(e_s[edge_src] + e_d[edge_dst], NEG_SLOPE)
        m = jax.ops.segment_max(scores, edge_dst, num_segments=N)
        m = jnp.where(jnp.isfinite(m), m, 0.0)
        ex = jnp.exp(scores - m[edge_dst])
        denom = jax.ops.segment_sum(ex, edge_dst, num_segments=N)
        alpha = ex / jnp.maximum(denom[edge_dst], 1e-09)
        msg = alpha[:, :, None] * h[edge_src]
        agg = jax.ops.segment_sum(msg, edge_dst, num_segments=N)
        return jax.nn.relu(agg).reshape(N, H * F_OUT)

    def _L0_ffn_ref(x, gamma, beta, Wr, br, W1, b1, W2, b2):
        import jax, jax.numpy as jnp
        import numpy as np
        E = 8
        K = 2
        D = 256
        H = 512
        DOUT = 256
        EPS = 1e-05
        mu = jnp.mean(x, axis=-1, keepdims=True)
        var = jnp.mean(jnp.square(x - mu), axis=-1, keepdims=True)
        xn = (x - mu) * jax.lax.rsqrt(var + EPS) * gamma + beta
        logits = jnp.einsum('bsd,de->bse', xn, Wr) + br
        top_vals, top_idx = jax.lax.top_k(logits, K)
        w = jax.nn.softmax(top_vals, axis=-1)
        w_full = jnp.einsum('bsk,bske->bse', w, jax.nn.one_hot(top_idx, E, dtype=w.dtype))
        y = jnp.zeros(x.shape[:-1] + (DOUT,), x.dtype)
        for e in range(E):
            h = jax.nn.gelu(jnp.einsum('bsd,dh->bsh', xn, W1[e]) + b1[e], approximate=False)
            y_e = jnp.einsum('bsh,hd->bsd', h, W2[e]) + b2[e]
            y = y + y_e * w_full[..., e, None]
        return y
    x = x + _L0_gnn_ref(_layernorm(x, axis=-1), src, dst, L0_gnn_W, L0_gnn_a_src, L0_gnn_a_dst)
    x = x + _L0_ffn_ref(_layernorm(x, axis=-1)[None], L0_ffn_gamma, L0_ffn_beta, L0_ffn_Wr, L0_ffn_br, L0_ffn_W1, L0_ffn_b1, L0_ffn_W2, L0_ffn_b2)[0]
    return x

_drawn_inputs = setup_inputs


def setup_inputs(seed=0):
    import zlib

    import numpy as np

    out = dict(_drawn_inputs(seed))
    spreads = {'L0_ffn_br': (0.0, 0.1)}
    factors = {'L0_ffn_gamma': 5.929, 'L0_ffn_beta': 4.756, 'L0_ffn_b1': 8.0, 'L0_ffn_b2': 4.279}
    for name, (base, spread) in spreads.items():
        noise = np.random.default_rng([zlib.crc32(name.encode()), seed]).standard_normal(out[name].shape)
        drawn = base * np.exp(spread * noise) if base else spread * noise
        out[name] = jnp.asarray(drawn.astype(out[name].dtype))
    for name, factor in factors.items():
        out[name] = (out[name] * factor).astype(out[name].dtype)
    return out
```

```python
import concourse.bass as bass
from concourse import mybir
from contextlib import ExitStack


class Chain:

    def __init__(self, eng, sem):
        self.eng, self.sem, self.done, self.trip, self.per_trip, self.base = eng, sem, 0, 0, 0, 0

    def link(self, ins):
        self.done += 1
        ins.then_inc(self.sem, 1)
        self.eng.wait_ge(self.sem, self.done + self.trip * self.per_trip)

    def enter(self, trip, per_trip):
        self.trip, self.per_trip, self.base = trip, per_trip, self.done

    def leave(self, trips):
        assert self.done - self.base == self.per_trip, (self.done - self.base, self.per_trip)
        self.done = self.base + trips * self.per_trip
        self.trip, self.per_trip = 0, 0


def gat_moe_kernel(nc, x, src, dst, gnn_w, a_src, a_dst, gamma, beta, wr, br, w1, b1, w2, b2, out):
    fp32, bf16, i32, u32 = mybir.dt.float32, mybir.dt.bfloat16, mybir.dt.int32, mybir.dt.uint32
    ALU = mybir.AluOpType
    ACT = mybir.ActivationFunctionType
    AX = mybir.AxisListType
    P = 128

    N, F = x.shape
    H, _, FO = gnn_w.shape
    HF = H * FO
    KF = F // P
    E = src.shape[0]
    TPR = 5
    RL = TPR * P
    Q = E // RL
    assert Q * RL == E and Q <= P
    NB = (N + P - 1) // P
    LASTB = N - (NB - 1) * P
    G = Q + NB - 1
    RING = 25
    assert Q % RING == 0 and RING >= NB + TPR
    MW = HF + H
    NE, _, HID = w1.shape
    FC = HID // P
    BS = 256
    BM = BS // P
    TOP = 2
    NBLK = (TOP * N + NE * (BS - 1)) // BS
    EG = (N + BS - 1) // BS
    BIG = 1e38
    EPS = 1e-5

    h_tab = nc.dram_tensor("h_tab", (NB * P, HF), fp32).ap()
    lo_tab = nc.dram_tensor("lo_tab", (Q, RL), bf16).ap()
    dst_tab = nc.dram_tensor("dst_tab", (Q, RL), fp32).ap()
    ed_tab = nc.dram_tensor("ed_tab", (E + NB * P, H), fp32).ap()
    xs_tab = nc.dram_tensor("xs_tab", (NBLK * BS, F), fp32).ap()
    ys_tab = nc.dram_tensor("ys_tab", (NBLK * BS, F), fp32).ap()
    ed_rows = ed_tab[0:E, :].rearrange("(q j) h -> q (j h)", q=Q)
    src_rows = src.rearrange("(q j) -> q j", q=Q)
    dst_rows = dst.rearrange("(q j) -> q j", q=Q)

    ctx = ExitStack()
    with ctx:
        def sb(name, shape, dt=fp32):
            return ctx.enter_context(nc.sbuf_tensor(name, shape, dt))

        def sem(name):
            return ctx.enter_context(nc.semaphore(name))

        bank = [ctx.enter_context(nc.psum_tensor(f"bank{i}", [P, 512], fp32)) for i in range(8)]

        ring = sb("ring", [P, RING, TPR, MW])
        ring_flat = ring[:, :, :, :].rearrange("p s r w -> p (s r w)")
        used = [0]

        def early(width, dt=fp32):
            a = ring_flat[:, used[0]:used[0] + width]
            used[0] += width
            return a if dt == fp32 else a.bitcast(dt)

        xs0 = early(NB * F).rearrange("p (b f) -> p b f", b=NB)
        xn0 = early(2 * F).rearrange("p (u f) -> p u f", u=2)
        xT0 = early(2 * F).rearrange("p (u k n) -> p u k n", u=2, k=KF)
        h_stage = early(2 * HF).rearrange("p (u f) -> p u f", u=2)
        wide = HF + 2 * H
        w_ext = early(KF * wide).rearrange("p (k w) -> p k w", k=KF)
        a_bc = early(2 * HF).rearrange("p (s f) -> p s f", s=2)
        w_tmp = early(2 * HF).rearrange("p (s f) -> p s f", s=2)
        q_tmp = early(NB * Q).rearrange("p (b q) -> p b q", b=NB)
        path_tmp = early(G * (NB - 1)).rearrange("p (g b) -> p g b", b=NB - 1)
        src_f = early(RL)
        lo_i = early(RL, i32)
        lo_b = early(RL // 2, bf16)
        hi_i = early(Q * TPR, i32)
        diag = early(Q)
        src_i = early(RL, i32)
        dst_i = early(RL + 2, i32)
        zeros = early(RL * H)
        ROWBUF = 4
        drow = early(ROWBUF * RL).rearrange("p (u j) -> p u j", u=ROWBUF)
        dst_f = early(RL + 2)
        shift = early(P)
        corner = early(P)
        st0 = early(NB * 6).rearrange("p (b s) -> p b s", s=6)
        mean, rstd, sm1, sm2, qn, node_id = (early(NB) for _ in range(6))
        qi, spos = early(NB, i32), early(NB, i32)
        start = early(NB + 1)
        coef = early(3 * H)
        enters = early(NB - 1)
        iota_g = early(G)
        slot_f, path_f = early(G)[0:1, :], early(G)[0:1, :]
        assert used[0] <= RING * TPR * MW, used

        keep = sb("keep", [P, RL + 1])
        reset = sb("reset", [P, RL + 1])
        srcA = sb("srcA", [P, Q + 1, TPR], i32)
        dstA = sb("dstA", [P, Q, TPR])
        hiA = sb("hiA", [P, Q, TPR], bf16)
        exA = sb("exA", [P, Q, TPR, H])
        esB = sb("esB", [P, H, RL])
        edB = sb("edB", [P, RL, H])
        OHS = 5
        shared = sb("shared", [P, OHS * RL])
        half = OHS * RL // 2
        lo_bc = shared[:, 0:half].bitcast(bf16).rearrange("p (u j) -> p u j", u=OHS)
        lo_oh = shared[:, half:2 * half].bitcast(bf16).rearrange("p (u j) -> p u j", u=OHS)
        bwdB = shared[:, 0:H * RL].rearrange("p (h j) -> p h j", h=H)
        dst_oh = shared[:, :].rearrange("p (u r d) -> p u r d", u=OHS, r=TPR)
        hi_oh = sb("hi_oh", [P, TPR, NB], bf16)
        acc = sb("acc", [P, NB, MW])
        acc_flat = acc[:, :, :].rearrange("p b w -> p (b w)")
        mxB = acc_flat[:, 0:H * RL].rearrange("p (h j) -> p h j", h=H)
        after = H * RL + TPR * H * NB
        coef_row = acc_flat[0:H, after:after + 3 * Q].rearrange("h (n q) -> h n q", n=3)
        carry_row = acc_flat[0:H, after + 3 * Q:after + 4 * Q + 1]
        carry = acc_flat[:, after + 4 * Q + 1:after + 4 * Q + 1 + H]
        es_sel = acc_flat[:, H * RL:H * RL + TPR * H * NB].rearrange("p (a b) -> p a b", b=NB)

        ident = sb("ident", [P, P])
        ones = sb("ones", [P, P])
        iota_f = sb("iota_f", [P, P])
        pcol = sb("pcol", [P, 1])
        e_node = sb("e_node", [P, NB, 2 * H])
        t3 = sb("t3", [P, 3, H, NB], bf16)
        beta_f = sb("beta_f", [P, G])
        t_res = sb("t_res", [P, H, NB])
        beta_i = sb("beta_i", [1, G], i32)
        tau_i = sb("tau_i", [1, G], i32)
        slot_i = sb("slot_i", [1, G], i32)
        ring_slot = sb("ring_slot", [1, Q], i32)
        picks = sb("picks", [P, RING, TPR], i32)

        edB_flat = edB[:, :, :].rearrange("p j h -> p (j h)")
        gamma_bc, beta_bc = edB_flat[:, 0:F], edB_flat[:, F:2 * F]
        wr_sb = edB_flat[:, 2 * F:2 * F + KF * NE].rearrange("p (k e) -> p k e", k=KF)
        at = 2 * F + KF * NE
        br_bc = edB_flat[:, at:at + NE]
        b1_rows = edB_flat[0:NE * FC, at + NE:at + NE + P]
        b1_T = edB_flat[:, at + NE + P:at + NE + P + NE * FC]
        at += NE + P + NE * FC
        zero_width = NBLK * BS * F // P // 9
        zero_src = edB_flat[:, 2 * F * KF:2 * F * KF + zero_width]
        assert zero_width * 9 * P == NBLK * BS * F and at <= 2 * F * KF
        assert 2 * F * KF + zero_width <= RL * H
        b2_bc = esB[:, :, :].rearrange("p h j -> p (h j)")[:, 0:NE * F].rearrange("p (e f) -> p e f", e=NE)
        used[0] = 0
        late = early
        xn1 = late(NB * F).rearrange("p (b f) -> p b f", b=NB)
        xn_u = late(2 * F).rearrange("p (u f) -> p u f", u=2)
        st1 = late(NB * 6).rearrange("p (b s) -> p b s", s=6)
        mean1, rstd1, tmp1, tmp2, top1, top2, w_a, w_b, valid = (late(NB) for _ in range(9))
        rden = late(NB * H).rearrange("p (b h) -> p b h", h=H)
        xT1 = late(2 * F).rearrange("p (u k n) -> p u k n", u=2, k=KF)
        upper = late(P)
        lg, eq, oh_a, oh_b, mask, pos_e, rank, tot = (
            late(NB * NE).rearrange("p (b e) -> p b e", e=NE) for _ in range(8))
        incl = late(NE * NB).rearrange("p (e b) -> p e b", e=NE)
        carry_on = late(NE * NB).rearrange("p (e b) -> p e b", e=NE)
        e_less = late(NE)
        gran = late(EG)
        n_blk, n_incl, n_excl = late(NE), late(NE), late(NE)
        n_cmp = late(NE * EG).rearrange("p (e g) -> p e g", e=NE)
        blk_cmp = late(NBLK * (NE - 1)).rearrange("p (j e) -> p j e", j=NBLK)
        blk_f = late(NBLK)
        blk_e = late(NBLK, i32)[0:1, :]
        pos_i = late(TOP * NB, i32).rearrange("p (k b) -> p k b", k=TOP)
        w1_all = late(NE * KF * HID).rearrange("p (e w) -> p e w", e=NE)
        w2_flat = late(NE * FC * F)
        w2_all = w2_flat.rearrange("p (e c f) -> p e c f", e=NE, c=FC)
        W2_FIRST = (NE * FC * F - NB * F) // (FC * F)
        x_again = w2_flat[:, NE * FC * F - NB * F:].rearrange("p (b f) -> p b f", b=NB)
        w1_now = late(2 * KF * HID).rearrange("p (u k h) -> p u k h", u=2, k=KF)
        xs_in = late(2 * BM * F).rearrange("p (u m f) -> p u m f", u=2, m=BM)
        xsT = late(2 * KF * BS).rearrange("p (u k n) -> p u k n", u=2, k=KF)
        hT = exA[:, :, :, :].rearrange("p q r h -> p (q r h)")[:, 0:2 * FC * BS]\
            .rearrange("p (u c n) -> p u c n", u=2, c=FC)
        y_out = shared[:, 0:2 * BM * F].rearrange("p (u m f) -> p u m f", u=2, m=BM)
        YS = 4
        y_in = shared[:, 2 * BM * F:(2 * BM + YS * TOP) * F]\
            .rearrange("p (u k f) -> p u k f", u=YS, k=TOP)
        assert used[0] <= RING * TPR * MW, used

        s_const = sem("s_const")
        s_pool = sem("s_pool")
        s_dve = sem("s_dve")
        x_in, w_in, a_in, src_in, dst_in = (sem(n) for n in ("x_in", "w_in", "a_in", "src_in", "dst_in"))
        pads_set = sem("pads_set")
        edges_f, edges_T, edges_A = sem("edges_f"), sem("edges_T"), sem("edges_A")
        lo_ready, lo_stored = sem("lo_ready"), sem("lo_stored")
        dst_stored = sem("dst_stored")
        row_diag, row_ends, q_ready = sem("row_diag"), sem("row_ends"), sem("q_ready")
        rows_got = [sem(f"rows_got{u}") for u in range(ROWBUF)]
        rows_used = sem("rows_used")
        var_ready, std_ready = sem("var_ready"), sem("std_ready")
        wext_ready = sem("wext_ready")
        xn_ready, xT_done, xT_copied, h_done, h_copied = (
            sem(n) for n in ("xn_ready", "xT_done", "xT_copied", "h_done", "h_copied"))
        h_stored = [sem(f"h_stored{u}") for u in range(2)]
        start_ready, next_done, spos_ready = sem("start_ready"), sem("next_done"), sem("spos_ready")
        zeros_set, ed_zeroed, ed_put, ed_in = (
            sem(n) for n in ("zeros_set", "ed_zeroed", "ed_put", "ed_in"))
        lo_in = [sem(f"lo_in{u}") for u in range(OHS)]
        lo_oh_ready, es_done, es_picked = sem("lo_oh_ready"), sem("es_done"), sem("es_picked")
        esT_done, esB_copied = sem("esT_done"), sem("esB_copied")
        coef_ready, coefT_done, tb_done = sem("coef_ready"), sem("coefT_done"), sem("tb_done")
        tails_ready, tailsT_done, rows_scanned, carry_done = (
            sem(n) for n in ("tails_ready", "tailsT_done", "rows_scanned", "carry_done"))
        score_ready, ex_ready, exT_done, exA_copied = (
            sem(n) for n in ("score_ready", "ex_ready", "exT_done", "exA_copied"))
        early_over = sem("early_over")
        picks_set = sem("picks_set")
        gathered = [sem(f"gathered{u}") for u in range(OHS)]
        dst_oh_ready, group_done, flushed = sem("dst_oh_ready"), sem("group_done"), sem("flushed")
        consts_in, b1_T_done, b1_T_ready = sem("consts_in"), sem("b1_T_done"), sem("b1_T_ready")
        zero_ready, xs_zeroed, x_again_in = sem("zero_ready"), sem("xs_zeroed"), sem("x_again_in")
        x_pad_set = sem("x_pad_set")
        xn1_kept = sem("xn1_kept")
        xn1_ready, xT1_done, xT1_copied, logits_done = (
            sem(n) for n in ("xn1_ready", "xT1_done", "xT1_copied", "logits_done"))
        gap_ready, gap_exp, mask_ready, ranks_done, pos_ready = (
            sem(n) for n in ("gap_ready", "gap_exp", "mask_ready", "ranks_done", "pos_ready"))
        xs_put = sem("xs_put")
        x1_made, w1_in, w2_in, w1_picked = (sem(n) for n in ("x1_made", "w1_in", "w2_in", "w1_picked"))
        xs_got = [sem(f"xs_got{u}") for u in range(2)]
        xsT_done, xsT_copied, l1_done, gelu_done, l2_done, y_ready = (
            sem(n) for n in ("xsT_done", "xsT_copied", "l1_done", "gelu_done", "l2_done", "y_ready"))
        y_stored = [sem(f"y_stored{u}") for u in range(2)]
        y_got = [sem(f"y_got{u}") for u in range(YS)]
        combined = sem("combined")
        s_out = sem("s_out")
        block = ctx.enter_context(nc.Block())

        @block.sync
        def _(sp):
            sp.wait_ge(pads_set, 1)
            sp.dma_start(dst_i[0:1, 1:RL + 2], dst[0:RL + 1].rearrange("(a j) -> a j", a=1))\
              .then_inc(dst_in, 16)
            for lo, hi in ((1, 65), (65, Q - 1)):
                sp.dma_start(dst_i[lo:hi, 1:RL + 1], dst_rows[lo:hi, :]).then_inc(dst_in, 16)
            sp.dma_start(dst_i[Q - 1:Q, 0:RL + 1],
                         dst[(Q - 1) * RL - 1:E].rearrange("(a j) -> a j", a=1)).then_inc(dst_in, 16)
            prev = dst_rows[0:Q - 2, RL - 1:RL]
            nxt = dst_rows[2:Q, 0:1]
            with nc.allow_non_contiguous_dma(reason="one element a row"):
                sp.dma_start(dst_i[1:Q - 1, 0:1], prev).then_inc(dst_in, 16)
                sp.dma_start(dst_i[1:Q - 1, RL + 1:RL + 2], nxt).then_inc(dst_in, 16)
            sp.dma_start(src_i[0:Q, :], src_rows).then_inc(src_in, 16)
            sp.wait_ge(pads_set, 2)
            full = (NB - 1) * P
            sp.dma_start(xs0[:, 0:NB - 1, :], x[0:full, :].rearrange("(b p) f -> p b f", p=P))\
              .then_inc(x_in, 16)
            sp.dma_start(xs0[0:LASTB, NB - 1, :], x[full:N, :]).then_inc(x_in, 16)
            for k in range(KF):
                sp.dma_start(w_ext[:, k, 0:HF].rearrange("p (h o) -> p h o", h=H),
                             gnn_w[:, k * P:(k + 1) * P, :].rearrange("h f o -> f h o"))\
                  .then_inc(w_in, 16)
            for s, a in enumerate((a_src, a_dst)):
                sp.dma_start(a_bc[:, s, :], a.rearrange("h o -> (h o)").partition_broadcast(P))\
                  .then_inc(a_in, 16)
            sp.wait_ge(edges_f, 1)
            sp.dma_start(dst_tab, dst_f[0:Q, 1:RL + 1]).then_inc(dst_stored, 16)
            sp.wait_ge(lo_ready, 1)
            sp.dma_start(lo_tab, lo_b[0:Q, :]).then_inc(lo_stored, 16)
            sp.wait_ge(zeros_set, 1)
            sp.dma_start(ed_rows, zeros[0:Q, :]).then_inc(ed_zeroed, 16)
            with sp.Fori(0, NB // 2, 1) as i:
                for u in range(2):
                    sp.wait_ge(h_copied, 2 * i + u + 1)
                    sp.dma_start(h_tab[bass.ds((2 * i + u) * P, P), :], h_stage[:, u, :])\
                      .then_inc(h_stored[u], 16)
            def lo_row(q, u, first=False):
                if not first:
                    sp.wait_ge(lo_oh_ready, q - OHS + 1)
                sp.dma_start(lo_bc[:, u, :],
                             lo_tab[bass.ds(q, 1), :].rearrange("a j -> (a j)").partition_broadcast(P))\
                  .then_inc(lo_in[u], 16)

            sp.wait_ge(lo_stored, 16)
            for u in range(OHS):
                lo_row(u, u, first=True)
            with sp.Fori(1, Q // OHS, 1) as i:
                for u in range(OHS):
                    lo_row(i * OHS + u, u)
            sp.wait_ge(exT_done, TPR)
            for to, frm in ((gamma_bc, gamma.partition_broadcast(P)), (beta_bc, beta.partition_broadcast(P)),
                            (br_bc, br.partition_broadcast(P)),
                            (wr_sb, wr.rearrange("(k p) e -> p k e", p=P)),
                            (b1_rows, b1.rearrange("e (c p) -> (e c) p", p=P)),
                            (b2_bc.rearrange("p e f -> p (e f)"),
                             b2.rearrange("e f -> (e f)").partition_broadcast(P))):
                sp.dma_start(to, frm).then_inc(consts_in, 16)
            sp.wait_ge(zero_ready, 1)
            xs_flat = xs_tab.rearrange("(p a) f -> p (a f)", p=P)
            for n in range(9):
                sp.dma_start(xs_flat[:, n * zero_width:(n + 1) * zero_width], zero_src)\
                  .then_inc(xs_zeroed, 16)
            sp.wait_ge(group_done, G)
            sp.dma_start(x_again[:, 0:NB - 1, :], x[0:full, :].rearrange("(b p) f -> p b f", p=P))\
              .then_inc(x_again_in, 16)
            sp.wait_ge(x_pad_set, 1)
            sp.dma_start(x_again[0:LASTB, NB - 1, :], x[full:N, :]).then_inc(x_again_in, 16)

            for e in range(NE):
                sp.dma_start(w1_all[:, e, :].rearrange("p (k h) -> p k h", k=KF),
                             w1[e, :, :].rearrange("(k p) h -> p k h", p=P)).then_inc(w1_in, 16)
            for e in range(NE):
                if e == W2_FIRST:
                    sp.wait_ge(x1_made, 1)
                sp.dma_start(w2_all[:, e, :, :], w2[e, :, :].rearrange("(c p) f -> p c f", p=P))\
                  .then_inc(w2_in, 16)

            def load_slots(j, u, first=False):
                if not first:
                    sp.wait_ge(xsT_done, j - 1)
                sp.dma_start(xs_in[:, u, :, :],
                             xs_tab[bass.ds(j * BS, BS), :].rearrange("(m p) f -> p m f", p=P))\
                  .then_inc(xs_got[u], 16)

            sp.wait_ge(xs_put, 16 * TOP * NB)
            load_slots(0, 0, first=True)
            load_slots(1, 1, first=True)
            with sp.Fori(1, NBLK // 2, 1) as i:
                load_slots(2 * i, 0)
                load_slots(2 * i + 1, 1)
            for j in range(NBLK // 2 * 2, NBLK):
                load_slots(j, j % 2)
            with sp.Fori(0, NB - 1, 1) as b:
                sp.wait_ge(combined, b + 1)
                sp.dma_start(out[bass.ds(b * P, P), :],
                             acc[:, bass.ds(b, 1), 0:F].rearrange("p b f -> p (b f)")).then_inc(s_out, 16)
            sp.wait_ge(combined, NB)
            sp.dma_start(out[full:N, :], acc[0:LASTB, NB - 1, 0:F]).then_inc(s_out, 16)
            sp.wait_ge(s_out, 16 * NB)

        @block.gpsimd
        def _(pool):
            for m in (ident, shift, corner):
                pool.memset(m[:, :], 0.0).then_inc(s_pool, 1)
            pool.memset(ones[:, :], 1.0).then_inc(s_const, 1)
            pool.wait_ge(s_pool, 3)
            for m, base, mult in ((ident, 0, 1), (shift, -1, 1), (corner, P - 1, P)):
                pool.affine_select(out=m[:, :], in_=m[:, :], compare_op=ALU.not_equal, fill=1.0,
                                   base=base, pattern=[[-1, P]], channel_multiplier=mult)\
                    .then_inc(s_const, 1)
            for t, base, pattern, mult in ((iota_f, 0, [[1, P]], 0), (iota_g, 0, [[1, G]], 0),
                                           (pcol, 0, [[1, 1]], 1), (node_id, 0, [[P, NB]], 1),
                           (ring_slot, 0, [[0, Q // RING], [1, RING]], 0)):
                pool.iota(t[:, :], pattern=pattern, base=base, channel_multiplier=mult,
                          allow_small_or_imprecise_dtypes=True).then_inc(s_const, 1)
            pool.wait_ge(dst_stored, 16)
            pool.wait_ge(q_ready, 1)
            for b in range(NB):
                if b >= ROWBUF:
                    pool.wait_ge(rows_used, b - ROWBUF + 1)
                pool.indirect_dma_start(
                    out=drow[:, b % ROWBUF, :], out_offset=None, in_=dst_tab,
                    in_offset=bass.IndirectOffsetOnAxis(ap=qi[:, b:b + 1], axis=0))\
                    .then_inc(rows_got[b % ROWBUF], 16)
            pool.wait_ge(ed_zeroed, 16)
            pool.wait_ge(h_copied, NB)
            pool.wait_ge(spos_ready, 1)
            for b in range(NB):
                pool.indirect_dma_start(
                    out=ed_tab, out_offset=bass.IndirectOffsetOnAxis(ap=spos[:, b:b + 1], axis=0),
                    in_=e_node[:, b, H:2 * H], in_offset=None).then_inc(ed_put, 16)

            def pick_row(t, u):
                pool.tensor_copy(picks[:, u, :],
                                 srcA[:, bass.ds(t, 1), :].rearrange("p q r -> p (q r)"))\
                    .then_inc(picks_set, 1)

            def gather_row(trip, u, first):
                t = trip * RING + u
                if not first or u >= OHS:
                    pool.wait_ge(gathered[u % OHS], 16 * TPR * (trip * (RING // OHS) + u // OHS))
                if not first:
                    pool.wait_ge(group_done, t - RING + NB)
                pool.wait_ge(picks_set, t + 1)
                pick_row(t + 1, (u + 1) % RING)
                for r in range(TPR):
                    pool.indirect_dma_start(
                        out=ring[:, u, r, 0:HF], out_offset=None, in_=h_tab,
                        in_offset=bass.IndirectOffsetOnAxis(ap=picks[:, u, r:r + 1], axis=0))\
                        .then_inc(gathered[u % OHS], 16)

            pool.wait_ge(h_stored[0], 16 * (NB // 2))
            pool.wait_ge(h_stored[1], 16 * (NB // 2))
            pool.wait_ge(ed_put, 16 * NB)
            pool.wait_ge(edges_A, 1)
            pool.wait_ge(early_over, 1)
            pick_row(0, 0)
            for u in range(RING):
                gather_row(0, u, True)
            with pool.Fori(1, Q // RING, 1) as trip:
                for u in range(RING):
                    gather_row(trip, u, False)

            pool.wait_ge(pos_ready, 1)
            pool.wait_ge(xs_zeroed, 16 * 9)
            for k in range(TOP):
                for b in range(NB):
                    rows = P if b < NB - 1 else LASTB
                    pool.indirect_dma_start(
                        out=xs_tab, out_offset=bass.IndirectOffsetOnAxis(ap=pos_i[0:rows, k, b:b + 1], axis=0),
                        in_=xn1[0:rows, b, :], in_offset=None).then_inc(xs_put, 16)
            pool.wait_ge(y_stored[0], 16 * ((NBLK + 1) // 2))
            pool.wait_ge(y_stored[1], 16 * (NBLK // 2))
            for b in range(NB):
                rows = P if b < NB - 1 else LASTB
                if b >= YS:
                    pool.wait_ge(combined, b - YS + 1)
                for k in range(TOP):
                    pool.indirect_dma_start(
                        out=y_in[0:rows, b % YS, k, :], out_offset=None, in_=ys_tab,
                        in_offset=bass.IndirectOffsetOnAxis(ap=pos_i[0:rows, k, b:b + 1], axis=0))\
                        .then_inc(y_got[b % YS], 16)

        NCONST = 9

        @block.tensor
        def _(pe):
            pe.wait_ge(s_const, NCONST)
            pe.wait_ge(edges_f, 1)
            for r in range(TPR):
                for n, row in enumerate((src_f[0:Q, :], dst_f[0:Q, 1:RL + 1])):
                    to = bank[4 + n][:, r * Q:(r + 1) * Q] if r < 4 else bank[6][:, n * Q:(n + 1) * Q]
                    last = pe.transpose(to, row[:, r * P:(r + 1) * P], ident[0:Q, 0:Q])
            last.then_inc(edges_T, 1)
            pe.wait_ge(row_diag, 1)
            pe.matmul(bank[7][:, 0:Q], ones[0:Q, :], diag[0:Q, :], start=True, stop=True)\
              .then_inc(row_ends, 1)
            pe.wait_ge(q_ready, 1)
            pe.matmul(bank[7][:, 0:NB], ones[0:1, :], qn[0:1, :], start=True, stop=True)\
              .then_inc(tb_done, 1)

            pe.wait_ge(wext_ready, 1)

            def transposes(b, u, first=False):
                pe.wait_ge(xn_ready, b + 1)
                if not first:
                    pe.wait_ge(xT_copied, b - 1)
                for k in range(KF):
                    last = pe.transpose(bank[u][:, k * P:(k + 1) * P], xn0[:, u, k * P:(k + 1) * P],
                                        ident[:, :])
                last.then_inc(xT_done, 1)

            def project(b, u, first=False):
                pe.wait_ge(xT_copied, b + 1)
                if not first:
                    pe.wait_ge(h_copied, b - 1)
                for k in range(KF):
                    last = pe.matmul(bank[2 + u][:, 0:wide], xT0[:, u, k, :], w_ext[:, k, :],
                                     start=(k == 0), stop=(k == KF - 1))
                last.then_inc(h_done, 1)

            transposes(0, 0, first=True)
            transposes(1, 1, first=True)
            project(0, 0, first=True)
            transposes(2, 0)
            project(1, 1, first=True)
            with pe.Fori(1, NB // 2 - 1, 1) as i:
                transposes(2 * i + 1, 1)
                project(2 * i, 0)
                transposes(2 * i + 2, 0)
                project(2 * i + 1, 1)
            transposes(NB - 1, 1)
            project(NB - 2, 0)
            project(NB - 1, 1)

            pe.wait_ge(start_ready, 1)
            pe.matmul(bank[7][:, 0:NB], shift[:, :], start[:, 0:NB], start=True, stop=False)
            pe.matmul(bank[7][:, 0:NB], corner[:, :], start[:, 1:NB + 1], start=False,
                      stop=True).then_inc(next_done, 1)
            pe.wait_ge(coef_ready, 1)
            pe.wait_ge(spos_ready, 1)
            for n in range(3):
                last = pe.transpose(bank[7][0:H, n * Q:(n + 1) * Q], coef[0:Q, n * H:(n + 1) * H],
                                    ident[0:Q, 0:Q])
            last.then_inc(coefT_done, 1)

            def pick_es(q, u, first=False):
                pe.wait_ge(lo_oh_ready, q + 1)
                if not first:
                    pe.wait_ge(es_picked, q - OHS + 1)
                for r in range(TPR):
                    for n in range(3):
                        last = pe.matmul(bank[u][:, r * H * NB:(r + 1) * H * NB],
                                         lo_oh[:, u, r * P:(r + 1) * P],
                                         t3[:, n, :, :].rearrange("p h b -> p (h b)"),
                                         start=(n == 0), stop=(n == 2))
                last.then_inc(es_done, 1)

            for u in range(OHS):
                pick_es(u, u, first=True)
            with pe.Fori(1, Q // OHS, 1) as i:
                for u in range(OHS):
                    pick_es(i * OHS + u, u)
            pe.wait_ge(es_picked, Q)
            for r in range(TPR):
                if r >= 2:
                    pe.wait_ge(esB_copied, r - 1)
                for h in range(H):
                    last = pe.transpose(bank[5 + r % 2][0:Q, h * P:(h + 1) * P], exA[:, :, r, h],
                                        ident[:, :])
                last.then_inc(esT_done, 1)
            for n in range(3):
                pe.wait_ge(tails_ready, n + 1)
                tails = (mxB[0:Q, :, RL - 1], mxB[0:Q, :, RL - 1], bwdB[0:Q, :, 0])[n]
                pe.transpose(bank[7][0:H, 0:Q], tails, ident[0:Q, 0:Q]).then_inc(tailsT_done, 1)
                pe.wait_ge(rows_scanned, n + 1)
                pe.transpose(bank[7][0:Q, 256:256 + H], carry_row[:, (0, 0, 1)[n]:(0, 0, 1)[n] + Q],
                             ident[0:H, 0:H]).then_inc(carry_done, 1)
            pe.wait_ge(ex_ready, 1)
            for r in range(TPR):
                if r >= 2:
                    pe.wait_ge(exA_copied, r - 1)
                for h in range(H):
                    last = pe.transpose(bank[5 + r % 2][:, h * Q:(h + 1) * Q],
                                        esB[0:Q, h, r * P:(r + 1) * P], ident[0:Q, 0:Q])
                last.then_inc(exT_done, 1)

            def group(i, u, first=False):
                pe.wait_ge(dst_oh_ready, i + 1)
                if not first:
                    pe.wait_ge(flushed, i - OHS + 1)
                slot = pe.value_load(slot_i[0:1, bass.ds(i, 1)], min_val=0, max_val=RING - 1)
                for r in range(TPR):
                    last = pe.matmul(bank[u][:, 0:MW], dst_oh[:, u, r, :],
                                     ring[:, bass.ds(slot, 1), r, :].rearrange("p s w -> p (s w)"),
                                     start=(r == 0), stop=(r == TPR - 1))
                last.then_inc(group_done, 1)

            for u in range(OHS):
                group(u, u, first=True)
            with pe.Fori(1, G // OHS, 1) as i:
                for u in range(OHS):
                    group(i * OHS + u, u)
            for i in range(G // OHS * OHS, G):
                group(i, i % OHS)

            pe.wait_ge(consts_in, 16 * 6)
            pe.transpose(bank[7][:, 0:NE * FC], b1_rows, ident[0:NE * FC, 0:NE * FC])\
              .then_inc(b1_T_done, 1)

            def node_T(b, u, first=False):
                pe.wait_ge(xn1_ready, b + 1)
                if not first:
                    pe.wait_ge(xT1_copied, b - 1)
                for k in range(KF):
                    last = pe.transpose(bank[u][:, k * P:(k + 1) * P], xn_u[:, u, k * P:(k + 1) * P],
                                        ident[:, :])
                last.then_inc(xT1_done, 1)

            def router(b, u):
                pe.wait_ge(xT1_copied, b + 1)
                for k in range(KF):
                    last = pe.matmul(bank[2][:, bass.ds(b * NE, NE)], xT1[:, u, k, :], wr_sb[:, k, :],
                                     start=(k == 0), stop=(k == KF - 1))
                last.then_inc(logits_done, 1)

            node_T(0, 0, first=True)
            node_T(1, 1, first=True)
            router(0, 0)
            with pe.Fori(1, NB // 2, 1) as i:
                node_T(2 * i, 0)
                router(2 * i - 1, 1)
                node_T(2 * i + 1, 1)
                router(2 * i, 0)
            router(NB - 1, 1)
            pe.wait_ge(mask_ready, 1)
            mask_flat = mask.rearrange("p b e -> p (b e)")
            pe.matmul(bank[3][:, 0:NB * NE], upper, mask_flat, start=True, stop=True)
            pe.matmul(bank[4][:, 0:NB * NE], ones[:, :], mask_flat, start=True, stop=True)\
              .then_inc(ranks_done, 1)

            def slots_T(j, u, n, first=False):
                pe.wait_ge(xs_got[u], 16 * (n + 1))
                if not first:
                    pe.wait_ge(xsT_copied, j - 1)
                for k in range(KF):
                    for m in range(BM):
                        last = pe.transpose(bank[u][:, k * BS + m * P:k * BS + (m + 1) * P],
                                            xs_in[:, u, m, k * P:(k + 1) * P], ident[:, :])
                last.then_inc(xsT_done, 1)

            def layer_1(j, u, first=False):
                pe.wait_ge(xsT_copied, j + 1)
                pe.wait_ge(w1_picked, j + 1)
                if not first:
                    pe.wait_ge(gelu_done, FC * (j - 1))
                for c in range(FC):
                    for k in range(KF):
                        last = pe.matmul(bank[2 + 2 * u + c // 2][:, c % 2 * BS:(c % 2 + 1) * BS],
                                         w1_now[:, u, k, c * P:(c + 1) * P], xsT[:, u, k, :],
                                         start=(k == 0), stop=(k == KF - 1))
                    if c % 2:
                        last.then_inc(l1_done, 1)

            def layer_2(j, u, first=False):
                e = pe.value_load(blk_e[0:1, bass.ds(j, 1)], min_val=0, max_val=NE - 1)
                pe.wait_ge(gelu_done, FC * (j + 1))
                if not first:
                    pe.wait_ge(y_ready, j - 1)
                for m in range(BM):
                    for c in range(FC):
                        last = pe.matmul(bank[6 + u][:, m * F:(m + 1) * F],
                                         hT[:, u, c, m * P:(m + 1) * P],
                                         w2_all[:, bass.ds(e, 1), c, :].rearrange("p e f -> p (e f)"),
                                         start=(c == 0), stop=(c == FC - 1))
                last.then_inc(l2_done, 1)

            pe.wait_ge(w2_in, 16 * NE)
            slots_T(0, 0, 0, first=True)
            layer_1(0, 0, first=True)
            slots_T(1, 1, 0, first=True)
            layer_1(1, 1, first=True)
            layer_2(0, 0, first=True)
            slots_T(2, 0, 1)
            layer_1(2, 0)
            layer_2(1, 1, first=True)
            with pe.Fori(1, (NBLK - 1) // 2, 1) as i:
                slots_T(2 * i + 1, 1, i)
                layer_1(2 * i + 1, 1)
                layer_2(2 * i, 0)
                slots_T(2 * i + 2, 0, i + 1)
                layer_1(2 * i + 2, 0)
                layer_2(2 * i + 1, 1)
            for j in range(2 * ((NBLK - 1) // 2), NBLK):
                if j + 1 < NBLK:
                    slots_T(j + 1, (j + 1) % 2, (j + 1) // 2)
                    layer_1(j + 1, (j + 1) % 2)
                layer_2(j, j % 2)

        @block.scalar
        def _(act):
            act.wait_ge(var_ready, 1)
            act.activation(rstd[:, :], sm1[:, :], ACT.Sqrt).then_inc(std_ready, 1)

            def node_block(b, u, stores):
                act.wait_ge(xT_done, b + 1)
                act.activation(xT0[:, u, :, :].rearrange("p k n -> p (k n)"), bank[u][:, 0:F],
                               ACT.Copy).then_inc(xT_copied, 1)
                act.wait_ge(h_done, b + 1)
                act.activation(e_node[:, bass.ds(b, 1), :].rearrange("p b w -> p (b w)"),
                               bank[2 + u][:, HF:wide], ACT.Copy)
                if stores is not None:
                    act.wait_ge(h_stored[u], 16 * stores)
                act.activation(h_stage[:, u, :], bank[2 + u][:, 0:HF], ACT.Copy)\
                   .then_inc(h_copied, 1)

            node_block(0, 0, None)
            node_block(1, 1, None)
            with act.Fori(1, NB // 2, 1) as i:
                node_block(2 * i, 0, i)
                node_block(2 * i + 1, 1, i)

            act.wait_ge(ed_put, 16 * NB)
            act.dma_start(edB[0:Q, :, :].rearrange("q j h -> q (j h)"), ed_rows).then_inc(ed_in, 16)
            for r in range(TPR):
                act.wait_ge(esT_done, r + 1)
                act.activation(esB[0:Q, :, r * P:(r + 1) * P],
                               bank[5 + r % 2][0:Q, :].rearrange("q (h p) -> q h p", h=H),
                               ACT.Copy).then_inc(esB_copied, 1)
            act.wait_ge(score_ready, 1)
            act.activation(esB[0:Q, :, :], esB[0:Q, :, :], ACT.Exp).then_inc(ex_ready, 1)
            for r in range(TPR):
                act.wait_ge(exT_done, r + 1)
                act.activation(exA[:, :, r, :].rearrange("p q h -> p h q"),
                               bank[5 + r % 2][:, 0:H * Q].rearrange("p (h q) -> p h q", h=H),
                               ACT.Copy).then_inc(exA_copied, 1)

            for n in range(2):
                act.wait_ge(var_ready, n + 2)
                act.activation(rstd1, tmp1, ACT.Sqrt).then_inc(std_ready, 1)

            def keep_node(b, u):
                act.wait_ge(xn1_ready, b + 1)
                act.activation(xn1[:, bass.ds(b, 1), :].rearrange("p b f -> p (b f)"), xn_u[:, u, :],
                               ACT.Copy).then_inc(xn1_kept, 1)
                act.wait_ge(xT1_done, b + 1)
                act.activation(xT1[:, u, :, :].rearrange("p k n -> p (k n)"), bank[u][:, 0:F],
                               ACT.Copy).then_inc(xT1_copied, 1)

            def keep_node_later(b, u):
                act.wait_ge(logits_done, b - 1)
                keep_node(b, u)

            keep_node(0, 0)
            keep_node(1, 1)
            with act.Fori(1, NB // 2, 1) as i:
                keep_node_later(2 * i, 0)
                keep_node_later(2 * i + 1, 1)
            act.wait_ge(gap_ready, 1)
            act.activation(w_b, tmp1, ACT.Exp).then_inc(gap_exp, 1)

            def hidden(j, u, first=False):
                e = act.value_load(blk_e[0:1, bass.ds(j, 1)], min_val=0, max_val=NE - 1)
                if not first:
                    act.wait_ge(l2_done, j - 1)
                for c in range(FC):
                    if c % 2 == 0:
                        act.wait_ge(l1_done, FC // 2 * j + c // 2 + 1)
                    act.activation(hT[:, u, c, :],
                                   bank[2 + 2 * u + c // 2][:, c % 2 * BS:(c % 2 + 1) * BS], ACT.Gelu,
                                   bias=b1_T[:, bass.ds(e * FC + c, 1)]).then_inc(gelu_done, 1)

            def store_y(j, u):
                act.wait_ge(y_ready, j + 1)
                act.dma_start(ys_tab[bass.ds(j * BS, BS), :].rearrange("(m p) f -> p m f", p=P),
                              y_out[:, u, :, :]).then_inc(y_stored[u], 16)

            act.wait_ge(pos_ready, 1)
            act.wait_ge(b1_T_ready, 1)
            hidden(0, 0, first=True)
            hidden(1, 1, first=True)
            store_y(0, 0)
            with act.Fori(1, NBLK // 2, 1) as i:
                hidden(2 * i, 0)
                store_y(2 * i - 1, 1)
                hidden(2 * i + 1, 1)
                store_y(2 * i, 0)
            for j in range(NBLK // 2 * 2, NBLK + 1):
                if j < NBLK:
                    hidden(j, j % 2)
                store_y(j - 1, (j - 1) % 2)

        @block.vector
        def _(v):
            c = Chain(v, s_dve)
            v.memset(dst_i[0:Q, :], -1).then_inc(pads_set, 1)
            v.memset(xs0[:, NB - 1, :], 0.0).then_inc(pads_set, 1)
            v.memset(zeros[0:Q, :], 0.0).then_inc(zeros_set, 1)
            v.wait_ge(dst_in, 96)
            c.link(v.tensor_copy(dst_f[0:Q, :], dst_i[0:Q, :]))
            v.wait_ge(src_in, 16)
            v.tensor_copy(src_f[0:Q, :], src_i[0:Q, :]).then_inc(edges_f, 1)
            c.link(v.tensor_scalar(lo_i[0:Q, :], src_i[0:Q, :], P - 1, None, ALU.bitwise_and))
            v.tensor_copy(lo_b[0:Q, :], lo_i[0:Q, :]).then_inc(lo_ready, 1)
            c.link(v.tensor_tensor(keep[0:Q, :], dst_f[0:Q, 0:RL + 1], dst_f[0:Q, 1:RL + 2],
                                   ALU.is_equal))
            v.tensor_scalar(reset[0:Q, :], keep[0:Q, :], 1.0, BIG, ALU.subtract, ALU.mult)
            for n, (a, b) in enumerate(((RL, 0), (RL, 0), (1, RL + 1))):
                c.link(v.tensor_tensor(coef[0:Q, n * H:(n + 1) * H],
                                       dst_f[0:Q, a:a + 1].broadcast_to([Q, H]),
                                       dst_f[0:Q, b:b + 1].broadcast_to([Q, H]), ALU.is_equal))
            v.tensor_scalar(coef[0:Q, H:3 * H], coef[0:Q, H:3 * H], 1.0, BIG, ALU.subtract, ALU.mult)\
             .then_inc(coef_ready, 1)
            v.wait_ge(s_const, NCONST)
            v.tensor_scalar(diag[0:Q, :], ident[0:Q, 0:Q], dst_f[0:Q, RL:RL + 1], None, ALU.mult)\
             .then_inc(row_diag, 1)
            v.wait_ge(w_in, 16 * KF)
            v.wait_ge(a_in, 32)
            for k in range(KF):
                for s in range(2):
                    c.link(v.tensor_tensor(w_tmp[:, s, :], w_ext[:, k, 0:HF], a_bc[:, s, :], ALU.mult))
                c.link(v.tensor_reduce(
                    w_ext[:, k, HF:wide], w_tmp.rearrange("p s (h o) -> p (s h) o", h=H), AX.X, ALU.add))
            v.nop().then_inc(wext_ready, 1)
            v.wait_ge(edges_T, 1)
            for n, to in enumerate((srcA, dstA)):
                v.tensor_copy(to[:, 0:Q, 0:4], bank[4 + n][:, 0:4 * Q].rearrange("p (r q) -> p q r", r=4))
                c.link(v.tensor_copy(to[:, 0:Q, 4], bank[6][:, n * Q:(n + 1) * Q]))
            c.link(v.memset(srcA[:, Q, :], 0))
            c.link(v.tensor_scalar(hi_i, srcA[:, 0:Q, :].rearrange("p q r -> p (q r)"), 7, None,
                                   ALU.arith_shift_right))
            v.tensor_copy(hiA[:, :, :].rearrange("p q r -> p (q r)"), hi_i).then_inc(edges_A, 1)
            v.wait_ge(row_ends, 1)
            c.link(v.tensor_tensor(q_tmp, bank[7][:, 0:Q].unsqueeze(1).broadcast_to([P, NB, Q]),
                                   node_id[:, :].unsqueeze(2).broadcast_to([P, NB, Q]), ALU.is_lt))
            c.link(v.tensor_reduce(qn[:, :], q_tmp, AX.X, ALU.add))
            c.link(v.tensor_scalar(qn[:, :], qn[:, :], float(Q - 1), None, ALU.min))
            v.tensor_copy(qi[:, :], qn[:, :]).then_inc(q_ready, 1)
            v.wait_ge(tb_done, 1)
            c.link(v.tensor_tensor(enters[:, :], bank[7][:, 1:NB], iota_f[:, 1:NB], ALU.add))
            c.link(v.tensor_tensor(path_tmp, enters[:, :].unsqueeze(1).broadcast_to([P, G, NB - 1]),
                                   iota_g[:, :].unsqueeze(2).broadcast_to([P, G, NB - 1]), ALU.is_le))
            c.link(v.tensor_reduce(beta_f[:, :], path_tmp, AX.X, ALU.add))
            v.tensor_copy(beta_i[:, :], beta_f[0:1, :])
            c.link(v.tensor_tensor(slot_f[:, :], iota_g[0:1, :], beta_f[0:1, :], ALU.subtract))
            v.tensor_copy(tau_i[:, :], slot_f[:, :])
            for n in range(Q // RING - 1, 0, -1):
                c.link(v.tensor_scalar(path_f[:, :], slot_f[:, :], float(n * RING), float(RING * n),
                                       ALU.is_ge, ALU.mult))
                c.link(v.tensor_tensor(slot_f[:, :], slot_f[:, :], path_f[:, :], ALU.subtract))
            c.link(v.tensor_copy(slot_i[:, :], slot_f[:, :]))
            c.link(v.tensor_scalar(beta_f[:, :], beta_f[:, :], float(P), None, ALU.mult))
            v.wait_ge(x_in, 32)
            with v.Fori(0, NB, 1) as b:
                c.enter(b, 1)
                c.link(v.bn_stats(st0[:, bass.ds(b, 1), :].rearrange("p b s -> p (b s)"),
                                  xs0[:, bass.ds(b, 1), :].rearrange("p b f -> p (b f)")))
            c.leave(NB)
            c.link(v.tensor_tensor(mean[:, :], st0[:, :, 1], st0[:, :, 4], ALU.add))
            c.link(v.tensor_scalar(mean[:, :], mean[:, :], 0.5, None, ALU.mult))
            c.link(v.tensor_tensor(sm1[:, :], st0[:, :, 1], st0[:, :, 4], ALU.subtract))
            c.link(v.tensor_tensor(sm1[:, :], sm1[:, :], sm1[:, :], ALU.mult))
            c.link(v.tensor_tensor(sm2[:, :], st0[:, :, 2], st0[:, :, 5], ALU.add))
            c.link(v.scalar_tensor_tensor(sm1[:, :], sm1[:, :], F / 4.0, sm2[:, :], ALU.mult, ALU.add))
            v.tensor_scalar(sm1[:, :], sm1[:, :], 1.0 / F, EPS, ALU.mult, ALU.add).then_inc(var_ready, 1)
            v.wait_ge(std_ready, 1)
            c.link(v.reciprocal(rstd[:, :], rstd[:, :]))
            for u in range(2):
                v.tensor_scalar(xn0[:, u, :], xs0[:, u, :], mean[:, u:u + 1], rstd[:, u:u + 1],
                                ALU.subtract, ALU.mult).then_inc(xn_ready, 1)
            with v.Fori(1, NB // 2, 1) as i:
                for u in range(2):
                    b = 2 * i + u
                    v.wait_ge(xT_done, 2 * i + u - 1)
                    v.tensor_scalar(xn0[:, u, :], xs0[:, bass.ds(b, 1), :].rearrange("p b f -> p (b f)"),
                                    mean[:, bass.ds(b, 1)], rstd[:, bass.ds(b, 1)],
                                    ALU.subtract, ALU.mult).then_inc(xn_ready, 1)
            for b in range(NB):
                v.wait_ge(rows_got[b % ROWBUF], 16 * (b // ROWBUF + 1))
                v.tensor_scalar(drow[:, b % ROWBUF, :], drow[:, b % ROWBUF, :], node_id[:, b:b + 1], None,
                                ALU.is_lt, ALU.add, accum_out=start[:, b:b + 1]).then_inc(rows_used, 1)
            c.link(v.memset(start[:, NB:NB + 1], float(E)))
            c.link(v.scalar_tensor_tensor(start[:, 0:NB], qn[:, :], float(RL), start[:, 0:NB],
                                          ALU.mult, ALU.add))
            v.nop().then_inc(start_ready, 1)
            v.wait_ge(next_done, 1)
            c.link(v.tensor_tensor(sm1[:, :], bank[7][:, 0:NB], start[:, 0:NB], ALU.is_equal))
            c.link(v.scalar_tensor_tensor(sm2[:, :], node_id[:, :], float(E), start[:, 0:NB],
                                          ALU.add, ALU.subtract))
            c.link(v.tensor_tensor(sm1[:, :], sm1[:, :], sm2[:, :], ALU.mult))
            v.tensor_tensor(spos[:, :], sm1[:, :], start[:, 0:NB], ALU.add).then_inc(spos_ready, 1)

            v.wait_ge(coefT_done, 1)
            v.tensor_copy(coef_row[:, :, :], bank[7][0:H, 0:3 * Q].rearrange("h (n q) -> h n q", n=3))\
             .then_inc(early_over, 1)
            v.wait_ge(h_copied, NB)
            es = e_node[:, :, 0:H].rearrange("p b h -> p h b")
            res = t_res[:, :, :]
            c.link(v.tensor_copy(t3[:, 0, :, :], es))
            c.link(v.tensor_tensor(res, es, t3[:, 0, :, :], ALU.subtract))
            c.link(v.tensor_copy(t3[:, 1, :, :], res))
            c.link(v.tensor_tensor(res, res, t3[:, 1, :, :], ALU.subtract))
            c.link(v.tensor_copy(t3[:, 2, :, :], res))

            def onehot(trip, u):
                v.wait_ge(lo_in[u], 16 * (trip + 1))
                v.tensor_scalar(lo_oh[:, u, :], lo_bc[:, u, :], pcol[:, 0:1], None, ALU.is_equal)\
                 .then_inc(lo_oh_ready, 1)

            def pick(trip, u):
                q = trip * OHS + u
                c.link(v.tensor_tensor(
                    hi_oh[:, :, :],
                    hiA[:, bass.ds(q, 1), :].rearrange("p q r -> p (q r)").unsqueeze(2)
                    .broadcast_to([P, TPR, NB]),
                    iota_f[:, 0:NB].unsqueeze(1).broadcast_to([P, TPR, NB]), ALU.is_equal))
                v.wait_ge(es_done, q + 1)
                c.link(v.tensor_tensor(
                    es_sel.rearrange("p (r h) b -> p r h b", h=H),
                    bank[u][:, 0:TPR * H * NB].rearrange("p (r h b) -> p r h b", r=TPR, h=H),
                    hi_oh[:, :, :].unsqueeze(2).broadcast_to([P, TPR, H, NB]), ALU.mult))
                v.tensor_reduce(exA[:, bass.ds(q, 1), :, :].rearrange("p q r h -> p (q r h)"),
                                es_sel, AX.X, ALU.add).then_inc(es_picked, 1)
                v.wait_ge(es_picked, q + 1)

            for u in range(OHS):
                onehot(0, u)
            with v.Fori(0, Q // OHS - 1, 1) as i:
                c.enter(i, 2 * OHS)
                for u in range(OHS):
                    pick(i, u)
                    onehot(i + 1, u)
            c.leave(Q // OHS - 1)
            for u in range(OHS):
                pick(Q // OHS - 1, u)

            keep0, reset0 = keep[0:Q, 0:RL], reset[0:Q, 0:RL]
            reset1 = reset[0:Q, 1:RL + 1][:, ::-1]

            def across_rows(n, fill, op0, op1, back=False):
                v.nop().then_inc(tails_ready, 1)
                v.wait_ge(tailsT_done, n + 1)
                if back:
                    c.link(v.memset(carry_row[:, Q:Q + 1], fill))
                    v.tensor_tensor_scan(carry_row[:, 0:Q][:, ::-1], coef_row[:, n, :][:, ::-1],
                                         bank[7][0:H, 0:Q][:, ::-1], fill, op0, op1)\
                     .then_inc(rows_scanned, 1)
                else:
                    c.link(v.memset(carry_row[:, 0:1], fill))
                    v.tensor_tensor_scan(carry_row[:, 1:Q + 1], coef_row[:, n, :], bank[7][0:H, 0:Q],
                                         fill, op0, op1).then_inc(rows_scanned, 1)
                v.wait_ge(carry_done, n + 1)
                c.link(v.tensor_copy(carry[0:Q, :], bank[7][0:Q, 256:256 + H]))

            v.wait_ge(ed_in, 16)
            for h in range(H):
                c.link(v.tensor_tensor_scan(mxB[0:Q, h, :], keep0, edB[0:Q, :, h], 0.0,
                                            ALU.mult, ALU.add))
            across_rows(0, 0.0, ALU.mult, ALU.add)
            for h in range(H):
                c.link(v.tensor_tensor_scan(edB[0:Q, :, h], keep0, edB[0:Q, :, h], carry[0:Q, h:h + 1],
                                            ALU.mult, ALU.add))
            v.wait_ge(esB_copied, TPR)
            for h in range(H):
                c.link(v.tensor_tensor_scan(mxB[0:Q, h, :], reset0, esB[0:Q, h, :], -BIG,
                                            ALU.add, ALU.max))
            across_rows(1, -BIG, ALU.add, ALU.max)
            for h in range(H):
                c.link(v.tensor_tensor_scan(mxB[0:Q, h, :], reset0, esB[0:Q, h, :], carry[0:Q, h:h + 1],
                                            ALU.add, ALU.max))
            for h in range(H):
                c.link(v.tensor_tensor_scan(bwdB[0:Q, h, :][:, ::-1], reset1, mxB[0:Q, h, :][:, ::-1],
                                            -BIG, ALU.add, ALU.max))
            across_rows(2, -BIG, ALU.add, ALU.max, back=True)
            for h in range(H):
                c.link(v.tensor_tensor_scan(mxB[0:Q, h, :][:, ::-1], reset1, mxB[0:Q, h, :][:, ::-1],
                                            carry[0:Q, h:h + 1], ALU.add, ALU.max))
            ed_hj = edB[0:Q, :, :].rearrange("q j h -> q h j")
            for t in (esB, mxB):
                c.link(v.tensor_tensor(t[0:Q, :, :], t[0:Q, :, :], ed_hj, ALU.add))
                c.link(v.scalar_tensor_tensor(t[0:Q, :, :], t[0:Q, :, :], 0.2, t[0:Q, :, :],
                                              ALU.mult, ALU.max))
            v.tensor_tensor(esB[0:Q, :, :], esB[0:Q, :, :], mxB[0:Q, :, :], ALU.subtract)\
             .then_inc(score_ready, 1)
            v.wait_ge(score_ready, 1)
            c.link(v.memset(acc_flat, 0.0))

            def scale_row(trip, u):
                t = trip * OHS + u
                s = v.value_load(ring_slot[0:1, bass.ds(t, 1)], min_val=0, max_val=RING - 1)
                v.wait_ge(gathered[u], 16 * TPR * (trip + 1))
                msg = ring[:, bass.ds(s, 1), :, 0:HF].rearrange("p s r (h o) -> p (s r) h o", h=H)
                ex = exA[:, bass.ds(t, 1), :, :].rearrange("p q r h -> p (q r) h")
                v.tensor_tensor(msg, msg, ex.unsqueeze(3).broadcast_to([P, TPR, H, FO]), ALU.mult)
                v.tensor_copy(ring[:, bass.ds(s, 1), :, HF:MW].rearrange("p s r h -> p (s r) h"), ex)

            def dst_onehot(trip, u):
                t = trip * OHS + u
                tau = v.value_load(tau_i[0:1, bass.ds(t, 1)], min_val=0, max_val=Q - 1)
                v.scalar_tensor_tensor(
                    dst_oh[:, u, :, :], iota_f[:, :].unsqueeze(1).broadcast_to([P, TPR, P]),
                    beta_f[:, bass.ds(t, 1)],
                    dstA[:, bass.ds(tau, 1), :].rearrange("p q r -> p (q r)").unsqueeze(2)
                    .broadcast_to([P, TPR, P]), ALU.add, ALU.is_equal).then_inc(dst_oh_ready, 1)

            def flush(trip, u):
                i = trip * OHS + u
                blk = v.value_load(beta_i[0:1, bass.ds(i, 1)], min_val=0, max_val=NB - 1)
                v.wait_ge(group_done, i + 1)
                a = acc[:, bass.ds(blk, 1), :].rearrange("p b w -> p (b w)")
                v.tensor_tensor(a, a, bank[u][:, 0:MW], ALU.add).then_inc(flushed, 1)
                v.wait_ge(flushed, i + 1)

            v.wait_ge(exA_copied, TPR)
            v.memset(zero_src, 0.0).then_inc(zero_ready, 1)
            for u in range(OHS):
                scale_row(0, u)
                dst_onehot(0, u)
            with v.Fori(0, Q // OHS - 1, 1) as i:
                for u in range(OHS):
                    flush(i, u)
                    scale_row(i + 1, u)
                    dst_onehot(i + 1, u)
            full_rows, full_steps = Q // OHS, G // OHS
            with v.Fori(full_rows - 1, full_steps - 1, 1) as i:
                for u in range(OHS):
                    flush(i, u)
                    dst_onehot(i + 1, u)
            for i in range((full_steps - 1) * OHS, G):
                flush(i // OHS, i % OHS)
                if i + OHS < G:
                    dst_onehot(i // OHS + 1, i % OHS)


            v.wait_ge(group_done, G)
            v.memset(x_again[:, NB - 1, :], 0.0).then_inc(x_pad_set, 1)
            c.link(v.tensor_scalar(rden, acc[:, :, HF:MW], 1e-9, None, ALU.max))
            c.link(v.reciprocal(rden, rden))
            x1_h = acc[:, :, 0:HF].rearrange("p b (h o) -> p b h o", h=H)
            x1 = acc[:, :, 0:HF]
            c.link(v.tensor_tensor(x1_h, x1_h, rden.unsqueeze(3).broadcast_to([P, NB, H, FO]), ALU.mult))
            v.wait_ge(x_again_in, 32)
            v.scalar_tensor_tensor(x1, x1, 0.0, x_again, ALU.max, ALU.add).then_inc(x1_made, 1)
            v.wait_ge(x1_made, 1)

            def moments(source, n):
                with v.Fori(0, NB, 1) as b:
                    c.enter(b, 1)
                    c.link(v.bn_stats(st1[:, bass.ds(b, 1), :].rearrange("p b s -> p (b s)"),
                                      source[:, bass.ds(b, 1), :].rearrange("p b f -> p (b f)")))
                c.leave(NB)
                c.link(v.tensor_tensor(mean1, st1[:, :, 1], st1[:, :, 4], ALU.add))
                c.link(v.tensor_scalar(mean1, mean1, 0.5, None, ALU.mult))
                c.link(v.tensor_tensor(tmp1, st1[:, :, 1], st1[:, :, 4], ALU.subtract))
                c.link(v.tensor_tensor(tmp1, tmp1, tmp1, ALU.mult))
                c.link(v.tensor_tensor(tmp2, st1[:, :, 2], st1[:, :, 5], ALU.add))
                c.link(v.scalar_tensor_tensor(tmp1, tmp1, F / 4.0, tmp2, ALU.mult, ALU.add))
                v.tensor_scalar(tmp1, tmp1, 1.0 / F, EPS, ALU.mult, ALU.add).then_inc(var_ready, 1)
                v.wait_ge(std_ready, n + 2)
                c.link(v.reciprocal(rstd1, rstd1))

            def block_of(t, b):
                return t[:, bass.ds(b, 1), :].rearrange("p b f -> p (b f)")

            moments(x1, 0)
            with v.Fori(0, NB, 1) as b:
                c.enter(b, 1)
                c.link(v.tensor_scalar(block_of(xn1, b), block_of(x1, b), mean1[:, bass.ds(b, 1)],
                                       rstd1[:, bass.ds(b, 1)], ALU.subtract, ALU.mult))
            c.leave(NB)
            moments(xn1, 1)
            v.wait_ge(consts_in, 16 * 6)

            def second_norm(b, u):
                row = block_of(xn1, b)
                c.link(v.tensor_scalar(row, row, mean1[:, bass.ds(b, 1)], rstd1[:, bass.ds(b, 1)],
                                       ALU.subtract, ALU.mult))
                c.link(v.tensor_tensor(row, row, gamma_bc, ALU.mult))
                v.tensor_tensor(xn_u[:, u, :], row, beta_bc, ALU.add).then_inc(xn1_ready, 1)

            for b in range(2):
                second_norm(b, b)
            with v.Fori(1, NB // 2, 1) as i:
                c.enter(i - 1, 4)
                for u in range(2):
                    v.wait_ge(xT1_done, 2 * i + u - 1)
                    v.wait_ge(xn1_kept, 2 * i + u - 1)
                    second_norm(2 * i + u, u)
            c.leave(NB // 2 - 1)
            c.link(v.tensor_scalar(upper, iota_f[:, :], pcol[:, 0:1], None, ALU.is_gt))
            c.link(v.tensor_scalar(tmp2, iota_f[:, 0:NB], float(P), pcol[:, 0:1], ALU.mult, ALU.add))
            c.link(v.tensor_scalar(valid, tmp2, float(N), None, ALU.is_lt))
            c.link(v.tensor_scalar(e_less, iota_f[:, 0:NE], float(NE), None, ALU.subtract))
            c.link(v.tensor_scalar(gran, iota_f[:, 0:EG], float(BS), None, ALU.mult))
            c.link(v.memset(carry_on, 1.0))
            c.link(v.memset(carry_on[:, :, 0], 0.0))
            v.wait_ge(b1_T_done, 1)
            v.tensor_copy(b1_T, bank[7][:, 0:NE * FC]).then_inc(b1_T_ready, 1)

            def each_b(t):
                return t.unsqueeze(1).broadcast_to([P, NB, NE])

            def each_e(t):
                return t.unsqueeze(2).broadcast_to([P, NB, NE])

            v.wait_ge(logits_done, NB)
            c.link(v.tensor_tensor(lg, bank[2][:, 0:NB * NE].rearrange("p (b e) -> p b e", e=NE),
                                   each_b(br_bc), ALU.add))
            for top, oh in ((top1, oh_a), (top2, oh_b)):
                c.link(v.tensor_reduce(top, lg, AX.X, ALU.max))
                c.link(v.tensor_tensor(eq, lg, each_e(top), ALU.is_equal))
                c.link(v.tensor_tensor(eq, eq, each_b(e_less), ALU.mult))
                c.link(v.tensor_reduce(tmp2, eq, AX.X, ALU.min))
                c.link(v.tensor_tensor(oh, each_b(e_less), each_e(tmp2), ALU.is_equal))
                if oh is oh_a:
                    c.link(v.scalar_tensor_tensor(lg, oh, -BIG, lg, ALU.mult, ALU.add))
            v.tensor_tensor(tmp1, top2, top1, ALU.subtract).then_inc(gap_ready, 1)
            c.link(v.tensor_tensor(mask, oh_a, oh_b, ALU.add))
            v.tensor_tensor(mask, mask, each_e(valid), ALU.mult).then_inc(mask_ready, 1)
            v.wait_ge(gap_exp, 1)
            c.link(v.tensor_scalar(w_a, w_b, 1.0, None, ALU.add))
            c.link(v.reciprocal(w_a, w_a))
            c.link(v.tensor_tensor(w_b, w_b, w_a, ALU.mult))
            v.wait_ge(ranks_done, 1)
            c.link(v.tensor_copy(tot, bank[4][:, 0:NB * NE].rearrange("p (b e) -> p b e", e=NE)))
            c.link(v.tensor_copy(rank, bank[3][:, 0:NB * NE].rearrange("p (b e) -> p b e", e=NE)))
            tot_eb = eq.rearrange("p b e -> p (b e)")
            c.link(v.tensor_copy(tot_eb.rearrange("p (e b) -> p e b", e=NE),
                                 tot.rearrange("p b e -> p e b")))
            c.link(v.tensor_tensor_scan(incl.rearrange("p e b -> p (e b)"),
                                        carry_on.rearrange("p e b -> p (e b)"), tot_eb, 0.0,
                                        ALU.mult, ALU.add))
            c.link(v.tensor_tensor(n_cmp, incl[:, :, NB - 1].unsqueeze(2).broadcast_to([P, NE, EG]),
                                   gran.unsqueeze(1).broadcast_to([P, NE, EG]), ALU.is_gt))
            c.link(v.tensor_reduce(n_blk, n_cmp, AX.X, ALU.add))
            c.link(v.tensor_tensor_scan(n_incl, ones[:, 0:NE], n_blk, 0.0, ALU.mult, ALU.add))
            c.link(v.tensor_tensor(n_excl, n_incl, n_blk, ALU.subtract))
            c.link(v.tensor_tensor(rank, rank, incl.rearrange("p e b -> p b e"), ALU.add))
            c.link(v.tensor_tensor(rank, rank, tot, ALU.subtract))
            c.link(v.scalar_tensor_tensor(pos_e, each_b(n_excl), float(BS), rank, ALU.mult, ALU.add))
            for k, oh in enumerate((oh_a, oh_b)):
                c.link(v.tensor_tensor(oh, oh, pos_e, ALU.mult))
                c.link(v.tensor_reduce(tmp2, oh, AX.X, ALU.add))
                c.link(v.tensor_copy(pos_i[:, k, :], tmp2))
            c.link(v.tensor_tensor(blk_cmp, n_excl[:, 1:NE].unsqueeze(1).broadcast_to([P, NBLK, NE - 1]),
                                   iota_f[:, 0:NBLK].unsqueeze(2).broadcast_to([P, NBLK, NE - 1]),
                                   ALU.is_le))
            c.link(v.tensor_reduce(blk_f, blk_cmp, AX.X, ALU.add))
            v.tensor_copy(blk_e, blk_f[0:1, :]).then_inc(pos_ready, 1)

            def pick_w1(j, u):
                e = v.value_load(blk_e[0:1, bass.ds(j, 1)], min_val=0, max_val=NE - 1)
                v.tensor_copy(w1_now[:, u, :, :].rearrange("p k h -> p (k h)"),
                              w1_all[:, bass.ds(e, 1), :].rearrange("p e w -> p (e w)"))\
                 .then_inc(w1_picked, 1)

            def turned_copy(j, u):
                v.wait_ge(xsT_done, j + 1)
                v.tensor_copy(xsT[:, u, :, :].rearrange("p k n -> p (k n)"), bank[u][:, :])\
                 .then_inc(xsT_copied, 1)

            def add_b2(j, u, n, first=False):
                e = v.value_load(blk_e[0:1, bass.ds(j, 1)], min_val=0, max_val=NE - 1)
                v.wait_ge(l2_done, j + 1)
                if not first:
                    v.wait_ge(y_stored[u], 16 * n)
                v.tensor_tensor(y_out[:, u, :, :], bank[6 + u][:, :].rearrange("p (m f) -> p m f", m=BM),
                                b2_bc[:, bass.ds(e, 1), :].broadcast_to([P, BM, F]), ALU.add)\
                 .then_inc(y_ready, 1)

            v.wait_ge(pos_ready, 1)
            v.wait_ge(w1_in, 16 * NE)
            pick_w1(0, 0)
            pick_w1(1, 1)
            turned_copy(0, 0)
            turned_copy(1, 1)
            v.wait_ge(l1_done, FC // 2)
            pick_w1(2, 0)
            turned_copy(2, 0)
            add_b2(0, 0, 0, first=True)
            v.wait_ge(l1_done, FC // 2 * 2)
            pick_w1(3, 1)
            turned_copy(3, 1)
            add_b2(1, 1, 0, first=True)
            with v.Fori(1, (NBLK - 2) // 2, 1) as i:
                v.wait_ge(l1_done, FC // 2 * (2 * i + 1))
                pick_w1(2 * i + 2, 0)
                turned_copy(2 * i + 2, 0)
                add_b2(2 * i, 0, i)
                v.wait_ge(l1_done, FC // 2 * (2 * i + 2))
                pick_w1(2 * i + 3, 1)
                turned_copy(2 * i + 3, 1)
                add_b2(2 * i + 1, 1, i)
            for j in range(2 * ((NBLK - 2) // 2), NBLK):
                if j + 2 < NBLK:
                    v.wait_ge(l1_done, FC // 2 * (j + 1))
                    pick_w1(j + 2, j % 2)
                    turned_copy(j + 2, j % 2)
                add_b2(j, j % 2, j // 2)
            def combine(b, u, n):
                row = block_of(x1, b)
                v.wait_ge(y_got[u], 16 * TOP * (n + 1))
                c.link(v.scalar_tensor_tensor(row, y_in[:, u, 0, :], w_a[:, bass.ds(b, 1)], row,
                                              ALU.mult, ALU.add))
                v.scalar_tensor_tensor(row, y_in[:, u, 1, :], w_b[:, bass.ds(b, 1)], row,
                                       ALU.mult, ALU.add).then_inc(combined, 1)

            with v.Fori(0, NB // YS, 1) as i:
                c.enter(i, YS)
                for u in range(YS):
                    combine(i * YS + u, u, i)
            c.leave(NB // YS)


_INS = ["x", "src", "dst", "L0_gnn_W", "L0_gnn_a_src", "L0_gnn_a_dst", "L0_ffn_gamma", "L0_ffn_beta",
        "L0_ffn_Wr", "L0_ffn_br", "L0_ffn_W1", "L0_ffn_b1", "L0_ffn_W2", "L0_ffn_b2"]


def kernel(**inputs):
    import numpy as _np
    import concourse.bacc as _bacc
    from concourse import mybir as _mybir
    from concourse.bass_utils import run_bass_kernel_spmd as _run

    nc = _bacc.Bacc("TRN2", target_bir_lowering=False, num_devices=1)
    arrays, args = {}, []
    for name in _INS:
        a = _np.ascontiguousarray(inputs[name])
        arrays[f"in_{name}"] = a
        args.append(nc.dram_tensor(f"in_{name}", a.shape, _mybir.dt.from_np(a.dtype), kind="ExternalInput").ap())
    x = inputs["x"]
    args.append(nc.dram_tensor("out", x.shape, _mybir.dt.from_np(_np.dtype("float32")), kind="ExternalOutput").ap())
    gat_moe_kernel(nc, *args)
    r = _run(nc, [arrays], core_ids=[0])
    return r.results[0]["out"]
```

```python
import concourse.bass as bass
from concourse import mybir
from contextlib import ExitStack


class Chain:

    def __init__(self, eng, sem):
        self.eng, self.sem, self.done, self.trip, self.per_trip, self.base = eng, sem, 0, 0, 0, 0

    def link(self, ins):
        self.done += 1
        ins.then_inc(self.sem, 1)
        self.eng.wait_ge(self.sem, self.done + self.trip * self.per_trip)

    def enter(self, trip, per_trip):
        self.trip, self.per_trip, self.base = trip, per_trip, self.done

    def leave(self, trips):
        assert self.done - self.base == self.per_trip, (self.done - self.base, self.per_trip)
        self.done = self.base + trips * self.per_trip
        self.trip, self.per_trip = 0, 0


def gat_moe_kernel(nc, x, src, dst, gnn_w, a_src, a_dst, gamma, beta, wr, br, w1, b1, w2, b2, out):
    fp32, bf16, i32 = mybir.dt.float32, mybir.dt.bfloat16, mybir.dt.int32
    ALU = mybir.AluOpType
    ACT = mybir.ActivationFunctionType
    AX = mybir.AxisListType
    P = 128

    N, F = x.shape
    H, _, FO = gnn_w.shape
    HF = H * FO
    KF = F // P
    E = src.shape[0]
    TPR = 5
    RL = TPR * P
    Q = E // RL
    assert Q * RL == E and Q <= P
    NB = (N + P - 1) // P
    LASTB = N - (NB - 1) * P
    G = Q + NB - 1
    RING = 25
    assert Q % RING == 0 and RING >= NB + TPR
    MW = HF + H
    NE, _, HID = w1.shape
    FC = HID // P
    BS = 256
    BM = BS // P
    TOP = 2
    NBLK = (TOP * N + NE * (BS - 1)) // BS
    EG = (N + BS - 1) // BS
    BIG = 1e38
    EPS = 1e-5

    h_tab = nc.dram_tensor("h_tab", (NB * P, HF), fp32).ap()
    lo_tab = nc.dram_tensor("lo_tab", (Q, RL), bf16).ap()
    dst_tab = nc.dram_tensor("dst_tab", (Q, RL), fp32).ap()
    ed_tab = nc.dram_tensor("ed_tab", (E + NB * P, H), fp32).ap()
    xs_tab = nc.dram_tensor("xs_tab", (NBLK * BS, F), fp32).ap()
    ys_tab = nc.dram_tensor("ys_tab", (NBLK * BS, F), fp32).ap()
    ed_rows = ed_tab[0:E, :].rearrange("(q j) h -> q (j h)", q=Q)
    src_rows = src.rearrange("(q j) -> q j", q=Q)
    dst_rows = dst.rearrange("(q j) -> q j", q=Q)

    ctx = ExitStack()
    with ctx:
        def sb(name, shape, dt=fp32):
            return ctx.enter_context(nc.sbuf_tensor(name, shape, dt))

        def sem(name):
            return ctx.enter_context(nc.semaphore(name))

        psum = ctx.enter_context(nc.psum_tensor("psum", [P, 8, 512], fp32))
        bank = [psum[:, i, :] for i in range(8)]

        ring = sb("ring", [P, RING, TPR, MW])
        ring_flat = ring[:, :, :, :].rearrange("p s r w -> p (s r w)")
        used = [0]

        def early(width, dt=fp32):
            a = ring_flat[:, used[0]:used[0] + width]
            used[0] += width
            return a if dt == fp32 else a.bitcast(dt)

        xs0 = early(NB * F).rearrange("p (b f) -> p b f", b=NB)
        xT0 = early(4 * F).rearrange("p (u b k n) -> p u b k n", u=2, b=2, k=KF)
        h_stage = early(4 * HF).rearrange("p (u b f) -> p u b f", u=2, b=2)
        wide = HF + 2 * H
        w_ext = early(KF * wide).rearrange("p (k w) -> p k w", k=KF)
        a_bc = early(2 * HF).rearrange("p (s f) -> p s f", s=2)
        w_tmp = early(2 * HF).rearrange("p (s f) -> p s f", s=2)
        q_tmp = early(NB * Q).rearrange("p (b q) -> p b q", b=NB)
        path_tmp = early(G * (NB - 1)).rearrange("p (g b) -> p g b", b=NB - 1)
        src_f = early(RL)
        lo_i = early(RL, i32)
        lo_b = early(RL // 2, bf16)
        hi_i = early(Q * TPR, i32)
        diag = early(Q)
        src_i = early(RL, i32)
        dst_i = early(RL + 2, i32)
        zeros = early(RL * H)
        ROWBUF = 12
        drow = early(ROWBUF * RL).rearrange("p (u j) -> p u j", u=ROWBUF)
        dst_f = early(RL + 2)
        shift = early(P)
        corner = early(P)
        st0 = early(NB * 6).rearrange("p (b s) -> p b s", s=6)
        mean, rstd, sm1, sm2, qn, node_id = (early(NB) for _ in range(6))
        qi = early(NB, i32)
        start = early(NB + 1)
        coef = early(3 * H)
        enters = early(NB - 1)
        iota_g = early(G)
        slot_f, path_f = early(G)[0:1, :], early(G)[0:1, :]
        assert used[0] <= RING * TPR * MW, used

        keep = sb("keep", [P, RL + 1])
        reset = sb("reset", [P, RL + 1])
        srcA = sb("srcA", [P, Q + 1, TPR], i32)
        dstA = sb("dstA", [P, Q, TPR])
        hiA = sb("hiA", [P, Q, TPR], bf16)
        exA = sb("exA", [P, Q, TPR, H])
        esB = sb("esB", [P, H, RL])
        edB = sb("edB", [P, RL, H])
        OHS = 5
        shared = sb("shared", [P, OHS * RL])
        half = OHS * RL // 2
        bwdB = shared[:, 0:H * RL].rearrange("p (h j) -> p h j", h=H)
        dst_oh = shared[:, :].rearrange("p (u r d) -> p u r d", u=OHS, r=TPR)
        acc = sb("acc", [P, NB, MW])
        acc_flat = acc[:, :, :].rearrange("p b w -> p (b w)")
        mxB = acc_flat[:, 0:H * RL].rearrange("p (h j) -> p h j", h=H)
        after = H * RL + TPR * H * NB
        coef_row = acc_flat[0:H, after:after + 3 * Q].rearrange("h (n q) -> h n q", n=3)
        carry_row = acc_flat[0:H, after + 3 * Q:after + 4 * Q + 1]
        carry = acc_flat[:, after + 4 * Q + 1:after + 4 * Q + 1 + H]
        half = OHS * RL // 2
        lo_bc = shared[:, 0:half].bitcast(bf16).rearrange("p (u j) -> p u j", u=OHS)
        lo_oh = shared[:, half:2 * half].bitcast(bf16).rearrange("p (u j) -> p u j", u=OHS)
        es_w, hi_w = TPR * H * NB, TPR * NB // 2
        es_sel = acc_flat[:, 0:OHS * es_w].rearrange("p (u w) -> p u w", u=OHS)
        hi_oh = acc_flat[:, OHS * es_w:OHS * (es_w + hi_w)].bitcast(bf16)\
            .rearrange("p (u r b) -> p u r b", u=OHS, r=TPR)
        ACT_ROWS = (1, 3)
        off = acc_flat[:, OHS * (es_w + hi_w):OHS * (es_w + hi_w) + len(ACT_ROWS) * RL // 2]\
            .bitcast(bf16).rearrange("p (u j) -> p u j", j=RL)
        assert OHS * (es_w + hi_w) + len(ACT_ROWS) * RL // 2 <= after

        ident = sb("ident", [P, P])
        ones = sb("ones", [P, P])
        iota_f = sb("iota_f", [P, P])
        pcol = sb("pcol", [P, 1])
        minus_p = sb("minus_p", [P, 1])
        spos = sb("spos", [P, NB], i32)
        e_node = sb("e_node", [P, NB, 2 * H])
        t3 = sb("t3", [P, 3, H, NB], bf16)
        beta_f = sb("beta_f", [P, G])
        t_res = sb("t_res", [P, H, NB])
        beta_i = sb("beta_i", [1, G], i32)
        tau_i = sb("tau_i", [1, G], i32)
        slot_i = sb("slot_i", [1, G], i32)
        ring_slot = sb("ring_slot", [1, Q], i32)
        picks = sb("picks", [P, RING, TPR], i32)

        edB_flat = edB[:, :, :].rearrange("p j h -> p (j h)")
        gamma_bc, beta_bc = edB_flat[:, 0:F], edB_flat[:, F:2 * F]
        wr_sb = edB_flat[:, 2 * F:2 * F + KF * NE].rearrange("p (k e) -> p k e", k=KF)
        at = 2 * F + KF * NE
        br_bc = edB_flat[:, at:at + NE]
        b1_rows = edB_flat[0:NE * FC, at + NE:at + NE + P]
        b1_T = edB_flat[:, at + NE + P:at + NE + P + NE * FC]
        at += NE + P + NE * FC
        zero_width = NBLK * BS * F // P // 9
        zero_src = edB_flat[:, 2 * F * KF:2 * F * KF + zero_width]
        assert zero_width * 9 * P == NBLK * BS * F and at <= 2 * F * KF
        assert 2 * F * KF + zero_width <= RL * H
        b2_bc = esB[:, :, :].rearrange("p h j -> p (h j)")[:, 0:NE * F].rearrange("p (e f) -> p e f", e=NE)
        used[0] = 0
        late = early
        xn1 = late(NB * F).rearrange("p (b f) -> p b f", b=NB)
        xn_u = late(2 * F).rearrange("p (u f) -> p u f", u=2)
        st1 = late(NB * 6).rearrange("p (b s) -> p b s", s=6)
        mean1, rstd1, tmp1, tmp2, top1, top2, w_a, w_b, valid = (late(NB) for _ in range(9))
        rden = late(NB * H).rearrange("p (b h) -> p b h", h=H)
        xT1 = late(2 * F).rearrange("p (u k n) -> p u k n", u=2, k=KF)
        upper = late(P)
        lg, eq, oh_a, oh_b, mask, pos_e, rank, tot = (
            late(NB * NE).rearrange("p (b e) -> p b e", e=NE) for _ in range(8))
        incl = late(NE * NB).rearrange("p (e b) -> p e b", e=NE)
        carry_on = late(NE * NB).rearrange("p (e b) -> p e b", e=NE)
        e_less = late(NE)
        gran = late(EG)
        n_blk, n_incl, n_excl = late(NE), late(NE), late(NE)
        n_cmp = late(NE * EG).rearrange("p (e g) -> p e g", e=NE)
        blk_cmp = late(NBLK * (NE - 1)).rearrange("p (j e) -> p j e", j=NBLK)
        blk_f = late(NBLK)
        blk_e = late(NBLK, i32)[0:1, :]
        pos_i = late(TOP * NB, i32).rearrange("p (k b) -> p k b", k=TOP)
        w1_all = late(NE * KF * HID).rearrange("p (e w) -> p e w", e=NE)
        w2_flat = late(NE * FC * F)
        w2_all = w2_flat.rearrange("p (e c f) -> p e c f", e=NE, c=FC)
        W2_FIRST = (NE * FC * F - NB * F) // (FC * F)
        x_again = w2_flat[:, NE * FC * F - NB * F:].rearrange("p (b f) -> p b f", b=NB)
        w1_now = late(2 * KF * HID).rearrange("p (u k h) -> p u k h", u=2, k=KF)
        xs_in = late(2 * BM * F).rearrange("p (u m f) -> p u m f", u=2, m=BM)
        xsT = late(2 * KF * BS).rearrange("p (u k n) -> p u k n", u=2, k=KF)
        hT = exA[:, :, :, :].rearrange("p q r h -> p (q r h)")[:, 0:2 * FC * BS]\
            .rearrange("p (u c n) -> p u c n", u=2, c=FC)
        y_out = shared[:, 0:2 * BM * F].rearrange("p (u m f) -> p u m f", u=2, m=BM)
        YS = 4
        y_in = shared[:, 2 * BM * F:(2 * BM + YS * TOP) * F]\
            .rearrange("p (u k f) -> p u k f", u=YS, k=TOP)
        assert used[0] <= RING * TPR * MW, used

        s_const = sem("s_const")
        s_pool = sem("s_pool")
        e_copied, t3_ready = sem("e_copied"), sem("t3_ready")
        s_dve = sem("s_dve")
        x_in, w_in, a_in, src_in, dst_in = (sem(n) for n in ("x_in", "w_in", "a_in", "src_in", "dst_in"))
        pads_set = sem("pads_set")
        edges_f, edges_T, edges_A = sem("edges_f"), sem("edges_T"), sem("edges_A")
        lo_ready, lo_stored = sem("lo_ready"), sem("lo_stored")
        dst_stored = sem("dst_stored")
        row_diag, row_ends, q_ready = sem("row_diag"), sem("row_ends"), sem("q_ready")
        rows_got = [sem(f"rows_got{u}") for u in range(ROWBUF)]
        rows_used = sem("rows_used")
        var_ready, std_ready = sem("var_ready"), sem("std_ready")
        wext_ready = sem("wext_ready")
        xn_ready, xT_done, xT_copied, h_done, h_copied = (
            sem(n) for n in ("xn_ready", "xT_done", "xT_copied", "h_done", "h_copied"))
        h_stored = [sem(f"h_stored{u}") for u in range(2)]
        start_ready, next_done, spos_ready = sem("start_ready"), sem("next_done"), sem("spos_ready")
        zeros_set, ed_zeroed, ed_put, ed_in = (
            sem(n) for n in ("zeros_set", "ed_zeroed", "ed_put", "ed_in"))
        lo_in = [sem(f"lo_in{u}") for u in range(OHS)]
        lo_oh_ready = [sem(f"lo_oh_ready{u}") for u in range(OHS)]
        off_ready, minus_p_set = sem("off_ready"), sem("minus_p_set")
        es_done, es_selected, es_picked, hi_oh_ready = (
            sem(n) for n in ("es_done", "es_selected", "es_picked", "hi_oh_ready"))
        esT_done, esB_copied = sem("esT_done"), sem("esB_copied")
        coef_ready, coefT_done, tb_done = sem("coef_ready"), sem("coefT_done"), sem("tb_done")
        tails_ready, tailsT_done, rows_scanned, carry_done = (
            sem(n) for n in ("tails_ready", "tailsT_done", "rows_scanned", "carry_done"))
        score_ready, ex_ready, exT_done, exA_copied = (
            sem(n) for n in ("score_ready", "ex_ready", "exT_done", "exA_copied"))
        early_over, acc_zeroed = sem("early_over"), sem("acc_zeroed")
        picks_set = sem("picks_set")
        gathered = [sem(f"gathered{u}") for u in range(OHS)]
        dst_oh_ready, group_done, flushed = sem("dst_oh_ready"), sem("group_done"), sem("flushed")
        consts_in, b1_T_done, b1_T_ready = sem("consts_in"), sem("b1_T_done"), sem("b1_T_ready")
        zero_ready, xs_zeroed, x_again_in = sem("zero_ready"), sem("xs_zeroed"), sem("x_again_in")
        x_pad_set = sem("x_pad_set")
        xn1_kept = sem("xn1_kept")
        xn1_ready, xT1_done, xT1_copied, logits_done = (
            sem(n) for n in ("xn1_ready", "xT1_done", "xT1_copied", "logits_done"))
        gap_ready, gap_exp, mask_ready, ranks_done, pos_ready = (
            sem(n) for n in ("gap_ready", "gap_exp", "mask_ready", "ranks_done", "pos_ready"))
        xs_put = sem("xs_put")
        x1_made, w1_in, w2_in, w1_picked = (sem(n) for n in ("x1_made", "w1_in", "w2_in", "w1_picked"))
        xs_got = [sem(f"xs_got{u}") for u in range(2)]
        xsT_done, xsT_copied, l1_done, gelu_done, l2_done, y_ready = (
            sem(n) for n in ("xsT_done", "xsT_copied", "l1_done", "gelu_done", "l2_done", "y_ready"))
        y_stored = [sem(f"y_stored{u}") for u in range(2)]
        y_got = [sem(f"y_got{u}") for u in range(YS)]
        combined = sem("combined")
        s_out = sem("s_out")
        block = ctx.enter_context(nc.Block())

        @block.sync
        def _(sp):
            sp.wait_ge(pads_set, 1)
            sp.dma_start(dst_i[0:1, 1:RL + 2], dst[0:RL + 1].rearrange("(a j) -> a j", a=1))\
              .then_inc(dst_in, 16)
            for lo, hi in ((1, 65), (65, Q - 1)):
                sp.dma_start(dst_i[lo:hi, 1:RL + 1], dst_rows[lo:hi, :]).then_inc(dst_in, 16)
            sp.dma_start(dst_i[Q - 1:Q, 0:RL + 1],
                         dst[(Q - 1) * RL - 1:E].rearrange("(a j) -> a j", a=1)).then_inc(dst_in, 16)
            prev = dst_rows[0:Q - 2, RL - 1:RL]
            nxt = dst_rows[2:Q, 0:1]
            with nc.allow_non_contiguous_dma(reason="one element a row"):
                sp.dma_start(dst_i[1:Q - 1, 0:1], prev).then_inc(dst_in, 16)
                sp.dma_start(dst_i[1:Q - 1, RL + 1:RL + 2], nxt).then_inc(dst_in, 16)
            sp.dma_start(src_i[0:Q, :], src_rows).then_inc(src_in, 16)
            sp.wait_ge(pads_set, 2)
            full = (NB - 1) * P
            sp.dma_start(xs0[:, 0:NB - 1, :], x[0:full, :].rearrange("(b p) f -> p b f", p=P))\
              .then_inc(x_in, 16)
            sp.dma_start(xs0[0:LASTB, NB - 1, :], x[full:N, :]).then_inc(x_in, 16)
            for k in range(KF):
                sp.dma_start(w_ext[:, k, 0:HF].rearrange("p (h o) -> p h o", h=H),
                             gnn_w[:, k * P:(k + 1) * P, :].rearrange("h f o -> f h o"))\
                  .then_inc(w_in, 16)
            for s, a in enumerate((a_src, a_dst)):
                sp.dma_start(a_bc[:, s, :], a.rearrange("h o -> (h o)").partition_broadcast(P))\
                  .then_inc(a_in, 16)
            sp.wait_ge(edges_f, 1)
            sp.dma_start(dst_tab, dst_f[0:Q, 1:RL + 1]).then_inc(dst_stored, 16)
            sp.wait_ge(lo_ready, 1)
            sp.dma_start(lo_tab, lo_b[0:Q, :]).then_inc(lo_stored, 16)
            sp.wait_ge(zeros_set, 1)
            sp.dma_start(ed_rows, zeros[0:Q, :]).then_inc(ed_zeroed, 16)
            def lo_row(q, u, n=None):
                if n is not None:
                    sp.wait_ge(lo_oh_ready[u], n)
                sp.dma_start(lo_bc[:, u, :],
                             lo_tab[bass.ds(q, 1), :].rearrange("a j -> (a j)").partition_broadcast(P))\
                  .then_inc(lo_in[u], 16)

            sp.wait_ge(lo_stored, 16)
            for u in range(OHS):
                lo_row(u, u)
            for i in range(NB // 2):
                sp.wait_ge(h_copied, i + 1)
                sp.dma_start(h_tab[2 * i * P:(2 * i + 2) * P, :].rearrange("(b p) f -> p b f", p=P),
                             h_stage[:, i % 2, :, :]).then_inc(h_stored[i % 2], 16)
            with sp.Fori(1, Q // OHS, 1) as i:
                for u in range(OHS):
                    lo_row(i * OHS + u, u, i)
            sp.wait_ge(ed_put, 16 * NB)
            sp.dma_start(edB[0:Q, :, :].rearrange("q j h -> q (j h)"), ed_rows).then_inc(ed_in, 16)
            sp.wait_ge(exT_done, TPR)
            for to, frm in ((gamma_bc, gamma.partition_broadcast(P)), (beta_bc, beta.partition_broadcast(P)),
                            (br_bc, br.partition_broadcast(P)),
                            (wr_sb, wr.rearrange("(k p) e -> p k e", p=P)),
                            (b1_rows, b1.rearrange("e (c p) -> (e c) p", p=P)),
                            (b2_bc.rearrange("p e f -> p (e f)"),
                             b2.rearrange("e f -> (e f)").partition_broadcast(P))):
                sp.dma_start(to, frm).then_inc(consts_in, 16)
            sp.wait_ge(zero_ready, 1)
            xs_flat = xs_tab.rearrange("(p a) f -> p (a f)", p=P)
            for n in range(9):
                sp.dma_start(xs_flat[:, n * zero_width:(n + 1) * zero_width], zero_src)\
                  .then_inc(xs_zeroed, 16)
            sp.wait_ge(group_done, G)
            sp.dma_start(x_again[:, 0:NB - 1, :], x[0:full, :].rearrange("(b p) f -> p b f", p=P))\
              .then_inc(x_again_in, 16)
            sp.wait_ge(x_pad_set, 1)
            sp.dma_start(x_again[0:LASTB, NB - 1, :], x[full:N, :]).then_inc(x_again_in, 16)

            for e in range(NE):
                sp.dma_start(w1_all[:, e, :].rearrange("p (k h) -> p k h", k=KF),
                             w1[e, :, :].rearrange("(k p) h -> p k h", p=P)).then_inc(w1_in, 16)
            for e in range(NE):
                if e == W2_FIRST:
                    sp.wait_ge(x1_made, 1)
                sp.dma_start(w2_all[:, e, :, :], w2[e, :, :].rearrange("(c p) f -> p c f", p=P))\
                  .then_inc(w2_in, 16)

            def load_slots(j, u, first=False):
                if not first:
                    sp.wait_ge(xsT_done, j - 1)
                sp.dma_start(xs_in[:, u, :, :],
                             xs_tab[bass.ds(j * BS, BS), :].rearrange("(m p) f -> p m f", p=P))\
                  .then_inc(xs_got[u], 16)

            sp.wait_ge(xs_put, 16 * TOP * NB)
            load_slots(0, 0, first=True)
            load_slots(1, 1, first=True)
            with sp.Fori(1, NBLK // 2, 1) as i:
                load_slots(2 * i, 0)
                load_slots(2 * i + 1, 1)
            for j in range(NBLK // 2 * 2, NBLK):
                load_slots(j, j % 2)
            with sp.Fori(0, NB - 1, 1) as b:
                sp.wait_ge(combined, b + 1)
                sp.dma_start(out[bass.ds(b * P, P), :],
                             acc[:, bass.ds(b, 1), 0:F].rearrange("p b f -> p (b f)")).then_inc(s_out, 16)
            sp.wait_ge(combined, NB)
            sp.dma_start(out[full:N, :], acc[0:LASTB, NB - 1, 0:F]).then_inc(s_out, 16)
            sp.wait_ge(s_out, 16 * NB)

        @block.gpsimd
        def _(pool):
            for m in (ident, shift, corner):
                pool.memset(m[:, :], 0.0).then_inc(s_pool, 1)
            pool.memset(ones[:, :], 1.0).then_inc(s_const, 1)
            pool.memset(zeros[0:Q, :], 0.0).then_inc(zeros_set, 1)
            pool.memset(srcA[:, Q, :], 0).then_inc(s_const, 1)
            pool.wait_ge(s_pool, 3)
            for m, base, mult in ((ident, 0, 1), (shift, -1, 1), (corner, P - 1, P)):
                pool.affine_select(out=m[:, :], in_=m[:, :], compare_op=ALU.not_equal, fill=1.0,
                                   base=base, pattern=[[-1, P]], channel_multiplier=mult)\
                    .then_inc(s_const, 1)
            for t, base, pattern, mult in ((iota_f, 0, [[1, P]], 0), (iota_g, 0, [[1, G]], 0),
                                           (pcol, 0, [[1, 1]], 1), (node_id, 0, [[P, NB]], 1),
                           (ring_slot, 0, [[0, Q // RING], [1, RING]], 0)):
                pool.iota(t[:, :], pattern=pattern, base=base, channel_multiplier=mult,
                          allow_small_or_imprecise_dtypes=True).then_inc(s_const, 1)
            pool.wait_ge(dst_stored, 16)
            pool.wait_ge(q_ready, 1)
            for b in range(NB):
                if b >= ROWBUF:
                    pool.wait_ge(rows_used, b - ROWBUF + 1)
                pool.indirect_dma_start(
                    out=drow[:, b % ROWBUF, :], out_offset=None, in_=dst_tab,
                    in_offset=bass.IndirectOffsetOnAxis(ap=qi[:, b:b + 1], axis=0))\
                    .then_inc(rows_got[b % ROWBUF], 16)
            def pick_row(t, u):
                pool.tensor_copy(picks[:, u, :],
                                 srcA[:, bass.ds(t, 1), :].rearrange("p q r -> p (q r)"))\
                    .then_inc(picks_set, 1)

            def gather_row(trip, u, first):
                t = trip * RING + u
                if not first or u >= OHS:
                    pool.wait_ge(gathered[u % OHS], 16 * TPR * (trip * (RING // OHS) + u // OHS))
                if not first:
                    pool.wait_ge(group_done, t - RING + NB)
                pool.wait_ge(picks_set, t + 1)
                pick_row(t + 1, (u + 1) % RING)
                for r in range(TPR):
                    pool.indirect_dma_start(
                        out=ring[:, u, r, 0:HF], out_offset=None, in_=h_tab,
                        in_offset=bass.IndirectOffsetOnAxis(ap=picks[:, u, r:r + 1], axis=0))\
                        .then_inc(gathered[u % OHS], 16)

            pool.wait_ge(h_stored[0], 16 * ((NB // 2 + 1) // 2))
            pool.wait_ge(h_stored[1], 16 * (NB // 2 // 2))
            pool.wait_ge(edges_A, 4)
            pool.wait_ge(early_over, 1)
            pool.wait_ge(ed_zeroed, 16)
            pool.wait_ge(lo_stored, 16)
            pick_row(0, 0)
            for u in range(RING):
                gather_row(0, u, True)
                if u == 2 * OHS:
                    pool.wait_ge(spos_ready, 1)
                    for b in range(NB):
                        pool.indirect_dma_start(
                            out=ed_tab, out_offset=bass.IndirectOffsetOnAxis(ap=spos[:, b:b + 1], axis=0),
                            in_=e_node[:, b, H:2 * H], in_offset=None).then_inc(ed_put, 16)
            pool.wait_ge(score_ready, 1)
            pool.memset(acc_flat, 0.0).then_inc(acc_zeroed, 1)
            pool.memset(zero_src, 0.0).then_inc(zero_ready, 1)
            with pool.Fori(1, Q // RING, 1) as trip:
                for u in range(RING):
                    gather_row(trip, u, False)

            pool.wait_ge(pos_ready, 1)
            pool.wait_ge(xs_zeroed, 16 * 9)
            for k in range(TOP):
                for b in range(NB):
                    rows = P if b < NB - 1 else LASTB
                    pool.indirect_dma_start(
                        out=xs_tab, out_offset=bass.IndirectOffsetOnAxis(ap=pos_i[0:rows, k, b:b + 1], axis=0),
                        in_=xn1[0:rows, b, :], in_offset=None).then_inc(xs_put, 16)
            pool.wait_ge(y_stored[0], 16 * ((NBLK + 1) // 2))
            pool.wait_ge(y_stored[1], 16 * (NBLK // 2))
            for b in range(NB):
                rows = P if b < NB - 1 else LASTB
                if b >= YS:
                    pool.wait_ge(combined, b - YS + 1)
                for k in range(TOP):
                    pool.indirect_dma_start(
                        out=y_in[0:rows, b % YS, k, :], out_offset=None, in_=ys_tab,
                        in_offset=bass.IndirectOffsetOnAxis(ap=pos_i[0:rows, k, b:b + 1], axis=0))\
                        .then_inc(y_got[b % YS], 16)

        NCONST = 10

        @block.tensor
        def _(pe):
            pe.wait_ge(s_const, NCONST)
            pe.wait_ge(edges_f, 1)
            for r in range(TPR):
                for n, row in enumerate((src_f[0:Q, :], dst_f[0:Q, 1:RL + 1])):
                    to = bank[4 + n][:, r * Q:(r + 1) * Q] if r < 4 else bank[6][:, n * Q:(n + 1) * Q]
                    last = pe.transpose(to, row[:, r * P:(r + 1) * P], ident[0:Q, 0:Q])
            last.then_inc(edges_T, 1)
            pe.wait_ge(row_diag, 1)
            pe.matmul(bank[7][:, 0:Q], ones[0:Q, :], diag[0:Q, :], start=True, stop=True)\
              .then_inc(row_ends, 1)
            pe.wait_ge(q_ready, 1)
            pe.matmul(bank[7][:, 0:NB], ones[0:1, :], qn[0:1, :], start=True, stop=True)\
              .then_inc(tb_done, 1)

            pe.wait_ge(wext_ready, 1)

            def transposes(i):
                pe.wait_ge(xn_ready, 2 * i + 2)
                if i >= 2:
                    pe.wait_ge(xT_copied, i - 1)
                for b in range(2):
                    for k in range(KF):
                        last = pe.transpose(bank[i % 2][:, (b * KF + k) * P:(b * KF + k + 1) * P],
                                            xs0[:, 2 * i + b, k * P:(k + 1) * P], ident[:, :])
                last.then_inc(xT_done, 1)

            def project(i):
                pe.wait_ge(xT_copied, i + 1)
                if i >= 2:
                    pe.wait_ge(h_copied, i - 1)
                for b in range(2):
                    for k in range(KF):
                        last = pe.matmul(bank[2 + 2 * (i % 2) + b][:, 0:wide], xT0[:, i % 2, b, k, :],
                                         w_ext[:, k, :], start=(k == 0), stop=(k == KF - 1))
                last.then_inc(h_done, 1)

            pe.wait_ge(edges_A, 4)
            transposes(0)
            for i in range(NB // 2):
                if i + 1 < NB // 2:
                    transposes(i + 1)
                project(i)

            pe.wait_ge(start_ready, 1)
            pe.matmul(bank[7][:, 0:NB], shift[:, :], start[:, 0:NB], start=True, stop=False)
            pe.matmul(bank[7][:, 0:NB], corner[:, :], start[:, 1:NB + 1], start=False,
                      stop=True).then_inc(next_done, 1)
            pe.wait_ge(coef_ready, 1)
            pe.wait_ge(spos_ready, 1)
            for n in range(3):
                last = pe.transpose(bank[7][0:H, n * Q:(n + 1) * Q], coef[0:Q, n * H:(n + 1) * H],
                                    ident[0:Q, 0:Q])
            last.then_inc(coefT_done, 1)

            def look_up(q, u, n, first=False):
                pe.wait_ge(lo_oh_ready[u], n + 1)
                if not first:
                    pe.wait_ge(es_selected, q - OHS + 1)
                for r in range(TPR):
                    for part in range(3):
                        last = pe.matmul(bank[u][:, r * H * NB:(r + 1) * H * NB],
                                         lo_oh[:, u, r * P:(r + 1) * P],
                                         t3[:, part, :, :].rearrange("p h b -> p (h b)"),
                                         start=(part == 0), stop=(part == 2))
                last.then_inc(es_done, 1)

            pe.wait_ge(h_copied, NB // 2)
            pe.wait_ge(t3_ready, 1)
            for u in range(OHS):
                look_up(u, u, 0, first=True)
            with pe.Fori(1, Q // OHS, 1) as i:
                for u in range(OHS):
                    look_up(i * OHS + u, u, i)
            pe.wait_ge(es_picked, Q)
            for r in range(TPR):
                if r >= 2:
                    pe.wait_ge(esB_copied, r - 1)
                for h in range(H):
                    last = pe.transpose(bank[5 + r % 2][0:Q, h * P:(h + 1) * P], exA[:, :, r, h],
                                        ident[:, :])
                last.then_inc(esT_done, 1)
            for n in range(3):
                pe.wait_ge(tails_ready, n + 1)
                tails = (mxB[0:Q, :, RL - 1], mxB[0:Q, :, RL - 1], bwdB[0:Q, :, 0])[n]
                pe.transpose(bank[7][0:H, 0:Q], tails, ident[0:Q, 0:Q]).then_inc(tailsT_done, 1)
                pe.wait_ge(rows_scanned, n + 1)
                pe.transpose(bank[7][0:Q, 256:256 + H], carry_row[:, (0, 0, 1)[n]:(0, 0, 1)[n] + Q],
                             ident[0:H, 0:H]).then_inc(carry_done, 1)
            pe.wait_ge(ex_ready, 1)
            for r in range(TPR):
                if r >= 2:
                    pe.wait_ge(exA_copied, r - 1)
                for h in range(H):
                    last = pe.transpose(bank[5 + r % 2][:, h * Q:(h + 1) * Q],
                                        esB[0:Q, h, r * P:(r + 1) * P], ident[0:Q, 0:Q])
                last.then_inc(exT_done, 1)

            def group(i, u, first=False):
                pe.wait_ge(dst_oh_ready, i + 1)
                if not first:
                    pe.wait_ge(flushed, i - OHS + 1)
                slot = pe.value_load(slot_i[0:1, bass.ds(i, 1)], min_val=0, max_val=RING - 1)
                for r in range(TPR):
                    last = pe.matmul(bank[u][:, 0:MW], dst_oh[:, u, r, :],
                                     ring[:, bass.ds(slot, 1), r, :].rearrange("p s w -> p (s w)"),
                                     start=(r == 0), stop=(r == TPR - 1))
                last.then_inc(group_done, 1)

            for u in range(OHS):
                group(u, u, first=True)
            with pe.Fori(1, G // OHS, 1) as i:
                for u in range(OHS):
                    group(i * OHS + u, u)
            for i in range(G // OHS * OHS, G):
                group(i, i % OHS)

            pe.wait_ge(consts_in, 16 * 6)
            pe.transpose(bank[7][:, 0:NE * FC], b1_rows, ident[0:NE * FC, 0:NE * FC])\
              .then_inc(b1_T_done, 1)

            def node_T(b, u, first=False):
                pe.wait_ge(xn1_ready, b + 1)
                if not first:
                    pe.wait_ge(xT1_copied, b - 1)
                for k in range(KF):
                    last = pe.transpose(bank[u][:, k * P:(k + 1) * P], xn_u[:, u, k * P:(k + 1) * P],
                                        ident[:, :])
                last.then_inc(xT1_done, 1)

            def router(b, u):
                pe.wait_ge(xT1_copied, b + 1)
                for k in range(KF):
                    last = pe.matmul(bank[2][:, bass.ds(b * NE, NE)], xT1[:, u, k, :], wr_sb[:, k, :],
                                     start=(k == 0), stop=(k == KF - 1))
                last.then_inc(logits_done, 1)

            node_T(0, 0, first=True)
            node_T(1, 1, first=True)
            router(0, 0)
            with pe.Fori(1, NB // 2, 1) as i:
                node_T(2 * i, 0)
                router(2 * i - 1, 1)
                node_T(2 * i + 1, 1)
                router(2 * i, 0)
            router(NB - 1, 1)
            pe.wait_ge(mask_ready, 1)
            mask_flat = mask.rearrange("p b e -> p (b e)")
            pe.matmul(bank[3][:, 0:NB * NE], upper, mask_flat, start=True, stop=True)
            pe.matmul(bank[4][:, 0:NB * NE], ones[:, :], mask_flat, start=True, stop=True)\
              .then_inc(ranks_done, 1)

            def slots_T(j, u, n, first=False):
                pe.wait_ge(xs_got[u], 16 * (n + 1))
                if not first:
                    pe.wait_ge(xsT_copied, j - 1)
                for k in range(KF):
                    for m in range(BM):
                        last = pe.transpose(bank[u][:, k * BS + m * P:k * BS + (m + 1) * P],
                                            xs_in[:, u, m, k * P:(k + 1) * P], ident[:, :])
                last.then_inc(xsT_done, 1)

            def layer_1(j, u, first=False):
                pe.wait_ge(xsT_copied, j + 1)
                pe.wait_ge(w1_picked, j + 1)
                if not first:
                    pe.wait_ge(gelu_done, FC * (j - 1))
                for c in range(FC):
                    for k in range(KF):
                        last = pe.matmul(bank[2 + 2 * u + c // 2][:, c % 2 * BS:(c % 2 + 1) * BS],
                                         w1_now[:, u, k, c * P:(c + 1) * P], xsT[:, u, k, :],
                                         start=(k == 0), stop=(k == KF - 1))
                    if c % 2:
                        last.then_inc(l1_done, 1)

            def layer_2(j, u, first=False):
                e = pe.value_load(blk_e[0:1, bass.ds(j, 1)], min_val=0, max_val=NE - 1)
                pe.wait_ge(gelu_done, FC * (j + 1))
                if not first:
                    pe.wait_ge(y_ready, j - 1)
                for m in range(BM):
                    for c in range(FC):
                        last = pe.matmul(bank[6 + u][:, m * F:(m + 1) * F],
                                         hT[:, u, c, m * P:(m + 1) * P],
                                         w2_all[:, bass.ds(e, 1), c, :].rearrange("p e f -> p (e f)"),
                                         start=(c == 0), stop=(c == FC - 1))
                last.then_inc(l2_done, 1)

            pe.wait_ge(w2_in, 16 * NE)
            slots_T(0, 0, 0, first=True)
            layer_1(0, 0, first=True)
            slots_T(1, 1, 0, first=True)
            layer_1(1, 1, first=True)
            layer_2(0, 0, first=True)
            slots_T(2, 0, 1)
            layer_1(2, 0)
            layer_2(1, 1, first=True)
            with pe.Fori(1, (NBLK - 1) // 2, 1) as i:
                slots_T(2 * i + 1, 1, i)
                layer_1(2 * i + 1, 1)
                layer_2(2 * i, 0)
                slots_T(2 * i + 2, 0, i + 1)
                layer_1(2 * i + 2, 0)
                layer_2(2 * i + 1, 1)
            for j in range(2 * ((NBLK - 1) // 2), NBLK):
                if j + 1 < NBLK:
                    slots_T(j + 1, (j + 1) % 2, (j + 1) // 2)
                    layer_1(j + 1, (j + 1) % 2)
                layer_2(j, j % 2)

        @block.scalar
        def _(act):
            act.wait_ge(edges_T, 1)
            for n, to in enumerate((srcA, dstA)):
                act.activation(to[:, 0:Q, 0:4], bank[4 + n][:, 0:4 * Q].rearrange("p (r q) -> p q r", r=4),
                               ACT.Copy).then_inc(edges_A, 1)
                act.activation(to[:, 0:Q, 4], bank[6][:, n * Q:(n + 1) * Q], ACT.Copy).then_inc(edges_A, 1)
            act.wait_ge(var_ready, 1)
            act.activation(rstd[:, :], sm1[:, :], ACT.Sqrt).then_inc(std_ready, 1)
            for i in range(NB // 2):
                act.wait_ge(xT_done, i + 1)
                if i >= 2:
                    act.wait_ge(h_done, i - 1)
                act.activation(xT0[:, i % 2, :, :, :].rearrange("p b k n -> p (b k n)"), bank[i % 2],
                               ACT.Copy).then_inc(xT_copied, 1)
                act.wait_ge(h_done, i + 1)
                two = psum[:, 2 + 2 * (i % 2):4 + 2 * (i % 2), :]
                act.activation(e_node[:, 2 * i:2 * i + 2, :], two[:, :, HF:wide], ACT.Copy)\
                   .then_inc(e_copied, 1)
                if i >= 2:
                    act.wait_ge(h_stored[i % 2], 16 * (i // 2))
                act.activation(h_stage[:, i % 2, :, :], two[:, :, 0:HF], ACT.Copy).then_inc(h_copied, 1)

            def onehot(i, u, n, first=False):
                act.wait_ge(lo_in[u], 16 * (i + 1))
                if not first:
                    act.wait_ge(es_done, OHS * i - OHS + u + 1)
                act.activation(off[:, n, :], lo_bc[:, u, :], ACT.Abs, bias=minus_p[:, 0:1])\
                   .then_inc(off_ready, 1)
                act.wait_ge(off_ready, len(ACT_ROWS) * i + n + 1)
                act.activation(lo_oh[:, u, :], off[:, n, :], ACT.Relu, bias=ones[:, 0:1], scale=-1.0)\
                   .then_inc(lo_oh_ready[u], 1)

            act.wait_ge(minus_p_set, 1)
            for n, u in enumerate(ACT_ROWS):
                onehot(0, u, n, first=True)
            with act.Fori(1, Q // OHS, 1) as i:
                for n, u in enumerate(ACT_ROWS):
                    onehot(i, u, n)

            for r in range(TPR):
                act.wait_ge(esT_done, r + 1)
                act.activation(esB[0:Q, :, r * P:(r + 1) * P],
                               bank[5 + r % 2][0:Q, :].rearrange("q (h p) -> q h p", h=H),
                               ACT.Copy).then_inc(esB_copied, 1)
            act.wait_ge(score_ready, 1)
            act.activation(esB[0:Q, :, :], esB[0:Q, :, :], ACT.Exp).then_inc(ex_ready, 1)
            for r in range(TPR):
                act.wait_ge(exT_done, r + 1)
                act.activation(exA[:, :, r, :].rearrange("p q h -> p h q"),
                               bank[5 + r % 2][:, 0:H * Q].rearrange("p (h q) -> p h q", h=H),
                               ACT.Copy).then_inc(exA_copied, 1)

            for n in range(2):
                act.wait_ge(var_ready, n + 2)
                act.activation(rstd1, tmp1, ACT.Sqrt).then_inc(std_ready, 1)

            def keep_node(b, u):
                act.wait_ge(xn1_ready, b + 1)
                act.activation(xn1[:, bass.ds(b, 1), :].rearrange("p b f -> p (b f)"), xn_u[:, u, :],
                               ACT.Copy).then_inc(xn1_kept, 1)
                act.wait_ge(xT1_done, b + 1)
                act.activation(xT1[:, u, :, :].rearrange("p k n -> p (k n)"), bank[u][:, 0:F],
                               ACT.Copy).then_inc(xT1_copied, 1)

            def keep_node_later(b, u):
                act.wait_ge(logits_done, b - 1)
                keep_node(b, u)

            keep_node(0, 0)
            keep_node(1, 1)
            with act.Fori(1, NB // 2, 1) as i:
                keep_node_later(2 * i, 0)
                keep_node_later(2 * i + 1, 1)
            act.wait_ge(gap_ready, 1)
            act.activation(w_b, tmp1, ACT.Exp).then_inc(gap_exp, 1)

            def hidden(j, u, first=False):
                e = act.value_load(blk_e[0:1, bass.ds(j, 1)], min_val=0, max_val=NE - 1)
                if not first:
                    act.wait_ge(l2_done, j - 1)
                for c in range(FC):
                    if c % 2 == 0:
                        act.wait_ge(l1_done, FC // 2 * j + c // 2 + 1)
                    act.activation(hT[:, u, c, :],
                                   bank[2 + 2 * u + c // 2][:, c % 2 * BS:(c % 2 + 1) * BS], ACT.Gelu,
                                   bias=b1_T[:, bass.ds(e * FC + c, 1)]).then_inc(gelu_done, 1)

            def store_y(j, u):
                act.wait_ge(y_ready, j + 1)
                act.dma_start(ys_tab[bass.ds(j * BS, BS), :].rearrange("(m p) f -> p m f", p=P),
                              y_out[:, u, :, :]).then_inc(y_stored[u], 16)

            act.wait_ge(pos_ready, 1)
            act.wait_ge(b1_T_ready, 1)
            hidden(0, 0, first=True)
            hidden(1, 1, first=True)
            store_y(0, 0)
            with act.Fori(1, NBLK // 2, 1) as i:
                hidden(2 * i, 0)
                store_y(2 * i - 1, 1)
                hidden(2 * i + 1, 1)
                store_y(2 * i, 0)
            for j in range(NBLK // 2 * 2, NBLK + 1):
                if j < NBLK:
                    hidden(j, j % 2)
                store_y(j - 1, (j - 1) % 2)

        @block.vector
        def _(v):
            c = Chain(v, s_dve)
            v.memset(dst_i[0:Q, :], -1).then_inc(pads_set, 1)
            v.memset(xs0[:, NB - 1, :], 0.0).then_inc(pads_set, 1)
            v.wait_ge(dst_in, 96)
            c.link(v.tensor_copy(dst_f[0:Q, :], dst_i[0:Q, :]))
            v.wait_ge(src_in, 16)
            v.tensor_copy(src_f[0:Q, :], src_i[0:Q, :]).then_inc(edges_f, 1)
            c.link(v.tensor_scalar(lo_i[0:Q, :], src_i[0:Q, :], P - 1, None, ALU.bitwise_and))
            v.tensor_copy(lo_b[0:Q, :], lo_i[0:Q, :]).then_inc(lo_ready, 1)
            c.link(v.tensor_tensor(keep[0:Q, :], dst_f[0:Q, 0:RL + 1], dst_f[0:Q, 1:RL + 2],
                                   ALU.is_equal))
            v.tensor_scalar(reset[0:Q, :], keep[0:Q, :], 1.0, BIG, ALU.subtract, ALU.mult)
            for n, (a, b) in enumerate(((RL, 0), (RL, 0), (1, RL + 1))):
                c.link(v.tensor_tensor(coef[0:Q, n * H:(n + 1) * H],
                                       dst_f[0:Q, a:a + 1].broadcast_to([Q, H]),
                                       dst_f[0:Q, b:b + 1].broadcast_to([Q, H]), ALU.is_equal))
            v.tensor_scalar(coef[0:Q, H:3 * H], coef[0:Q, H:3 * H], 1.0, BIG, ALU.subtract, ALU.mult)\
             .then_inc(coef_ready, 1)
            v.wait_ge(s_const, NCONST)
            v.tensor_scalar(diag[0:Q, :], ident[0:Q, 0:Q], dst_f[0:Q, RL:RL + 1], None, ALU.mult)\
             .then_inc(row_diag, 1)
            v.tensor_scalar(minus_p[:, :], pcol[:, :], -1.0, None, ALU.mult).then_inc(minus_p_set, 1)
            v.wait_ge(w_in, 16 * KF)
            v.wait_ge(a_in, 32)
            for k in range(KF):
                for s in range(2):
                    c.link(v.tensor_tensor(w_tmp[:, s, :], w_ext[:, k, 0:HF], a_bc[:, s, :], ALU.mult))
                c.link(v.tensor_reduce(
                    w_ext[:, k, HF:wide], w_tmp.rearrange("p s (h o) -> p (s h) o", h=H), AX.X, ALU.add))
            v.nop().then_inc(wext_ready, 1)
            v.wait_ge(row_ends, 1)
            c.link(v.tensor_tensor(q_tmp, bank[7][:, 0:Q].unsqueeze(1).broadcast_to([P, NB, Q]),
                                   node_id[:, :].unsqueeze(2).broadcast_to([P, NB, Q]), ALU.is_lt))
            c.link(v.tensor_reduce(qn[:, :], q_tmp, AX.X, ALU.add))
            c.link(v.tensor_scalar(qn[:, :], qn[:, :], float(Q - 1), None, ALU.min))
            v.tensor_copy(qi[:, :], qn[:, :]).then_inc(q_ready, 1)
            v.wait_ge(x_in, 32)
            for b in range(NB):
                last = v.bn_stats(st0[:, b, :], xs0[:, b, :])
            c.link(last)
            c.link(v.tensor_tensor(mean[:, :], st0[:, :, 1], st0[:, :, 4], ALU.add))
            c.link(v.tensor_scalar(mean[:, :], mean[:, :], 0.5, None, ALU.mult))
            c.link(v.tensor_tensor(sm1[:, :], st0[:, :, 1], st0[:, :, 4], ALU.subtract))
            c.link(v.tensor_tensor(sm1[:, :], sm1[:, :], sm1[:, :], ALU.mult))
            c.link(v.tensor_tensor(sm2[:, :], st0[:, :, 2], st0[:, :, 5], ALU.add))
            c.link(v.scalar_tensor_tensor(sm1[:, :], sm1[:, :], F / 4.0, sm2[:, :], ALU.mult, ALU.add))
            v.tensor_scalar(sm1[:, :], sm1[:, :], 1.0 / F, EPS, ALU.mult, ALU.add).then_inc(var_ready, 1)
            v.wait_ge(std_ready, 1)
            c.link(v.reciprocal(rstd[:, :], rstd[:, :]))
            for b in range(NB):
                v.tensor_scalar(xs0[:, b, :], xs0[:, b, :], mean[:, b:b + 1], rstd[:, b:b + 1],
                                ALU.subtract, ALU.mult).then_inc(xn_ready, 1)
            v.wait_ge(edges_A, 4)
            c.link(v.tensor_scalar(hi_i, srcA[:, 0:Q, :].rearrange("p q r -> p (q r)"), 7, None,
                                   ALU.arith_shift_right))
            c.link(v.tensor_copy(hiA[:, :, :].rearrange("p q r -> p (q r)"), hi_i))
            v.wait_ge(tb_done, 1)
            c.link(v.tensor_tensor(enters[:, :], bank[7][:, 1:NB], iota_f[:, 1:NB], ALU.add))
            c.link(v.tensor_tensor(path_tmp, enters[:, :].unsqueeze(1).broadcast_to([P, G, NB - 1]),
                                   iota_g[:, :].unsqueeze(2).broadcast_to([P, G, NB - 1]), ALU.is_le))
            c.link(v.tensor_reduce(beta_f[:, :], path_tmp, AX.X, ALU.add))
            v.tensor_copy(beta_i[:, :], beta_f[0:1, :])
            c.link(v.tensor_tensor(slot_f[:, :], iota_g[0:1, :], beta_f[0:1, :], ALU.subtract))
            v.tensor_copy(tau_i[:, :], slot_f[:, :])
            for n in range(Q // RING - 1, 0, -1):
                c.link(v.tensor_scalar(path_f[:, :], slot_f[:, :], float(n * RING), float(RING * n),
                                       ALU.is_ge, ALU.mult))
                c.link(v.tensor_tensor(slot_f[:, :], slot_f[:, :], path_f[:, :], ALU.subtract))
            c.link(v.tensor_copy(slot_i[:, :], slot_f[:, :]))
            c.link(v.tensor_scalar(beta_f[:, :], beta_f[:, :], float(P), None, ALU.mult))
            for b in range(NB):
                v.wait_ge(rows_got[b % ROWBUF], 16 * (b // ROWBUF + 1))
                v.tensor_scalar(drow[:, b % ROWBUF, :], drow[:, b % ROWBUF, :], node_id[:, b:b + 1], None,
                                ALU.is_lt, ALU.add, accum_out=start[:, b:b + 1]).then_inc(rows_used, 1)
            c.link(v.memset(start[:, NB:NB + 1], float(E)))
            c.link(v.scalar_tensor_tensor(start[:, 0:NB], qn[:, :], float(RL), start[:, 0:NB],
                                          ALU.mult, ALU.add))
            v.nop().then_inc(start_ready, 1)
            v.wait_ge(next_done, 1)
            c.link(v.tensor_tensor(sm1[:, :], bank[7][:, 0:NB], start[:, 0:NB], ALU.is_equal))
            c.link(v.scalar_tensor_tensor(sm2[:, :], node_id[:, :], float(E), start[:, 0:NB],
                                          ALU.add, ALU.subtract))
            c.link(v.tensor_tensor(sm1[:, :], sm1[:, :], sm2[:, :], ALU.mult))
            v.tensor_tensor(spos[:, :], sm1[:, :], start[:, 0:NB], ALU.add).then_inc(spos_ready, 1)

            v.wait_ge(coefT_done, 1)
            v.tensor_copy(coef_row[:, :, :], bank[7][0:H, 0:3 * Q].rearrange("h (n q) -> h n q", n=3))\
             .then_inc(early_over, 1)
            v.wait_ge(e_copied, NB // 2)
            es = e_node[:, :, 0:H].rearrange("p b h -> p h b")
            res = t_res[:, :, :]
            c.link(v.tensor_copy(t3[:, 0, :, :], es))
            c.link(v.tensor_tensor(res, es, t3[:, 0, :, :], ALU.subtract))
            c.link(v.tensor_copy(t3[:, 1, :, :], res))
            c.link(v.tensor_tensor(res, res, t3[:, 1, :, :], ALU.subtract))
            v.tensor_copy(t3[:, 2, :, :], res).then_inc(t3_ready, 1)

            def lo_onehot(i, u):
                if u not in ACT_ROWS:
                    v.wait_ge(lo_in[u], 16 * (i + 1))
                    v.tensor_scalar(lo_oh[:, u, :], lo_bc[:, u, :], pcol[:, 0:1], None, ALU.is_equal)\
                     .then_inc(lo_oh_ready[u], 1)

            def hi_onehot(q, u):
                v.tensor_tensor(
                    hi_oh[:, u, :, :],
                    hiA[:, bass.ds(q, 1), :].rearrange("p q r -> p (q r)").unsqueeze(2)
                    .broadcast_to([P, TPR, NB]),
                    iota_f[:, 0:NB].unsqueeze(1).broadcast_to([P, TPR, NB]), ALU.is_equal)\
                 .then_inc(hi_oh_ready, 1)

            def pick(i, u, more=True):
                q = i * OHS + u
                v.wait_ge(hi_oh_ready, q + 1)
                v.wait_ge(es_done, q + 1)
                v.tensor_tensor(
                    es_sel[:, u, :].rearrange("p (r h b) -> p r h b", r=TPR, h=H),
                    bank[u][:, 0:TPR * H * NB].rearrange("p (r h b) -> p r h b", r=TPR, h=H),
                    hi_oh[:, u, :, :].unsqueeze(2).broadcast_to([P, TPR, H, NB]), ALU.mult)\
                 .then_inc(es_selected, 1)
                if more:
                    lo_onehot(i + 1, u)
                v.wait_ge(es_selected, q + 1)
                v.tensor_reduce(exA[:, bass.ds(q, 1), :, :].rearrange("p q r h -> p (q r h)"),
                                es_sel[:, u, :].rearrange("p (a b) -> p a b", b=NB), AX.X, ALU.add)\
                 .then_inc(es_picked, 1)
                if more:
                    hi_onehot(q + OHS, u)

            for u in range(OHS):
                lo_onehot(0, u)
                hi_onehot(u, u)
            with v.Fori(0, Q // OHS - 1, 1) as i:
                for u in range(OHS):
                    pick(i, u)
            for u in range(OHS):
                pick(Q // OHS - 1, u, more=False)
            v.wait_ge(es_picked, Q)

            keep0, reset0 = keep[0:Q, 0:RL], reset[0:Q, 0:RL]
            reset1 = reset[0:Q, 1:RL + 1][:, ::-1]

            def across_rows(n, fill, op0, op1, back=False):
                v.nop().then_inc(tails_ready, 1)
                v.wait_ge(tailsT_done, n + 1)
                if back:
                    c.link(v.memset(carry_row[:, Q:Q + 1], fill))
                    v.tensor_tensor_scan(carry_row[:, 0:Q][:, ::-1], coef_row[:, n, :][:, ::-1],
                                         bank[7][0:H, 0:Q][:, ::-1], fill, op0, op1)\
                     .then_inc(rows_scanned, 1)
                else:
                    c.link(v.memset(carry_row[:, 0:1], fill))
                    v.tensor_tensor_scan(carry_row[:, 1:Q + 1], coef_row[:, n, :], bank[7][0:H, 0:Q],
                                         fill, op0, op1).then_inc(rows_scanned, 1)
                v.wait_ge(carry_done, n + 1)
                c.link(v.tensor_copy(carry[0:Q, :], bank[7][0:Q, 256:256 + H]))

            v.wait_ge(ed_in, 16)
            for h in range(H):
                c.link(v.tensor_tensor_scan(mxB[0:Q, h, :], keep0, edB[0:Q, :, h], 0.0,
                                            ALU.mult, ALU.add))
            across_rows(0, 0.0, ALU.mult, ALU.add)
            for h in range(H):
                c.link(v.tensor_tensor_scan(edB[0:Q, :, h], keep0, edB[0:Q, :, h], carry[0:Q, h:h + 1],
                                            ALU.mult, ALU.add))
            v.wait_ge(esB_copied, TPR)
            for h in range(H):
                c.link(v.tensor_tensor_scan(mxB[0:Q, h, :], reset0, esB[0:Q, h, :], -BIG,
                                            ALU.add, ALU.max))
            across_rows(1, -BIG, ALU.add, ALU.max)
            for h in range(H):
                c.link(v.tensor_tensor_scan(mxB[0:Q, h, :], reset0, esB[0:Q, h, :], carry[0:Q, h:h + 1],
                                            ALU.add, ALU.max))
            for h in range(H):
                c.link(v.tensor_tensor_scan(bwdB[0:Q, h, :][:, ::-1], reset1, mxB[0:Q, h, :][:, ::-1],
                                            -BIG, ALU.add, ALU.max))
            across_rows(2, -BIG, ALU.add, ALU.max, back=True)
            for h in range(H):
                c.link(v.tensor_tensor_scan(mxB[0:Q, h, :][:, ::-1], reset1, mxB[0:Q, h, :][:, ::-1],
                                            carry[0:Q, h:h + 1], ALU.add, ALU.max))
            ed_hj = edB[0:Q, :, :].rearrange("q j h -> q h j")
            for t in (esB, mxB):
                c.link(v.tensor_tensor(t[0:Q, :, :], t[0:Q, :, :], ed_hj, ALU.add))
                c.link(v.scalar_tensor_tensor(t[0:Q, :, :], t[0:Q, :, :], 0.2, t[0:Q, :, :],
                                              ALU.mult, ALU.max))
            v.tensor_tensor(esB[0:Q, :, :], esB[0:Q, :, :], mxB[0:Q, :, :], ALU.subtract)\
             .then_inc(score_ready, 1)

            def scale_row(trip, u):
                t = trip * OHS + u
                s = v.value_load(ring_slot[0:1, bass.ds(t, 1)], min_val=0, max_val=RING - 1)
                v.wait_ge(gathered[u], 16 * TPR * (trip + 1))
                msg = ring[:, bass.ds(s, 1), :, 0:HF].rearrange("p s r (h o) -> p (s r) h o", h=H)
                ex = exA[:, bass.ds(t, 1), :, :].rearrange("p q r h -> p (q r) h")
                v.tensor_tensor(msg, msg, ex.unsqueeze(3).broadcast_to([P, TPR, H, FO]), ALU.mult)
                v.tensor_copy(ring[:, bass.ds(s, 1), :, HF:MW].rearrange("p s r h -> p (s r) h"), ex)

            def dst_onehot(trip, u):
                t = trip * OHS + u
                tau = v.value_load(tau_i[0:1, bass.ds(t, 1)], min_val=0, max_val=Q - 1)
                v.scalar_tensor_tensor(
                    dst_oh[:, u, :, :], iota_f[:, :].unsqueeze(1).broadcast_to([P, TPR, P]),
                    beta_f[:, bass.ds(t, 1)],
                    dstA[:, bass.ds(tau, 1), :].rearrange("p q r -> p (q r)").unsqueeze(2)
                    .broadcast_to([P, TPR, P]), ALU.add, ALU.is_equal).then_inc(dst_oh_ready, 1)

            def flush(trip, u):
                i = trip * OHS + u
                blk = v.value_load(beta_i[0:1, bass.ds(i, 1)], min_val=0, max_val=NB - 1)
                v.wait_ge(group_done, i + 1)
                a = acc[:, bass.ds(blk, 1), :].rearrange("p b w -> p (b w)")
                v.tensor_tensor(a, a, bank[u][:, 0:MW], ALU.add).then_inc(flushed, 1)
                v.wait_ge(flushed, i + 1)

            v.wait_ge(exA_copied, TPR)
            v.wait_ge(acc_zeroed, 1)
            for u in range(OHS):
                scale_row(0, u)
                dst_onehot(0, u)
            with v.Fori(0, Q // OHS - 1, 1) as i:
                for u in range(OHS):
                    flush(i, u)
                    scale_row(i + 1, u)
                    dst_onehot(i + 1, u)
            full_rows, full_steps = Q // OHS, G // OHS
            with v.Fori(full_rows - 1, full_steps - 1, 1) as i:
                for u in range(OHS):
                    flush(i, u)
                    dst_onehot(i + 1, u)
            for i in range((full_steps - 1) * OHS, G):
                flush(i // OHS, i % OHS)
                if i + OHS < G:
                    dst_onehot(i // OHS + 1, i % OHS)


            v.wait_ge(group_done, G)
            v.memset(x_again[:, NB - 1, :], 0.0).then_inc(x_pad_set, 1)
            c.link(v.tensor_scalar(rden, acc[:, :, HF:MW], 1e-9, None, ALU.max))
            c.link(v.reciprocal(rden, rden))
            x1_h = acc[:, :, 0:HF].rearrange("p b (h o) -> p b h o", h=H)
            x1 = acc[:, :, 0:HF]
            c.link(v.tensor_tensor(x1_h, x1_h, rden.unsqueeze(3).broadcast_to([P, NB, H, FO]), ALU.mult))
            v.wait_ge(x_again_in, 32)
            v.scalar_tensor_tensor(x1, x1, 0.0, x_again, ALU.max, ALU.add).then_inc(x1_made, 1)
            v.wait_ge(x1_made, 1)

            def moments(source, n):
                with v.Fori(0, NB, 1) as b:
                    c.enter(b, 1)
                    c.link(v.bn_stats(st1[:, bass.ds(b, 1), :].rearrange("p b s -> p (b s)"),
                                      source[:, bass.ds(b, 1), :].rearrange("p b f -> p (b f)")))
                c.leave(NB)
                c.link(v.tensor_tensor(mean1, st1[:, :, 1], st1[:, :, 4], ALU.add))
                c.link(v.tensor_scalar(mean1, mean1, 0.5, None, ALU.mult))
                c.link(v.tensor_tensor(tmp1, st1[:, :, 1], st1[:, :, 4], ALU.subtract))
                c.link(v.tensor_tensor(tmp1, tmp1, tmp1, ALU.mult))
                c.link(v.tensor_tensor(tmp2, st1[:, :, 2], st1[:, :, 5], ALU.add))
                c.link(v.scalar_tensor_tensor(tmp1, tmp1, F / 4.0, tmp2, ALU.mult, ALU.add))
                v.tensor_scalar(tmp1, tmp1, 1.0 / F, EPS, ALU.mult, ALU.add).then_inc(var_ready, 1)
                v.wait_ge(std_ready, n + 2)
                c.link(v.reciprocal(rstd1, rstd1))

            def block_of(t, b):
                return t[:, bass.ds(b, 1), :].rearrange("p b f -> p (b f)")

            moments(x1, 0)
            with v.Fori(0, NB, 1) as b:
                c.enter(b, 1)
                c.link(v.tensor_scalar(block_of(xn1, b), block_of(x1, b), mean1[:, bass.ds(b, 1)],
                                       rstd1[:, bass.ds(b, 1)], ALU.subtract, ALU.mult))
            c.leave(NB)
            moments(xn1, 1)
            v.wait_ge(consts_in, 16 * 6)

            def second_norm(b, u):
                row = block_of(xn1, b)
                c.link(v.tensor_scalar(row, row, mean1[:, bass.ds(b, 1)], rstd1[:, bass.ds(b, 1)],
                                       ALU.subtract, ALU.mult))
                c.link(v.tensor_tensor(row, row, gamma_bc, ALU.mult))
                v.tensor_tensor(xn_u[:, u, :], row, beta_bc, ALU.add).then_inc(xn1_ready, 1)

            for b in range(2):
                second_norm(b, b)
            with v.Fori(1, NB // 2, 1) as i:
                c.enter(i - 1, 4)
                for u in range(2):
                    v.wait_ge(xT1_done, 2 * i + u - 1)
                    v.wait_ge(xn1_kept, 2 * i + u - 1)
                    second_norm(2 * i + u, u)
            c.leave(NB // 2 - 1)
            c.link(v.tensor_scalar(upper, iota_f[:, :], pcol[:, 0:1], None, ALU.is_gt))
            c.link(v.tensor_scalar(tmp2, iota_f[:, 0:NB], float(P), pcol[:, 0:1], ALU.mult, ALU.add))
            c.link(v.tensor_scalar(valid, tmp2, float(N), None, ALU.is_lt))
            c.link(v.tensor_scalar(e_less, iota_f[:, 0:NE], float(NE), None, ALU.subtract))
            c.link(v.tensor_scalar(gran, iota_f[:, 0:EG], float(BS), None, ALU.mult))
            c.link(v.memset(carry_on, 1.0))
            c.link(v.memset(carry_on[:, :, 0], 0.0))
            v.wait_ge(b1_T_done, 1)
            v.tensor_copy(b1_T, bank[7][:, 0:NE * FC]).then_inc(b1_T_ready, 1)

            def each_b(t):
                return t.unsqueeze(1).broadcast_to([P, NB, NE])

            def each_e(t):
                return t.unsqueeze(2).broadcast_to([P, NB, NE])

            v.wait_ge(logits_done, NB)
            c.link(v.tensor_tensor(lg, bank[2][:, 0:NB * NE].rearrange("p (b e) -> p b e", e=NE),
                                   each_b(br_bc), ALU.add))
            for top, oh in ((top1, oh_a), (top2, oh_b)):
                c.link(v.tensor_reduce(top, lg, AX.X, ALU.max))
                c.link(v.tensor_tensor(eq, lg, each_e(top), ALU.is_equal))
                c.link(v.tensor_tensor(eq, eq, each_b(e_less), ALU.mult))
                c.link(v.tensor_reduce(tmp2, eq, AX.X, ALU.min))
                c.link(v.tensor_tensor(oh, each_b(e_less), each_e(tmp2), ALU.is_equal))
                if oh is oh_a:
                    c.link(v.scalar_tensor_tensor(lg, oh, -BIG, lg, ALU.mult, ALU.add))
            v.tensor_tensor(tmp1, top2, top1, ALU.subtract).then_inc(gap_ready, 1)
            c.link(v.tensor_tensor(mask, oh_a, oh_b, ALU.add))
            v.tensor_tensor(mask, mask, each_e(valid), ALU.mult).then_inc(mask_ready, 1)
            v.wait_ge(gap_exp, 1)
            c.link(v.tensor_scalar(w_a, w_b, 1.0, None, ALU.add))
            c.link(v.reciprocal(w_a, w_a))
            c.link(v.tensor_tensor(w_b, w_b, w_a, ALU.mult))
            v.wait_ge(ranks_done, 1)
            c.link(v.tensor_copy(tot, bank[4][:, 0:NB * NE].rearrange("p (b e) -> p b e", e=NE)))
            c.link(v.tensor_copy(rank, bank[3][:, 0:NB * NE].rearrange("p (b e) -> p b e", e=NE)))
            tot_eb = eq.rearrange("p b e -> p (b e)")
            c.link(v.tensor_copy(tot_eb.rearrange("p (e b) -> p e b", e=NE),
                                 tot.rearrange("p b e -> p e b")))
            c.link(v.tensor_tensor_scan(incl.rearrange("p e b -> p (e b)"),
                                        carry_on.rearrange("p e b -> p (e b)"), tot_eb, 0.0,
                                        ALU.mult, ALU.add))
            c.link(v.tensor_tensor(n_cmp, incl[:, :, NB - 1].unsqueeze(2).broadcast_to([P, NE, EG]),
                                   gran.unsqueeze(1).broadcast_to([P, NE, EG]), ALU.is_gt))
            c.link(v.tensor_reduce(n_blk, n_cmp, AX.X, ALU.add))
            c.link(v.tensor_tensor_scan(n_incl, ones[:, 0:NE], n_blk, 0.0, ALU.mult, ALU.add))
            c.link(v.tensor_tensor(n_excl, n_incl, n_blk, ALU.subtract))
            c.link(v.tensor_tensor(rank, rank, incl.rearrange("p e b -> p b e"), ALU.add))
            c.link(v.tensor_tensor(rank, rank, tot, ALU.subtract))
            c.link(v.scalar_tensor_tensor(pos_e, each_b(n_excl), float(BS), rank, ALU.mult, ALU.add))
            for k, oh in enumerate((oh_a, oh_b)):
                c.link(v.tensor_tensor(oh, oh, pos_e, ALU.mult))
                c.link(v.tensor_reduce(tmp2, oh, AX.X, ALU.add))
                c.link(v.tensor_copy(pos_i[:, k, :], tmp2))
            c.link(v.tensor_tensor(blk_cmp, n_excl[:, 1:NE].unsqueeze(1).broadcast_to([P, NBLK, NE - 1]),
                                   iota_f[:, 0:NBLK].unsqueeze(2).broadcast_to([P, NBLK, NE - 1]),
                                   ALU.is_le))
            c.link(v.tensor_reduce(blk_f, blk_cmp, AX.X, ALU.add))
            v.tensor_copy(blk_e, blk_f[0:1, :]).then_inc(pos_ready, 1)

            def pick_w1(j, u):
                e = v.value_load(blk_e[0:1, bass.ds(j, 1)], min_val=0, max_val=NE - 1)
                v.tensor_copy(w1_now[:, u, :, :].rearrange("p k h -> p (k h)"),
                              w1_all[:, bass.ds(e, 1), :].rearrange("p e w -> p (e w)"))\
                 .then_inc(w1_picked, 1)

            def turned_copy(j, u):
                v.wait_ge(xsT_done, j + 1)
                v.tensor_copy(xsT[:, u, :, :].rearrange("p k n -> p (k n)"), bank[u][:, :])\
                 .then_inc(xsT_copied, 1)

            def add_b2(j, u, n, first=False):
                e = v.value_load(blk_e[0:1, bass.ds(j, 1)], min_val=0, max_val=NE - 1)
                v.wait_ge(l2_done, j + 1)
                if not first:
                    v.wait_ge(y_stored[u], 16 * n)
                v.tensor_tensor(y_out[:, u, :, :], bank[6 + u][:, :].rearrange("p (m f) -> p m f", m=BM),
                                b2_bc[:, bass.ds(e, 1), :].broadcast_to([P, BM, F]), ALU.add)\
                 .then_inc(y_ready, 1)

            v.wait_ge(pos_ready, 1)
            v.wait_ge(w1_in, 16 * NE)
            pick_w1(0, 0)
            pick_w1(1, 1)
            turned_copy(0, 0)
            turned_copy(1, 1)
            v.wait_ge(l1_done, FC // 2)
            pick_w1(2, 0)
            turned_copy(2, 0)
            add_b2(0, 0, 0, first=True)
            v.wait_ge(l1_done, FC // 2 * 2)
            pick_w1(3, 1)
            turned_copy(3, 1)
            add_b2(1, 1, 0, first=True)
            with v.Fori(1, (NBLK - 2) // 2, 1) as i:
                v.wait_ge(l1_done, FC // 2 * (2 * i + 1))
                pick_w1(2 * i + 2, 0)
                turned_copy(2 * i + 2, 0)
                add_b2(2 * i, 0, i)
                v.wait_ge(l1_done, FC // 2 * (2 * i + 2))
                pick_w1(2 * i + 3, 1)
                turned_copy(2 * i + 3, 1)
                add_b2(2 * i + 1, 1, i)
            for j in range(2 * ((NBLK - 2) // 2), NBLK):
                if j + 2 < NBLK:
                    v.wait_ge(l1_done, FC // 2 * (j + 1))
                    pick_w1(j + 2, j % 2)
                    turned_copy(j + 2, j % 2)
                add_b2(j, j % 2, j // 2)
            def combine(b, u, n):
                row = block_of(x1, b)
                v.wait_ge(y_got[u], 16 * TOP * (n + 1))
                c.link(v.scalar_tensor_tensor(row, y_in[:, u, 0, :], w_a[:, bass.ds(b, 1)], row,
                                              ALU.mult, ALU.add))
                v.scalar_tensor_tensor(row, y_in[:, u, 1, :], w_b[:, bass.ds(b, 1)], row,
                                       ALU.mult, ALU.add).then_inc(combined, 1)

            with v.Fori(0, NB // YS, 1) as i:
                c.enter(i, YS)
                for u in range(YS):
                    combine(i * YS + u, u, i)
            c.leave(NB // YS)


_INS = ["x", "src", "dst", "L0_gnn_W", "L0_gnn_a_src", "L0_gnn_a_dst", "L0_ffn_gamma", "L0_ffn_beta",
        "L0_ffn_Wr", "L0_ffn_br", "L0_ffn_W1", "L0_ffn_b1", "L0_ffn_W2", "L0_ffn_b2"]


def kernel(**inputs):
    import numpy as _np
    import concourse.bacc as _bacc
    from concourse import mybir as _mybir
    from concourse.bass_utils import run_bass_kernel_spmd as _run

    nc = _bacc.Bacc("TRN2", target_bir_lowering=False, num_devices=1)
    arrays, args = {}, []
    for name in _INS:
        a = _np.ascontiguousarray(inputs[name])
        arrays[f"in_{name}"] = a
        args.append(nc.dram_tensor(f"in_{name}", a.shape, _mybir.dt.from_np(a.dtype), kind="ExternalInput").ap())
    x = inputs["x"]
    args.append(nc.dram_tensor("out", x.shape, _mybir.dt.from_np(_np.dtype("float32")), kind="ExternalOutput").ap())
    gat_moe_kernel(nc, *args)
    r = _run(nc, [arrays], core_ids=[0])
    return r.results[0]["out"]
```

```python
import concourse.bass as bass
from concourse import mybir
from contextlib import ExitStack


class Chain:

    def __init__(self, eng, sem):
        self.eng, self.sem, self.done, self.trip, self.per_trip, self.base = eng, sem, 0, 0, 0, 0

    def link(self, ins):
        self.done += 1
        ins.then_inc(self.sem, 1)
        self.eng.wait_ge(self.sem, self.done + self.trip * self.per_trip)

    def enter(self, trip, per_trip):
        self.trip, self.per_trip, self.base = trip, per_trip, self.done

    def leave(self, trips):
        assert self.done - self.base == self.per_trip, (self.done - self.base, self.per_trip)
        self.done = self.base + trips * self.per_trip
        self.trip, self.per_trip = 0, 0


def gat_moe_kernel(nc, x, src, dst, gnn_w, a_src, a_dst, gamma, beta, wr, br, w1, b1, w2, b2, out):
    fp32, bf16, i32 = mybir.dt.float32, mybir.dt.bfloat16, mybir.dt.int32
    ALU = mybir.AluOpType
    ACT = mybir.ActivationFunctionType
    AX = mybir.AxisListType
    P = 128

    N, F = x.shape
    H, _, FO = gnn_w.shape
    HF = H * FO
    KF = F // P
    E = src.shape[0]
    TPR = 5
    RL = TPR * P
    Q = E // RL
    assert Q * RL == E and Q <= P
    NB = (N + P - 1) // P
    LASTB = N - (NB - 1) * P
    G = Q + NB - 1
    RING = 25
    LEFT = 2 * RING
    assert Q % RING == 0 and RING >= NB + TPR
    MW = HF + H
    NE, _, HID = w1.shape
    FC = HID // P
    BS = 256
    BM = BS // P
    TOP = 2
    NBLK = (TOP * N + NE * (BS - 1)) // BS
    EG = (N + BS - 1) // BS
    BIG = 1e38
    EPS = 1e-5

    h_tab = nc.dram_tensor("h_tab", (NB * P, HF), fp32).ap()
    lo_tab = nc.dram_tensor("lo_tab", (Q, RL), bf16).ap()
    dst_tab = nc.dram_tensor("dst_tab", (Q, RL), fp32).ap()
    ed_tab = nc.dram_tensor("ed_tab", (E + NB * P, H), fp32).ap()
    xs_tab = nc.dram_tensor("xs_tab", (NBLK * BS, F), fp32).ap()
    ys_tab = nc.dram_tensor("ys_tab", (NBLK * BS, F), fp32).ap()
    ed_rows = ed_tab[0:E, :].rearrange("(q j) h -> q (j h)", q=Q)
    src_rows = src.rearrange("(q j) -> q j", q=Q)
    dst_rows = dst.rearrange("(q j) -> q j", q=Q)

    ctx = ExitStack()
    with ctx:
        def sb(name, shape, dt=fp32):
            return ctx.enter_context(nc.sbuf_tensor(name, shape, dt))

        def sem(name):
            return ctx.enter_context(nc.semaphore(name))

        psum = ctx.enter_context(nc.psum_tensor("psum", [P, 8, 512], fp32))
        bank = [psum[:, i, :] for i in range(8)]

        ring = sb("ring", [P, RING, TPR, MW])
        ring_flat = ring[:, :, :, :].rearrange("p s r w -> p (s r w)")
        used = [0]

        def early(width, dt=fp32):
            a = ring_flat[:, used[0]:used[0] + width]
            used[0] += width
            return a if dt == fp32 else a.bitcast(dt)

        xs0 = early(NB * F).rearrange("p (b f) -> p b f", b=NB)
        xT0 = early(4 * F).rearrange("p (u b k n) -> p u b k n", u=2, b=2, k=KF)
        h_stage = early(4 * HF).rearrange("p (u b f) -> p u b f", u=2, b=2)
        wide = HF + 2 * H
        w_ext = early(KF * wide).rearrange("p (k w) -> p k w", k=KF)
        a_bc = early(2 * HF).rearrange("p (s f) -> p s f", s=2)
        w_tmp = early(2 * HF).rearrange("p (s f) -> p s f", s=2)
        q_tmp = early(NB * Q).rearrange("p (b q) -> p b q", b=NB)
        path_tmp = early(G * (NB - 1)).rearrange("p (g b) -> p g b", b=NB - 1)
        src_f = early(RL)
        lo_i = early(RL, i32)
        lo_b = early(RL // 2, bf16)
        hi_i = early(Q * TPR, i32)
        diag = early(Q)
        src_i = early(RL, i32)
        dst_i = early(RL + 2, i32)
        zeros = early(RL * H)
        ROWBUF = 12
        drow = early(ROWBUF * RL).rearrange("p (u j) -> p u j", u=ROWBUF)
        dst_f = early(RL + 2)
        shift = early(P)
        corner = early(P)
        st0 = early(NB * 6).rearrange("p (b s) -> p b s", s=6)
        mean, rstd, sm1, sm2, qn, node_id = (early(NB) for _ in range(6))
        qi = early(NB, i32)
        start = early(NB + 1)
        coef = early(3 * H)
        enters, first_row = early(NB - 1), early(NB - 1)
        left_tmp = early(LEFT * (NB - 1)).rearrange("p (s b) -> p s b", b=NB - 1)
        left_f = early(LEFT)
        iota_g = early(G)
        slot_f, path_f = early(G)[0:1, :], early(G)[0:1, :]
        assert used[0] <= RING * TPR * MW, used

        keep = sb("keep", [P, RL + 1])
        reset = sb("reset", [P, RL + 1])
        srcA = sb("srcA", [P, Q + 1, TPR], i32)
        dstA = sb("dstA", [P, Q, TPR])
        hiA = sb("hiA", [P, Q, TPR], bf16)
        exA_flat = sb("exA_flat", [P, H * RL])
        exA = exA_flat[:, 0:Q * TPR * H].rearrange("p (q r h) -> p q r h", q=Q, r=TPR)
        scoreB = exA_flat[:, :].rearrange("p (h j) -> p h j", h=H)
        esB = sb("esB", [P, H, RL])
        edB = sb("edB", [P, RL, H])
        OHS = 5
        shared = sb("shared", [P, OHS * RL])
        half = OHS * RL // 2
        bwdB = shared[:, 0:H * RL].rearrange("p (h j) -> p h j", h=H)
        dst_oh = shared[:, :].rearrange("p (u r d) -> p u r d", u=OHS, r=TPR)
        acc = sb("acc", [P, NB, MW])
        acc_flat = acc[:, :, :].rearrange("p b w -> p (b w)")
        mxB = acc_flat[:, 0:H * RL].rearrange("p (h j) -> p h j", h=H)
        after = H * RL + TPR * H * NB
        coef_row = acc_flat[0:H, after:after + 3 * Q].rearrange("h (n q) -> h n q", n=3)
        carry_row = acc_flat[0:H, after + 3 * Q:after + 4 * Q + 1]
        carry = acc_flat[:, after + 4 * Q + 1:after + 4 * Q + 1 + H]
        half = OHS * RL // 2
        lo_bc = shared[:, 0:half].bitcast(bf16).rearrange("p (u j) -> p u j", u=OHS)
        lo_oh = shared[:, half:2 * half].bitcast(bf16).rearrange("p (u j) -> p u j", u=OHS)
        es_w, hi_w = TPR * H * NB, TPR * NB // 2
        es_sel = acc_flat[:, 0:OHS * es_w].rearrange("p (u w) -> p u w", u=OHS)
        hi_oh = acc_flat[:, OHS * es_w:OHS * (es_w + hi_w)].bitcast(bf16)\
            .rearrange("p (u r b) -> p u r b", u=OHS, r=TPR)
        ACT_ROWS = (0, 1, 3, 4)
        behind = after + 4 * Q + 1 + H
        off = acc_flat[:, behind:behind + len(ACT_ROWS) * RL // 2].bitcast(bf16)\
            .rearrange("p (u j) -> p u j", j=RL)
        assert OHS * (es_w + hi_w) <= after and behind + len(ACT_ROWS) * RL // 2 <= NB * MW

        ident = sb("ident", [P, P])
        ones = sb("ones", [P, P])
        iota_f = sb("iota_f", [P, P])
        pcol = sb("pcol", [P, 1])
        minus_p = sb("minus_p", [P, 1])
        spos = sb("spos", [P, NB], i32)
        e_node = sb("e_node", [P, NB, 2 * H])
        t3 = sb("t3", [P, 3, H, NB], bf16)
        beta_f = sb("beta_f", [P, G])
        t_res = sb("t_res", [P, H, NB])
        beta_i = sb("beta_i", [1, G], i32)
        tau_i = sb("tau_i", [1, G], i32)
        slot_i = sb("slot_i", [1, G], i32)
        left_i = sb("left_i", [1, LEFT], i32)
        ring_slot = sb("ring_slot", [1, Q], i32)
        picks = sb("picks", [P, RING, TPR], i32)

        edB_flat = edB[:, :, :].rearrange("p j h -> p (j h)")
        gamma_bc, beta_bc = edB_flat[:, 0:F], edB_flat[:, F:2 * F]
        wr_sb = edB_flat[:, 2 * F:2 * F + KF * NE].rearrange("p (k e) -> p k e", k=KF)
        at = 2 * F + KF * NE
        br_bc = edB_flat[:, at:at + NE]
        b1_rows = edB_flat[0:NE * FC, at + NE:at + NE + P]
        b1_T = edB_flat[:, at + NE + P:at + NE + P + NE * FC]
        at += NE + P + NE * FC
        zero_width = NBLK * BS * F // P // 9
        zero_src = edB_flat[:, 2 * F * KF:2 * F * KF + zero_width]
        assert zero_width * 9 * P == NBLK * BS * F and at <= 2 * F * KF
        assert 2 * F * KF + zero_width <= RL * H
        b2_bc = esB[:, :, :].rearrange("p h j -> p (h j)")[:, 0:NE * F].rearrange("p (e f) -> p e f", e=NE)
        used[0] = 0
        late = early
        xn1 = late(NB * F).rearrange("p (b f) -> p b f", b=NB)
        st1 = late(NB * 6).rearrange("p (b s) -> p b s", s=6)
        mean1, rstd1, shift1, tmp1, tmp2, top1, top2, w_a, w_b, valid = (late(NB) for _ in range(10))
        rden = late(NB * H).rearrange("p (b h) -> p b h", h=H)
        xT1 = late(4 * F).rearrange("p (u b k n) -> p u b k n", u=2, b=2, k=KF)
        upper = late(P)
        lg, eq, oh_a, oh_b, mask, pos_e, rank, tot = (
            late(NB * NE).rearrange("p (b e) -> p b e", e=NE) for _ in range(8))
        incl = late(NE * NB).rearrange("p (e b) -> p e b", e=NE)
        carry_on = late(NE * NB).rearrange("p (e b) -> p e b", e=NE)
        e_less = late(NE)
        gran = late(EG)
        n_blk, n_incl, n_excl = late(NE), late(NE), late(NE)
        n_cmp = late(NE * EG).rearrange("p (e g) -> p e g", e=NE)
        blk_cmp = late(NBLK * (NE - 1)).rearrange("p (j e) -> p j e", j=NBLK)
        blk_f = late(NBLK)
        blk_e = late(NBLK, i32)[0:1, :]
        pos_i = late(TOP * NB, i32).rearrange("p (k b) -> p k b", k=TOP)
        w1_all = late(NE * KF * HID).rearrange("p (e w) -> p e w", e=NE)
        w2_flat = late(NE * FC * F)
        w2_all = w2_flat.rearrange("p (e c f) -> p e c f", e=NE, c=FC)
        W2_FIRST = (NE * FC * F - NB * F) // (FC * F)
        x_again = w2_flat[:, NE * FC * F - NB * F:].rearrange("p (b f) -> p b f", b=NB)
        w1_now = late(2 * KF * HID).rearrange("p (u k h) -> p u k h", u=2, k=KF)
        xs_in = late(2 * BM * F).rearrange("p (u m f) -> p u m f", u=2, m=BM)
        xsT = late(2 * KF * BS).rearrange("p (u k n) -> p u k n", u=2, k=KF)
        hT = exA_flat[:, 0:2 * FC * BS]\
            .rearrange("p (u c n) -> p u c n", u=2, c=FC)
        y_out = shared[:, 0:2 * BM * F].rearrange("p (u m f) -> p u m f", u=2, m=BM)
        YS = 4
        y_in = shared[:, 2 * BM * F:(2 * BM + YS * TOP) * F]\
            .rearrange("p (u k f) -> p u k f", u=YS, k=TOP)
        assert used[0] <= RING * TPR * MW, used

        s_const = sem("s_const")
        s_pool = sem("s_pool")
        left_ready = sem("left_ready")
        e_copied, t3_ready = sem("e_copied"), sem("t3_ready")
        s_dve = sem("s_dve")
        x_in, w_in, a_in, src_in, dst_in = (sem(n) for n in ("x_in", "w_in", "a_in", "src_in", "dst_in"))
        pads_set = sem("pads_set")
        edges_f, edges_T, edges_A = sem("edges_f"), sem("edges_T"), sem("edges_A")
        lo_ready, lo_stored = sem("lo_ready"), sem("lo_stored")
        dst_stored = sem("dst_stored")
        row_diag, row_ends, q_ready = sem("row_diag"), sem("row_ends"), sem("q_ready")
        rows_got = [sem(f"rows_got{u}") for u in range(ROWBUF)]
        rows_used = sem("rows_used")
        var_ready, std_ready = sem("var_ready"), sem("std_ready")
        wext_ready = sem("wext_ready")
        xn_ready, xT_done, xT_copied, h_done, h_copied = (
            sem(n) for n in ("xn_ready", "xT_done", "xT_copied", "h_done", "h_copied"))
        h_stored = [sem(f"h_stored{u}") for u in range(2)]
        start_ready, next_done, spos_ready = sem("start_ready"), sem("next_done"), sem("spos_ready")
        zeros_set, ed_zeroed, ed_put, ed_in = (
            sem(n) for n in ("zeros_set", "ed_zeroed", "ed_put", "ed_in"))
        lo_in = [sem(f"lo_in{u}") for u in range(OHS)]
        lo_oh_ready = [sem(f"lo_oh_ready{u}") for u in range(OHS)]
        off_ready, minus_p_set = sem("off_ready"), sem("minus_p_set")
        es_done, es_selected, es_picked, hi_oh_ready = (
            sem(n) for n in ("es_done", "es_selected", "es_picked", "hi_oh_ready"))
        esT_done, esB_copied = sem("esT_done"), sem("esB_copied")
        coef_ready, coefT_done, tb_done = sem("coef_ready"), sem("coefT_done"), sem("tb_done")
        tails_ready, tailsT_done, rows_scanned, carry_done = (
            sem(n) for n in ("tails_ready", "tailsT_done", "rows_scanned", "carry_done"))
        ed_full, z_made = sem("ed_full"), sem("z_made")
        score_ready, ex_ready, exT_done, exA_copied = (
            sem(n) for n in ("score_ready", "ex_ready", "exT_done", "exA_copied"))
        early_over, acc_zeroed = sem("early_over"), sem("acc_zeroed")
        picks_set = sem("picks_set")
        gathered = [sem(f"gathered{u}") for u in range(OHS)]
        dst_oh_ready, group_done, flushed = sem("dst_oh_ready"), sem("group_done"), sem("flushed")
        consts_in, b1_T_done, b1_T_ready = sem("consts_in"), sem("b1_T_done"), sem("b1_T_ready")
        zero_ready, xs_zeroed, x_again_in = sem("zero_ready"), sem("xs_zeroed"), sem("x_again_in")
        x_pad_set = sem("x_pad_set")
        norm_ready, normed = sem("norm_ready"), sem("normed")
        NORM_HALF, NORM_SET = NB // 2, 4
        assert NB % 2 == 0 and NB % NORM_SET == 0 and NORM_SET % 2 == 0
        xn1_ready, xT1_done, xT1_copied, logits_done = (
            sem(n) for n in ("xn1_ready", "xT1_done", "xT1_copied", "logits_done"))
        gap_ready, gap_exp, mask_ready, ranks_done, pos_ready = (
            sem(n) for n in ("gap_ready", "gap_exp", "mask_ready", "ranks_done", "pos_ready"))
        xs_put = sem("xs_put")
        x1_made, w1_in, w2_in, w1_picked = (sem(n) for n in ("x1_made", "w1_in", "w2_in", "w1_picked"))
        xs_got = [sem(f"xs_got{u}") for u in range(2)]
        xsT_done, xsT_copied, l1_done, gelu_done, l2_done, y_ready = (
            sem(n) for n in ("xsT_done", "xsT_copied", "l1_done", "gelu_done", "l2_done", "y_ready"))
        y_stored = [sem(f"y_stored{u}") for u in range(2)]
        y_got = [sem(f"y_got{u}") for u in range(YS)]
        combined = sem("combined")
        s_out = sem("s_out")
        block = ctx.enter_context(nc.Block())

        @block.sync
        def _(sp):
            sp.wait_ge(pads_set, 1)
            sp.dma_start(dst_i[0:1, 1:RL + 2], dst[0:RL + 1].rearrange("(a j) -> a j", a=1))\
              .then_inc(dst_in, 16)
            for lo, hi in ((1, 65), (65, Q - 1)):
                sp.dma_start(dst_i[lo:hi, 1:RL + 1], dst_rows[lo:hi, :]).then_inc(dst_in, 16)
            sp.dma_start(dst_i[Q - 1:Q, 0:RL + 1],
                         dst[(Q - 1) * RL - 1:E].rearrange("(a j) -> a j", a=1)).then_inc(dst_in, 16)
            prev = dst_rows[0:Q - 2, RL - 1:RL]
            nxt = dst_rows[2:Q, 0:1]
            with nc.allow_non_contiguous_dma(reason="one element a row"):
                sp.dma_start(dst_i[1:Q - 1, 0:1], prev).then_inc(dst_in, 16)
                sp.dma_start(dst_i[1:Q - 1, RL + 1:RL + 2], nxt).then_inc(dst_in, 16)
            sp.dma_start(src_i[0:Q, :], src_rows).then_inc(src_in, 16)
            sp.wait_ge(pads_set, 2)
            full = (NB - 1) * P
            sp.dma_start(xs0[:, 0:NB - 1, :], x[0:full, :].rearrange("(b p) f -> p b f", p=P))\
              .then_inc(x_in, 16)
            sp.dma_start(xs0[0:LASTB, NB - 1, :], x[full:N, :]).then_inc(x_in, 16)
            for k in range(KF):
                sp.dma_start(w_ext[:, k, 0:HF].rearrange("p (h o) -> p h o", h=H),
                             gnn_w[:, k * P:(k + 1) * P, :].rearrange("h f o -> f h o"))\
                  .then_inc(w_in, 16)
            for s, a in enumerate((a_src, a_dst)):
                sp.dma_start(a_bc[:, s, :], a.rearrange("h o -> (h o)").partition_broadcast(P))\
                  .then_inc(a_in, 16)
            sp.wait_ge(edges_f, 1)
            sp.dma_start(dst_tab, dst_f[0:Q, 1:RL + 1]).then_inc(dst_stored, 16)
            sp.wait_ge(lo_ready, 1)
            sp.dma_start(lo_tab, lo_b[0:Q, :]).then_inc(lo_stored, 16)
            sp.wait_ge(zeros_set, 1)
            sp.dma_start(ed_rows, zeros[0:Q, :]).then_inc(ed_zeroed, 16)
            def lo_row(q, u, n=None):
                if n is not None:
                    sp.wait_ge(lo_oh_ready[u], n)
                sp.dma_start(lo_bc[:, u, :],
                             lo_tab[bass.ds(q, 1), :].rearrange("a j -> (a j)").partition_broadcast(P))\
                  .then_inc(lo_in[u], 16)

            sp.wait_ge(lo_stored, 16)
            for u in range(OHS):
                lo_row(u, u)
            for i in range(NB // 2):
                sp.wait_ge(h_copied, i + 1)
                sp.dma_start(h_tab[2 * i * P:(2 * i + 2) * P, :].rearrange("(b p) f -> p b f", p=P),
                             h_stage[:, i % 2, :, :]).then_inc(h_stored[i % 2], 16)
            with sp.Fori(1, Q // OHS, 1) as i:
                for u in range(OHS):
                    lo_row(i * OHS + u, u, i)
            sp.wait_ge(ed_put, 16 * NB)
            sp.dma_start(edB[0:Q, :, :].rearrange("q j h -> q (j h)"), ed_rows).then_inc(ed_in, 16)
            sp.wait_ge(exT_done, TPR)
            for to, frm in ((gamma_bc, gamma.partition_broadcast(P)), (beta_bc, beta.partition_broadcast(P)),
                            (br_bc, br.partition_broadcast(P)),
                            (wr_sb, wr.rearrange("(k p) e -> p k e", p=P)),
                            (b1_rows, b1.rearrange("e (c p) -> (e c) p", p=P)),
                            (b2_bc.rearrange("p e f -> p (e f)"),
                             b2.rearrange("e f -> (e f)").partition_broadcast(P))):
                sp.dma_start(to, frm).then_inc(consts_in, 16)
            sp.wait_ge(zero_ready, 1)
            xs_flat = xs_tab.rearrange("(p a) f -> p (a f)", p=P)
            for n in range(9):
                sp.dma_start(xs_flat[:, n * zero_width:(n + 1) * zero_width], zero_src)\
                  .then_inc(xs_zeroed, 16)
            sp.wait_ge(group_done, G)
            sp.dma_start(x_again[:, 0:NB - 1, :], x[0:full, :].rearrange("(b p) f -> p b f", p=P))\
              .then_inc(x_again_in, 16)
            sp.wait_ge(x_pad_set, 1)
            sp.dma_start(x_again[0:LASTB, NB - 1, :], x[full:N, :]).then_inc(x_again_in, 16)

            for e in range(NE):
                sp.dma_start(w1_all[:, e, :].rearrange("p (k h) -> p k h", k=KF),
                             w1[e, :, :].rearrange("(k p) h -> p k h", p=P)).then_inc(w1_in, 16)
            for e in range(NE):
                if e == W2_FIRST:
                    sp.wait_ge(x1_made, 1)
                sp.dma_start(w2_all[:, e, :, :], w2[e, :, :].rearrange("(c p) f -> p c f", p=P))\
                  .then_inc(w2_in, 16)

            def load_slots(j, u, first=False):
                if not first:
                    sp.wait_ge(xsT_done, j - 1)
                sp.dma_start(xs_in[:, u, :, :],
                             xs_tab[bass.ds(j * BS, BS), :].rearrange("(m p) f -> p m f", p=P))\
                  .then_inc(xs_got[u], 16)

            sp.wait_ge(xs_put, 16 * TOP * NB)
            load_slots(0, 0, first=True)
            load_slots(1, 1, first=True)
            with sp.Fori(1, NBLK // 2, 1) as i:
                load_slots(2 * i, 0)
                load_slots(2 * i + 1, 1)
            for j in range(NBLK // 2 * 2, NBLK):
                load_slots(j, j % 2)
            with sp.Fori(0, NB - 1, 1) as b:
                sp.wait_ge(combined, b + 1)
                sp.dma_start(out[bass.ds(b * P, P), :],
                             acc[:, bass.ds(b, 1), 0:F].rearrange("p b f -> p (b f)")).then_inc(s_out, 16)
            sp.wait_ge(combined, NB)
            sp.dma_start(out[full:N, :], acc[0:LASTB, NB - 1, 0:F]).then_inc(s_out, 16)
            sp.wait_ge(s_out, 16 * NB)

        @block.gpsimd
        def _(pool):
            for m in (ident, shift, corner):
                pool.memset(m[:, :], 0.0).then_inc(s_pool, 1)
            pool.memset(ones[:, :], 1.0).then_inc(s_const, 1)
            pool.memset(zeros[0:Q, :], 0.0).then_inc(zeros_set, 1)
            pool.memset(srcA[:, Q, :], 0).then_inc(s_const, 1)
            pool.wait_ge(s_pool, 3)
            for m, base, mult in ((ident, 0, 1), (shift, -1, 1), (corner, P - 1, P)):
                pool.affine_select(out=m[:, :], in_=m[:, :], compare_op=ALU.not_equal, fill=1.0,
                                   base=base, pattern=[[-1, P]], channel_multiplier=mult)\
                    .then_inc(s_const, 1)
            for t, base, pattern, mult in ((iota_f, 0, [[1, P]], 0), (iota_g, 0, [[1, G]], 0),
                                           (pcol, 0, [[1, 1]], 1), (node_id, 0, [[P, NB]], 1),
                           (ring_slot, 0, [[0, Q // RING], [1, RING]], 0)):
                pool.iota(t[:, :], pattern=pattern, base=base, channel_multiplier=mult,
                          allow_small_or_imprecise_dtypes=True).then_inc(s_const, 1)
            pool.wait_ge(dst_stored, 16)
            pool.wait_ge(q_ready, 1)
            for b in range(NB):
                if b >= ROWBUF:
                    pool.wait_ge(rows_used, b - ROWBUF + 1)
                pool.indirect_dma_start(
                    out=drow[:, b % ROWBUF, :], out_offset=None, in_=dst_tab,
                    in_offset=bass.IndirectOffsetOnAxis(ap=qi[:, b:b + 1], axis=0))\
                    .then_inc(rows_got[b % ROWBUF], 16)
            def pick_row(t, u):
                pool.tensor_copy(picks[:, u, :],
                                 srcA[:, bass.ds(t, 1), :].rearrange("p q r -> p (q r)"))\
                    .then_inc(picks_set, 1)

            def gather_row(trip, u, first=False, exact=False):
                t = trip * RING + u
                if not first or u >= OHS:
                    pool.wait_ge(gathered[u % OHS], 16 * TPR * (trip * (RING // OHS) + u // OHS))
                if exact:
                    steps = pool.value_load(left_i[0:1, bass.ds(t - RING, 1)], min_val=1, max_val=LEFT + NB - 1)
                    pool.wait_ge(group_done, steps)
                elif not first:
                    pool.wait_ge(group_done, t - RING + NB)
                pool.wait_ge(picks_set, t + 1)
                pick_row(t + 1, (u + 1) % RING)
                for r in range(TPR):
                    pool.indirect_dma_start(
                        out=ring[:, u, r, 0:HF], out_offset=None, in_=h_tab,
                        in_offset=bass.IndirectOffsetOnAxis(ap=picks[:, u, r:r + 1], axis=0))\
                        .then_inc(gathered[u % OHS], 16)

            pool.wait_ge(h_stored[0], 16 * ((NB // 2 + 1) // 2))
            pool.wait_ge(h_stored[1], 16 * (NB // 2 // 2))
            pool.wait_ge(edges_A, 4)
            pool.wait_ge(early_over, 1)
            pool.wait_ge(ed_zeroed, 16)
            pool.wait_ge(lo_stored, 16)
            pick_row(0, 0)
            for u in range(RING):
                gather_row(0, u, first=True)
                if u == 2 * OHS:
                    pool.wait_ge(spos_ready, 1)
                    for b in range(NB):
                        pool.indirect_dma_start(
                            out=ed_tab, out_offset=bass.IndirectOffsetOnAxis(ap=spos[:, b:b + 1], axis=0),
                            in_=e_node[:, b, H:2 * H], in_offset=None).then_inc(ed_put, 16)
            ed_hj = edB[0:Q, :, :].rearrange("q j h -> q h j")
            scores = scoreB[0:Q, :, :]
            pool.wait_ge(esB_copied, TPR)
            pool.wait_ge(ed_full, 1)
            pool.tensor_tensor(scores, esB[0:Q, :, :], ed_hj, ALU.add).then_inc(z_made, 1)
            pool.wait_ge(score_ready, TPR)
            pool.memset(acc_flat, 0.0).then_inc(acc_zeroed, 1)
            pool.memset(zero_src, 0.0).then_inc(zero_ready, 1)
            pool.wait_ge(left_ready, 1)
            with pool.Fori(1, 1 + LEFT // RING, 1) as trip:
                for u in range(RING):
                    gather_row(trip, u, exact=True)
            with pool.Fori(1 + LEFT // RING, Q // RING, 1) as trip:
                for u in range(RING):
                    gather_row(trip, u)

            pool.wait_ge(pos_ready, 1)
            pool.wait_ge(xs_zeroed, 16 * 9)
            for k in range(TOP):
                for b in range(NB):
                    rows = P if b < NB - 1 else LASTB
                    pool.indirect_dma_start(
                        out=xs_tab, out_offset=bass.IndirectOffsetOnAxis(ap=pos_i[0:rows, k, b:b + 1], axis=0),
                        in_=xn1[0:rows, b, :], in_offset=None).then_inc(xs_put, 16)
            pool.wait_ge(y_stored[0], 16 * ((NBLK + 1) // 2))
            pool.wait_ge(y_stored[1], 16 * (NBLK // 2))
            for b in range(NB):
                rows = P if b < NB - 1 else LASTB
                if b >= YS:
                    pool.wait_ge(combined, b - YS + 1)
                for k in range(TOP):
                    pool.indirect_dma_start(
                        out=y_in[0:rows, b % YS, k, :], out_offset=None, in_=ys_tab,
                        in_offset=bass.IndirectOffsetOnAxis(ap=pos_i[0:rows, k, b:b + 1], axis=0))\
                        .then_inc(y_got[b % YS], 16)

        NCONST = 10

        @block.tensor
        def _(pe):
            pe.wait_ge(s_const, NCONST)
            pe.wait_ge(edges_f, 1)
            for r in range(TPR):
                for n, row in enumerate((src_f[0:Q, :], dst_f[0:Q, 1:RL + 1])):
                    to = bank[4 + n][:, r * Q:(r + 1) * Q] if r < 4 else bank[6][:, n * Q:(n + 1) * Q]
                    last = pe.transpose(to, row[:, r * P:(r + 1) * P], ident[0:Q, 0:Q])
            last.then_inc(edges_T, 1)
            pe.wait_ge(row_diag, 1)
            pe.matmul(bank[7][:, 0:Q], ones[0:Q, :], diag[0:Q, :], start=True, stop=True)\
              .then_inc(row_ends, 1)
            pe.wait_ge(q_ready, 1)
            pe.matmul(bank[7][:, 0:NB], ones[0:1, :], qn[0:1, :], start=True, stop=True)\
              .then_inc(tb_done, 1)

            pe.wait_ge(wext_ready, 1)

            def transposes(i):
                pe.wait_ge(xn_ready, 2 * i + 2)
                if i >= 2:
                    pe.wait_ge(xT_copied, i - 1)
                for b in range(2):
                    for k in range(KF):
                        last = pe.transpose(bank[i % 2][:, (b * KF + k) * P:(b * KF + k + 1) * P],
                                            xs0[:, 2 * i + b, k * P:(k + 1) * P], ident[:, :])
                last.then_inc(xT_done, 1)

            def project(i):
                pe.wait_ge(xT_copied, i + 1)
                if i >= 2:
                    pe.wait_ge(h_copied, i - 1)
                for b in range(2):
                    for k in range(KF):
                        last = pe.matmul(bank[2 + 2 * (i % 2) + b][:, 0:wide], xT0[:, i % 2, b, k, :],
                                         w_ext[:, k, :], start=(k == 0), stop=(k == KF - 1))
                last.then_inc(h_done, 1)

            pe.wait_ge(edges_A, 4)
            transposes(0)
            for i in range(NB // 2):
                if i + 1 < NB // 2:
                    transposes(i + 1)
                project(i)

            pe.wait_ge(start_ready, 1)
            pe.matmul(bank[7][:, 0:NB], shift[:, :], start[:, 0:NB], start=True, stop=False)
            pe.matmul(bank[7][:, 0:NB], corner[:, :], start[:, 1:NB + 1], start=False,
                      stop=True).then_inc(next_done, 1)
            pe.wait_ge(coef_ready, 1)
            pe.wait_ge(spos_ready, 1)
            for n in range(3):
                last = pe.transpose(bank[7][0:H, n * Q:(n + 1) * Q], coef[0:Q, n * H:(n + 1) * H],
                                    ident[0:Q, 0:Q])
            last.then_inc(coefT_done, 1)

            def look_up(q, u, n, first=False):
                pe.wait_ge(lo_oh_ready[u], n + 1)
                if not first:
                    pe.wait_ge(es_selected, q - OHS + 1)
                for r in range(TPR):
                    for part in range(3):
                        last = pe.matmul(bank[u][:, r * H * NB:(r + 1) * H * NB],
                                         lo_oh[:, u, r * P:(r + 1) * P],
                                         t3[:, part, :, :].rearrange("p h b -> p (h b)"),
                                         start=(part == 0), stop=(part == 2))
                last.then_inc(es_done, 1)

            pe.wait_ge(h_copied, NB // 2)
            pe.wait_ge(t3_ready, 1)
            for u in range(OHS):
                look_up(u, u, 0, first=True)
            with pe.Fori(1, Q // OHS, 1) as i:
                for u in range(OHS):
                    look_up(i * OHS + u, u, i)
            pe.wait_ge(es_picked, Q)
            for r in range(TPR):
                if r >= 2:
                    pe.wait_ge(esB_copied, r - 1)
                for h in range(H):
                    last = pe.transpose(bank[5 + r % 2][0:Q, h * P:(h + 1) * P], exA[:, :, r, h],
                                        ident[:, :])
                last.then_inc(esT_done, 1)
            for n in range(3):
                pe.wait_ge(tails_ready, n + 1)
                tails = (mxB[0:Q, :, RL - 1], mxB[0:Q, :, RL - 1], bwdB[0:Q, :, 0])[n]
                pe.transpose(bank[7][0:H, 0:Q], tails, ident[0:Q, 0:Q]).then_inc(tailsT_done, 1)
                pe.wait_ge(rows_scanned, n + 1)
                pe.transpose(bank[7][0:Q, 256:256 + H], carry_row[:, (0, 0, 1)[n]:(0, 0, 1)[n] + Q],
                             ident[0:H, 0:H]).then_inc(carry_done, 1)
            for r in range(TPR):
                pe.wait_ge(ex_ready, r + 1)
                if r >= 2:
                    pe.wait_ge(exA_copied, r - 1)
                for h in range(H):
                    last = pe.transpose(bank[5 + r % 2][:, h * Q:(h + 1) * Q],
                                        esB[0:Q, h, r * P:(r + 1) * P], ident[0:Q, 0:Q])
                last.then_inc(exT_done, 1)

            def group(i, u, first=False):
                pe.wait_ge(dst_oh_ready, i + 1)
                if not first:
                    pe.wait_ge(flushed, i - OHS + 1)
                slot = pe.value_load(slot_i[0:1, bass.ds(i, 1)], min_val=0, max_val=RING - 1)
                for r in range(TPR):
                    last = pe.matmul(bank[u][:, 0:MW], dst_oh[:, u, r, :],
                                     ring[:, bass.ds(slot, 1), r, :].rearrange("p s w -> p (s w)"),
                                     start=(r == 0), stop=(r == TPR - 1))
                last.then_inc(group_done, 1)

            for u in range(OHS):
                group(u, u, first=True)
            with pe.Fori(1, G // OHS, 1) as i:
                for u in range(OHS):
                    group(i * OHS + u, u)
            for i in range(G // OHS * OHS, G):
                group(i, i % OHS)

            pe.wait_ge(consts_in, 16 * 6)
            pe.transpose(bank[7][:, 0:NE * FC], b1_rows, ident[0:NE * FC, 0:NE * FC])\
              .then_inc(b1_T_done, 1)

            def nodes_T(i):
                pe.wait_ge(xn1_ready, 2 * i // NORM_SET + 1)
                if i >= 2:
                    pe.wait_ge(xT1_copied, i - 1)
                for b in range(2):
                    for k in range(KF):
                        last = pe.transpose(bank[i % 2][:, (b * KF + k) * P:(b * KF + k + 1) * P],
                                            xn1[:, 2 * i + b, k * P:(k + 1) * P], ident[:, :])
                last.then_inc(xT1_done, 1)

            def router(i):
                pe.wait_ge(xT1_copied, i + 1)
                for b in range(2):
                    at = (2 * i + b) * NE
                    for k in range(KF):
                        last = pe.matmul(bank[2][:, at:at + NE], xT1[:, i % 2, b, k, :], wr_sb[:, k, :],
                                         start=(k == 0), stop=(k == KF - 1))
                last.then_inc(logits_done, 1)

            nodes_T(0)
            for i in range(NB // 2):
                if i + 1 < NB // 2:
                    nodes_T(i + 1)
                router(i)
            pe.wait_ge(mask_ready, 1)
            mask_flat = mask.rearrange("p b e -> p (b e)")
            pe.matmul(bank[3][:, 0:NB * NE], upper, mask_flat, start=True, stop=True)
            pe.matmul(bank[4][:, 0:NB * NE], ones[:, :], mask_flat, start=True, stop=True)\
              .then_inc(ranks_done, 1)

            def slots_T(j, u, n, first=False):
                pe.wait_ge(xs_got[u], 16 * (n + 1))
                if not first:
                    pe.wait_ge(xsT_copied, j - 1)
                for k in range(KF):
                    for m in range(BM):
                        last = pe.transpose(bank[u][:, k * BS + m * P:k * BS + (m + 1) * P],
                                            xs_in[:, u, m, k * P:(k + 1) * P], ident[:, :])
                last.then_inc(xsT_done, 1)

            def layer_1(j, u, first=False):
                pe.wait_ge(xsT_copied, j + 1)
                pe.wait_ge(w1_picked, j + 1)
                if not first:
                    pe.wait_ge(gelu_done, FC * (j - 1))
                for c in range(FC):
                    for k in range(KF):
                        last = pe.matmul(bank[2 + 2 * u + c // 2][:, c % 2 * BS:(c % 2 + 1) * BS],
                                         w1_now[:, u, k, c * P:(c + 1) * P], xsT[:, u, k, :],
                                         start=(k == 0), stop=(k == KF - 1))
                    if c % 2:
                        last.then_inc(l1_done, 1)

            def layer_2(j, u, first=False):
                e = pe.value_load(blk_e[0:1, bass.ds(j, 1)], min_val=0, max_val=NE - 1)
                pe.wait_ge(gelu_done, FC * (j + 1))
                if not first:
                    pe.wait_ge(y_ready, j - 1)
                for m in range(BM):
                    for c in range(FC):
                        last = pe.matmul(bank[6 + u][:, m * F:(m + 1) * F],
                                         hT[:, u, c, m * P:(m + 1) * P],
                                         w2_all[:, bass.ds(e, 1), c, :].rearrange("p e f -> p (e f)"),
                                         start=(c == 0), stop=(c == FC - 1))
                last.then_inc(l2_done, 1)

            pe.wait_ge(w2_in, 16 * NE)
            slots_T(0, 0, 0, first=True)
            layer_1(0, 0, first=True)
            slots_T(1, 1, 0, first=True)
            layer_1(1, 1, first=True)
            layer_2(0, 0, first=True)
            slots_T(2, 0, 1)
            layer_1(2, 0)
            layer_2(1, 1, first=True)
            with pe.Fori(1, (NBLK - 1) // 2, 1) as i:
                slots_T(2 * i + 1, 1, i)
                layer_1(2 * i + 1, 1)
                layer_2(2 * i, 0)
                slots_T(2 * i + 2, 0, i + 1)
                layer_1(2 * i + 2, 0)
                layer_2(2 * i + 1, 1)
            for j in range(2 * ((NBLK - 1) // 2), NBLK):
                if j + 1 < NBLK:
                    slots_T(j + 1, (j + 1) % 2, (j + 1) // 2)
                    layer_1(j + 1, (j + 1) % 2)
                layer_2(j, j % 2)

        @block.scalar
        def _(act):
            act.wait_ge(edges_T, 1)
            for n, to in enumerate((srcA, dstA)):
                act.activation(to[:, 0:Q, 0:4], bank[4 + n][:, 0:4 * Q].rearrange("p (r q) -> p q r", r=4),
                               ACT.Copy).then_inc(edges_A, 1)
                act.activation(to[:, 0:Q, 4], bank[6][:, n * Q:(n + 1) * Q], ACT.Copy).then_inc(edges_A, 1)
            act.wait_ge(var_ready, 1)
            act.activation(rstd[:, :], sm1[:, :], ACT.Sqrt).then_inc(std_ready, 1)
            for i in range(NB // 2):
                act.wait_ge(xT_done, i + 1)
                if i >= 2:
                    act.wait_ge(h_done, i - 1)
                act.activation(xT0[:, i % 2, :, :, :].rearrange("p b k n -> p (b k n)"), bank[i % 2],
                               ACT.Copy).then_inc(xT_copied, 1)
                act.wait_ge(h_done, i + 1)
                two = psum[:, 2 + 2 * (i % 2):4 + 2 * (i % 2), :]
                act.activation(e_node[:, 2 * i:2 * i + 2, :], two[:, :, HF:wide], ACT.Copy)\
                   .then_inc(e_copied, 1)
                if i >= 2:
                    act.wait_ge(h_stored[i % 2], 16 * (i // 2))
                act.activation(h_stage[:, i % 2, :, :], two[:, :, 0:HF], ACT.Copy).then_inc(h_copied, 1)

            def onehot(i, u, n, first=False):
                act.wait_ge(lo_in[u], 16 * (i + 1))
                if not first:
                    act.wait_ge(es_done, OHS * i - OHS + u + 1)
                act.activation(off[:, n, :], lo_bc[:, u, :], ACT.Abs, bias=minus_p[:, 0:1])\
                   .then_inc(off_ready, 1)
                act.wait_ge(off_ready, len(ACT_ROWS) * i + n + 1)
                act.activation(lo_oh[:, u, :], off[:, n, :], ACT.Relu, bias=ones[:, 0:1], scale=-1.0)\
                   .then_inc(lo_oh_ready[u], 1)

            act.wait_ge(minus_p_set, 1)
            for n, u in enumerate(ACT_ROWS):
                onehot(0, u, n, first=True)
            with act.Fori(1, Q // OHS, 1) as i:
                for n, u in enumerate(ACT_ROWS):
                    onehot(i, u, n)

            for r in range(TPR):
                act.wait_ge(esT_done, r + 1)
                act.activation(esB[0:Q, :, r * P:(r + 1) * P],
                               bank[5 + r % 2][0:Q, :].rearrange("q (h p) -> q h p", h=H),
                               ACT.Copy).then_inc(esB_copied, 1)
            for r in range(TPR):
                at = slice(r * P, (r + 1) * P)
                act.wait_ge(score_ready, r + 1)
                act.activation(esB[0:Q, :, at], esB[0:Q, :, at], ACT.Exp).then_inc(ex_ready, 1)
            for r in range(TPR):
                act.wait_ge(exT_done, r + 1)
                act.activation(exA[:, :, r, :].rearrange("p q h -> p h q"),
                               bank[5 + r % 2][:, 0:H * Q].rearrange("p (h q) -> p h q", h=H),
                               ACT.Copy).then_inc(exA_copied, 1)

            for n in range(2):
                for part in range(2):
                    act.wait_ge(var_ready, 2 * n + part + 2)
                    of = slice(part * NORM_HALF, (part + 1) * NORM_HALF)
                    act.activation(rstd1[:, of], tmp1[:, of], ACT.Sqrt).then_inc(std_ready, 1)
                for b in range(NB):
                    if b % NORM_HALF == 0:
                        act.wait_ge(norm_ready, 2 * n + b // NORM_HALF + 1)
                    act.activation(xn1[:, b, :], acc[:, b, 0:HF] if n == 0 else xn1[:, b, :], ACT.Identity,
                                   scale=rstd1[:, b:b + 1], bias=shift1[:, b:b + 1]).then_inc(normed, 1)
            for i in range(NB // 2):
                act.wait_ge(xT1_done, i + 1)
                if i >= 2:
                    act.wait_ge(logits_done, i - 1)
                act.activation(xT1[:, i % 2, :, :, :].rearrange("p b k n -> p (b k n)"), bank[i % 2],
                               ACT.Copy).then_inc(xT1_copied, 1)
            act.wait_ge(gap_ready, 1)
            act.activation(w_b, tmp1, ACT.Exp).then_inc(gap_exp, 1)

            def hidden(j, u, first=False):
                e = act.value_load(blk_e[0:1, bass.ds(j, 1)], min_val=0, max_val=NE - 1)
                if not first:
                    act.wait_ge(l2_done, j - 1)
                for c in range(FC):
                    if c % 2 == 0:
                        act.wait_ge(l1_done, FC // 2 * j + c // 2 + 1)
                    act.activation(hT[:, u, c, :],
                                   bank[2 + 2 * u + c // 2][:, c % 2 * BS:(c % 2 + 1) * BS], ACT.Gelu,
                                   bias=b1_T[:, bass.ds(e * FC + c, 1)]).then_inc(gelu_done, 1)

            def store_y(j, u):
                act.wait_ge(y_ready, j + 1)
                act.dma_start(ys_tab[bass.ds(j * BS, BS), :].rearrange("(m p) f -> p m f", p=P),
                              y_out[:, u, :, :]).then_inc(y_stored[u], 16)

            act.wait_ge(pos_ready, 1)
            act.wait_ge(b1_T_ready, 1)
            hidden(0, 0, first=True)
            hidden(1, 1, first=True)
            store_y(0, 0)
            with act.Fori(1, NBLK // 2, 1) as i:
                hidden(2 * i, 0)
                store_y(2 * i - 1, 1)
                hidden(2 * i + 1, 1)
                store_y(2 * i, 0)
            for j in range(NBLK // 2 * 2, NBLK + 1):
                if j < NBLK:
                    hidden(j, j % 2)
                store_y(j - 1, (j - 1) % 2)

        @block.vector
        def _(v):
            c = Chain(v, s_dve)
            v.memset(dst_i[0:Q, :], -1).then_inc(pads_set, 1)
            v.memset(xs0[:, NB - 1, :], 0.0).then_inc(pads_set, 1)
            v.wait_ge(dst_in, 96)
            c.link(v.tensor_copy(dst_f[0:Q, :], dst_i[0:Q, :]))
            v.wait_ge(src_in, 16)
            v.tensor_copy(src_f[0:Q, :], src_i[0:Q, :]).then_inc(edges_f, 1)
            c.link(v.tensor_scalar(lo_i[0:Q, :], src_i[0:Q, :], P - 1, None, ALU.bitwise_and))
            v.tensor_copy(lo_b[0:Q, :], lo_i[0:Q, :]).then_inc(lo_ready, 1)
            c.link(v.tensor_tensor(keep[0:Q, :], dst_f[0:Q, 0:RL + 1], dst_f[0:Q, 1:RL + 2],
                                   ALU.is_equal))
            v.tensor_scalar(reset[0:Q, :], keep[0:Q, :], 1.0, BIG, ALU.subtract, ALU.mult)
            for n, (a, b) in enumerate(((RL, 0), (RL, 0), (1, RL + 1))):
                c.link(v.tensor_tensor(coef[0:Q, n * H:(n + 1) * H],
                                       dst_f[0:Q, a:a + 1].broadcast_to([Q, H]),
                                       dst_f[0:Q, b:b + 1].broadcast_to([Q, H]), ALU.is_equal))
            v.tensor_scalar(coef[0:Q, H:3 * H], coef[0:Q, H:3 * H], 1.0, BIG, ALU.subtract, ALU.mult)\
             .then_inc(coef_ready, 1)
            v.wait_ge(s_const, NCONST)
            v.tensor_scalar(diag[0:Q, :], ident[0:Q, 0:Q], dst_f[0:Q, RL:RL + 1], None, ALU.mult)\
             .then_inc(row_diag, 1)
            v.tensor_scalar(minus_p[:, :], pcol[:, :], -1.0, None, ALU.mult).then_inc(minus_p_set, 1)
            v.wait_ge(w_in, 16 * KF)
            v.wait_ge(a_in, 32)
            for k in range(KF):
                for s in range(2):
                    c.link(v.tensor_tensor(w_tmp[:, s, :], w_ext[:, k, 0:HF], a_bc[:, s, :], ALU.mult))
                c.link(v.tensor_reduce(
                    w_ext[:, k, HF:wide], w_tmp.rearrange("p s (h o) -> p (s h) o", h=H), AX.X, ALU.add))
            v.nop().then_inc(wext_ready, 1)
            v.wait_ge(row_ends, 1)
            c.link(v.tensor_tensor(q_tmp, bank[7][:, 0:Q].unsqueeze(1).broadcast_to([P, NB, Q]),
                                   node_id[:, :].unsqueeze(2).broadcast_to([P, NB, Q]), ALU.is_lt))
            c.link(v.tensor_reduce(qn[:, :], q_tmp, AX.X, ALU.add))
            c.link(v.tensor_scalar(qn[:, :], qn[:, :], float(Q - 1), None, ALU.min))
            v.tensor_copy(qi[:, :], qn[:, :]).then_inc(q_ready, 1)
            v.wait_ge(x_in, 32)
            for b in range(NB):
                last = v.bn_stats(st0[:, b, :], xs0[:, b, :])
            c.link(last)
            c.link(v.tensor_tensor(mean[:, :], st0[:, :, 1], st0[:, :, 4], ALU.add))
            c.link(v.tensor_scalar(mean[:, :], mean[:, :], 0.5, None, ALU.mult))
            c.link(v.tensor_tensor(sm1[:, :], st0[:, :, 1], st0[:, :, 4], ALU.subtract))
            c.link(v.tensor_tensor(sm1[:, :], sm1[:, :], sm1[:, :], ALU.mult))
            c.link(v.tensor_tensor(sm2[:, :], st0[:, :, 2], st0[:, :, 5], ALU.add))
            c.link(v.scalar_tensor_tensor(sm1[:, :], sm1[:, :], F / 4.0, sm2[:, :], ALU.mult, ALU.add))
            v.tensor_scalar(sm1[:, :], sm1[:, :], 1.0 / F, EPS, ALU.mult, ALU.add).then_inc(var_ready, 1)
            v.wait_ge(std_ready, 1)
            c.link(v.reciprocal(rstd[:, :], rstd[:, :]))
            for b in range(NB):
                v.tensor_scalar(xs0[:, b, :], xs0[:, b, :], mean[:, b:b + 1], rstd[:, b:b + 1],
                                ALU.subtract, ALU.mult).then_inc(xn_ready, 1)
            v.wait_ge(edges_A, 4)
            c.link(v.tensor_scalar(hi_i, srcA[:, 0:Q, :].rearrange("p q r -> p (q r)"), 7, None,
                                   ALU.arith_shift_right))
            c.link(v.tensor_copy(hiA[:, :, :].rearrange("p q r -> p (q r)"), hi_i))
            v.wait_ge(tb_done, 1)
            c.link(v.tensor_tensor(enters[:, :], bank[7][:, 1:NB], iota_f[:, 1:NB], ALU.add))
            c.link(v.tensor_tensor(path_tmp, enters[:, :].unsqueeze(1).broadcast_to([P, G, NB - 1]),
                                   iota_g[:, :].unsqueeze(2).broadcast_to([P, G, NB - 1]), ALU.is_le))
            c.link(v.tensor_reduce(beta_f[:, :], path_tmp, AX.X, ALU.add))
            v.tensor_copy(beta_i[:, :], beta_f[0:1, :])
            c.link(v.tensor_tensor(first_row[:, :], enters[:, :], iota_f[:, 1:NB], ALU.subtract))
            c.link(v.tensor_tensor(left_tmp[0:1], first_row[0:1, :].unsqueeze(1).broadcast_to([1, LEFT, NB - 1]),
                                   iota_g[0:1, 0:LEFT].unsqueeze(2).broadcast_to([1, LEFT, NB - 1]),
                                   ALU.is_le))
            c.link(v.tensor_reduce(left_f[0:1, :], left_tmp[0:1], AX.X, ALU.add))
            v.scalar_tensor_tensor(left_i[:, :], left_f[0:1, :], 1.0, iota_g[0:1, 0:LEFT],
                                   ALU.add, ALU.add).then_inc(left_ready, 1)
            c.link(v.tensor_tensor(slot_f[:, :], iota_g[0:1, :], beta_f[0:1, :], ALU.subtract))
            v.tensor_copy(tau_i[:, :], slot_f[:, :])
            for n in range(Q // RING - 1, 0, -1):
                c.link(v.tensor_scalar(path_f[:, :], slot_f[:, :], float(n * RING), float(RING * n),
                                       ALU.is_ge, ALU.mult))
                c.link(v.tensor_tensor(slot_f[:, :], slot_f[:, :], path_f[:, :], ALU.subtract))
            c.link(v.tensor_copy(slot_i[:, :], slot_f[:, :]))
            c.link(v.tensor_scalar(beta_f[:, :], beta_f[:, :], float(P), None, ALU.mult))
            for b in range(NB):
                v.wait_ge(rows_got[b % ROWBUF], 16 * (b // ROWBUF + 1))
                v.tensor_scalar(drow[:, b % ROWBUF, :], drow[:, b % ROWBUF, :], node_id[:, b:b + 1], None,
                                ALU.is_lt, ALU.add, accum_out=start[:, b:b + 1]).then_inc(rows_used, 1)
            c.link(v.memset(start[:, NB:NB + 1], float(E)))
            c.link(v.scalar_tensor_tensor(start[:, 0:NB], qn[:, :], float(RL), start[:, 0:NB],
                                          ALU.mult, ALU.add))
            v.nop().then_inc(start_ready, 1)
            v.wait_ge(next_done, 1)
            c.link(v.tensor_tensor(sm1[:, :], bank[7][:, 0:NB], start[:, 0:NB], ALU.is_equal))
            c.link(v.scalar_tensor_tensor(sm2[:, :], node_id[:, :], float(E), start[:, 0:NB],
                                          ALU.add, ALU.subtract))
            c.link(v.tensor_tensor(sm1[:, :], sm1[:, :], sm2[:, :], ALU.mult))
            v.tensor_tensor(spos[:, :], sm1[:, :], start[:, 0:NB], ALU.add).then_inc(spos_ready, 1)

            v.wait_ge(coefT_done, 1)
            v.tensor_copy(coef_row[:, :, :], bank[7][0:H, 0:3 * Q].rearrange("h (n q) -> h n q", n=3))\
             .then_inc(early_over, 1)
            v.wait_ge(e_copied, NB // 2)
            es = e_node[:, :, 0:H].rearrange("p b h -> p h b")
            res = t_res[:, :, :]
            c.link(v.tensor_copy(t3[:, 0, :, :], es))
            c.link(v.tensor_tensor(res, es, t3[:, 0, :, :], ALU.subtract))
            c.link(v.tensor_copy(t3[:, 1, :, :], res))
            c.link(v.tensor_tensor(res, res, t3[:, 1, :, :], ALU.subtract))
            v.tensor_copy(t3[:, 2, :, :], res).then_inc(t3_ready, 1)

            def lo_onehot(i, u):
                if u not in ACT_ROWS:
                    v.wait_ge(lo_in[u], 16 * (i + 1))
                    v.tensor_scalar(lo_oh[:, u, :], lo_bc[:, u, :], pcol[:, 0:1], None, ALU.is_equal)\
                     .then_inc(lo_oh_ready[u], 1)

            def hi_onehot(q, u):
                v.tensor_tensor(
                    hi_oh[:, u, :, :],
                    hiA[:, bass.ds(q, 1), :].rearrange("p q r -> p (q r)").unsqueeze(2)
                    .broadcast_to([P, TPR, NB]),
                    iota_f[:, 0:NB].unsqueeze(1).broadcast_to([P, TPR, NB]), ALU.is_equal)\
                 .then_inc(hi_oh_ready, 1)

            def pick(i, u, more=True):
                q = i * OHS + u
                v.wait_ge(hi_oh_ready, q + 1)
                v.wait_ge(es_done, q + 1)
                v.tensor_tensor(
                    es_sel[:, u, :].rearrange("p (r h b) -> p r h b", r=TPR, h=H),
                    bank[u][:, 0:TPR * H * NB].rearrange("p (r h b) -> p r h b", r=TPR, h=H),
                    hi_oh[:, u, :, :].unsqueeze(2).broadcast_to([P, TPR, H, NB]), ALU.mult)\
                 .then_inc(es_selected, 1)
                if more:
                    lo_onehot(i + 1, u)
                v.wait_ge(es_selected, q + 1)
                v.tensor_reduce(exA[:, bass.ds(q, 1), :, :].rearrange("p q r h -> p (q r h)"),
                                es_sel[:, u, :].rearrange("p (a b) -> p a b", b=NB), AX.X, ALU.add)\
                 .then_inc(es_picked, 1)
                if more:
                    hi_onehot(q + OHS, u)

            for u in range(OHS):
                lo_onehot(0, u)
                hi_onehot(u, u)
            with v.Fori(0, Q // OHS - 1, 1) as i:
                for u in range(OHS):
                    pick(i, u)
            for u in range(OHS):
                pick(Q // OHS - 1, u, more=False)
            v.wait_ge(es_picked, Q)

            keep0, reset0 = keep[0:Q, 0:RL], reset[0:Q, 0:RL]
            reset1 = reset[0:Q, 1:RL + 1][:, ::-1]

            def across_rows(n, fill, op0, op1, back=False):
                v.nop().then_inc(tails_ready, 1)
                v.wait_ge(tailsT_done, n + 1)
                if back:
                    c.link(v.memset(carry_row[:, Q:Q + 1], fill))
                    v.tensor_tensor_scan(carry_row[:, 0:Q][:, ::-1], coef_row[:, n, :][:, ::-1],
                                         bank[7][0:H, 0:Q][:, ::-1], fill, op0, op1)\
                     .then_inc(rows_scanned, 1)
                else:
                    c.link(v.memset(carry_row[:, 0:1], fill))
                    v.tensor_tensor_scan(carry_row[:, 1:Q + 1], coef_row[:, n, :], bank[7][0:H, 0:Q],
                                         fill, op0, op1).then_inc(rows_scanned, 1)
                v.wait_ge(carry_done, n + 1)
                c.link(v.tensor_copy(carry[0:Q, :], bank[7][0:Q, 256:256 + H]))

            v.wait_ge(ed_in, 16)
            for h in range(H):
                c.link(v.tensor_tensor_scan(mxB[0:Q, h, :], keep0, edB[0:Q, :, h], 0.0,
                                            ALU.mult, ALU.add))
            across_rows(0, 0.0, ALU.mult, ALU.add)
            for h in range(H):
                c.link(v.tensor_tensor_scan(edB[0:Q, :, h], keep0, edB[0:Q, :, h], carry[0:Q, h:h + 1],
                                            ALU.mult, ALU.add))
            v.nop().then_inc(ed_full, 1)
            v.wait_ge(esB_copied, TPR)
            for h in range(H):
                c.link(v.tensor_tensor_scan(mxB[0:Q, h, :], reset0, esB[0:Q, h, :], -BIG,
                                            ALU.add, ALU.max))
            across_rows(1, -BIG, ALU.add, ALU.max)
            for h in range(H):
                c.link(v.tensor_tensor_scan(mxB[0:Q, h, :], reset0, esB[0:Q, h, :], carry[0:Q, h:h + 1],
                                            ALU.add, ALU.max))
            for h in range(H):
                c.link(v.tensor_tensor_scan(bwdB[0:Q, h, :][:, ::-1], reset1, mxB[0:Q, h, :][:, ::-1],
                                            -BIG, ALU.add, ALU.max))
            across_rows(2, -BIG, ALU.add, ALU.max, back=True)
            for h in range(H):
                c.link(v.tensor_tensor_scan(mxB[0:Q, h, :][:, ::-1], reset1, mxB[0:Q, h, :][:, ::-1],
                                            carry[0:Q, h:h + 1], ALU.add, ALU.max))
            ed_hj = edB[0:Q, :, :].rearrange("q j h -> q h j")
            c.link(v.tensor_tensor(mxB[0:Q, :, :], mxB[0:Q, :, :], ed_hj, ALU.add))
            c.link(v.scalar_tensor_tensor(mxB[0:Q, :, :], mxB[0:Q, :, :], 0.2, mxB[0:Q, :, :],
                                          ALU.mult, ALU.max))
            v.wait_ge(z_made, 1)
            c.link(v.scalar_tensor_tensor(scoreB[0:Q, :, :], scoreB[0:Q, :, :], 0.2, scoreB[0:Q, :, :],
                                          ALU.mult, ALU.max))
            for r in range(TPR):
                at = slice(r * P, (r + 1) * P)
                v.tensor_tensor(esB[0:Q, :, at], scoreB[0:Q, :, at], mxB[0:Q, :, at], ALU.subtract)\
                 .then_inc(score_ready, 1)

            def scale_row(trip, u):
                t = trip * OHS + u
                s = v.value_load(ring_slot[0:1, bass.ds(t, 1)], min_val=0, max_val=RING - 1)
                v.wait_ge(gathered[u], 16 * TPR * (trip + 1))
                msg = ring[:, bass.ds(s, 1), :, 0:HF].rearrange("p s r (h o) -> p (s r) h o", h=H)
                ex = exA[:, bass.ds(t, 1), :, :].rearrange("p q r h -> p (q r) h")
                v.tensor_tensor(msg, msg, ex.unsqueeze(3).broadcast_to([P, TPR, H, FO]), ALU.mult)
                v.tensor_copy(ring[:, bass.ds(s, 1), :, HF:MW].rearrange("p s r h -> p (s r) h"), ex)

            def dst_onehot(trip, u):
                t = trip * OHS + u
                tau = v.value_load(tau_i[0:1, bass.ds(t, 1)], min_val=0, max_val=Q - 1)
                v.scalar_tensor_tensor(
                    dst_oh[:, u, :, :], iota_f[:, :].unsqueeze(1).broadcast_to([P, TPR, P]),
                    beta_f[:, bass.ds(t, 1)],
                    dstA[:, bass.ds(tau, 1), :].rearrange("p q r -> p (q r)").unsqueeze(2)
                    .broadcast_to([P, TPR, P]), ALU.add, ALU.is_equal).then_inc(dst_oh_ready, 1)

            def flush(trip, u):
                i = trip * OHS + u
                blk = v.value_load(beta_i[0:1, bass.ds(i, 1)], min_val=0, max_val=NB - 1)
                v.wait_ge(group_done, i + 1)
                a = acc[:, bass.ds(blk, 1), :].rearrange("p b w -> p (b w)")
                v.tensor_tensor(a, a, bank[u][:, 0:MW], ALU.add).then_inc(flushed, 1)
                v.wait_ge(flushed, i + 1)

            v.wait_ge(exA_copied, TPR)
            v.wait_ge(acc_zeroed, 1)
            for u in range(OHS):
                scale_row(0, u)
                dst_onehot(0, u)
            with v.Fori(0, Q // OHS - 1, 1) as i:
                for u in range(OHS):
                    flush(i, u)
                    scale_row(i + 1, u)
                    dst_onehot(i + 1, u)
            full_rows, full_steps = Q // OHS, G // OHS
            with v.Fori(full_rows - 1, full_steps - 1, 1) as i:
                for u in range(OHS):
                    flush(i, u)
                    dst_onehot(i + 1, u)
            for i in range((full_steps - 1) * OHS, G):
                flush(i // OHS, i % OHS)
                if i + OHS < G:
                    dst_onehot(i // OHS + 1, i % OHS)


            v.wait_ge(group_done, G)
            v.memset(x_again[:, NB - 1, :], 0.0).then_inc(x_pad_set, 1)
            c.link(v.tensor_scalar(rden, acc[:, :, HF:MW], 1e-9, None, ALU.max))
            c.link(v.reciprocal(rden, rden))
            x1_h = acc[:, :, 0:HF].rearrange("p b (h o) -> p b h o", h=H)
            x1 = acc[:, :, 0:HF]
            c.link(v.tensor_tensor(x1_h, x1_h, rden.unsqueeze(3).broadcast_to([P, NB, H, FO]), ALU.mult))
            v.wait_ge(x_again_in, 32)
            v.scalar_tensor_tensor(x1, x1, 0.0, x_again, ALU.max, ALU.add).then_inc(x1_made, 1)
            v.wait_ge(x1_made, 1)

            def stats(source, part):
                for b in range(part * NORM_HALF, (part + 1) * NORM_HALF):
                    last = v.bn_stats(st1[:, b, :], source[:, b, :])
                c.link(last)
                of = slice(part * NORM_HALF, (part + 1) * NORM_HALF)
                c.link(v.tensor_tensor(mean1[:, of], st1[:, of, 1], st1[:, of, 4], ALU.add))
                c.link(v.tensor_scalar(mean1[:, of], mean1[:, of], 0.5, None, ALU.mult))
                c.link(v.tensor_tensor(tmp1[:, of], st1[:, of, 1], st1[:, of, 4], ALU.subtract))
                c.link(v.tensor_tensor(tmp1[:, of], tmp1[:, of], tmp1[:, of], ALU.mult))
                c.link(v.tensor_tensor(tmp2[:, of], st1[:, of, 2], st1[:, of, 5], ALU.add))
                c.link(v.scalar_tensor_tensor(tmp1[:, of], tmp1[:, of], F / 4.0, tmp2[:, of],
                                              ALU.mult, ALU.add))
                v.tensor_scalar(tmp1[:, of], tmp1[:, of], 1.0 / F, EPS, ALU.mult, ALU.add)\
                 .then_inc(var_ready, 1)

            def scales(n, part):
                of = slice(part * NORM_HALF, (part + 1) * NORM_HALF)
                v.wait_ge(std_ready, 2 * n + part + 2)
                c.link(v.reciprocal(rstd1[:, of], rstd1[:, of]))
                v.scalar_tensor_tensor(shift1[:, of], mean1[:, of], -1.0, rstd1[:, of],
                                       ALU.mult, ALU.mult).then_inc(norm_ready, 1)

            stats(x1, 0)
            stats(x1, 1)
            scales(0, 0)
            scales(0, 1)
            c.link(v.tensor_scalar(upper, iota_f[:, :], pcol[:, 0:1], None, ALU.is_gt))
            c.link(v.tensor_scalar(tmp2, iota_f[:, 0:NB], float(P), pcol[:, 0:1], ALU.mult, ALU.add))
            c.link(v.tensor_scalar(valid, tmp2, float(N), None, ALU.is_lt))
            c.link(v.tensor_scalar(e_less, iota_f[:, 0:NE], float(NE), None, ALU.subtract))
            c.link(v.tensor_scalar(gran, iota_f[:, 0:EG], float(BS), None, ALU.mult))
            c.link(v.memset(carry_on, 1.0))
            c.link(v.memset(carry_on[:, :, 0], 0.0))
            v.wait_ge(b1_T_done, 1)
            v.tensor_copy(b1_T, bank[7][:, 0:NE * FC]).then_inc(b1_T_ready, 1)
            for part in range(2):
                v.wait_ge(normed, (part + 1) * NORM_HALF)
                stats(xn1, part)
            for part in range(2):
                scales(1, part)
            v.wait_ge(consts_in, 16 * 6)
            for n in range(NB // NORM_SET):
                rows = xn1[:, n * NORM_SET:(n + 1) * NORM_SET, :]
                v.wait_ge(normed, NB + (n + 1) * NORM_SET)
                c.link(v.tensor_tensor(rows, rows, gamma_bc.unsqueeze(1).broadcast_to([P, NORM_SET, F]),
                                       ALU.mult))
                v.tensor_tensor(rows, rows, beta_bc.unsqueeze(1).broadcast_to([P, NORM_SET, F]),
                                ALU.add).then_inc(xn1_ready, 1)

            def each_b(t):
                return t.unsqueeze(1).broadcast_to([P, NB, NE])

            def each_e(t):
                return t.unsqueeze(2).broadcast_to([P, NB, NE])

            v.wait_ge(logits_done, NB // 2)
            c.link(v.tensor_tensor(lg, bank[2][:, 0:NB * NE].rearrange("p (b e) -> p b e", e=NE),
                                   each_b(br_bc), ALU.add))
            for top, oh in ((top1, oh_a), (top2, oh_b)):
                c.link(v.tensor_reduce(top, lg, AX.X, ALU.max))
                c.link(v.tensor_tensor(eq, lg, each_e(top), ALU.is_equal))
                c.link(v.tensor_tensor(eq, eq, each_b(e_less), ALU.mult))
                c.link(v.tensor_reduce(tmp2, eq, AX.X, ALU.min))
                c.link(v.tensor_tensor(oh, each_b(e_less), each_e(tmp2), ALU.is_equal))
                if oh is oh_a:
                    c.link(v.scalar_tensor_tensor(lg, oh, -BIG, lg, ALU.mult, ALU.add))
            v.tensor_tensor(tmp1, top2, top1, ALU.subtract).then_inc(gap_ready, 1)
            c.link(v.tensor_tensor(mask, oh_a, oh_b, ALU.add))
            v.tensor_tensor(mask, mask, each_e(valid), ALU.mult).then_inc(mask_ready, 1)
            v.wait_ge(gap_exp, 1)
            c.link(v.tensor_scalar(w_a, w_b, 1.0, None, ALU.add))
            c.link(v.reciprocal(w_a, w_a))
            c.link(v.tensor_tensor(w_b, w_b, w_a, ALU.mult))
            v.wait_ge(ranks_done, 1)
            c.link(v.tensor_copy(tot, bank[4][:, 0:NB * NE].rearrange("p (b e) -> p b e", e=NE)))
            c.link(v.tensor_copy(rank, bank[3][:, 0:NB * NE].rearrange("p (b e) -> p b e", e=NE)))
            tot_eb = eq.rearrange("p b e -> p (b e)")
            c.link(v.tensor_copy(tot_eb.rearrange("p (e b) -> p e b", e=NE),
                                 tot.rearrange("p b e -> p e b")))
            c.link(v.tensor_tensor_scan(incl.rearrange("p e b -> p (e b)"),
                                        carry_on.rearrange("p e b -> p (e b)"), tot_eb, 0.0,
                                        ALU.mult, ALU.add))
            c.link(v.tensor_tensor(n_cmp, incl[:, :, NB - 1].unsqueeze(2).broadcast_to([P, NE, EG]),
                                   gran.unsqueeze(1).broadcast_to([P, NE, EG]), ALU.is_gt))
            c.link(v.tensor_reduce(n_blk, n_cmp, AX.X, ALU.add))
            c.link(v.tensor_tensor_scan(n_incl, ones[:, 0:NE], n_blk, 0.0, ALU.mult, ALU.add))
            c.link(v.tensor_tensor(n_excl, n_incl, n_blk, ALU.subtract))
            c.link(v.tensor_tensor(rank, rank, incl.rearrange("p e b -> p b e"), ALU.add))
            c.link(v.tensor_tensor(rank, rank, tot, ALU.subtract))
            c.link(v.scalar_tensor_tensor(pos_e, each_b(n_excl), float(BS), rank, ALU.mult, ALU.add))
            for k, oh in enumerate((oh_a, oh_b)):
                c.link(v.tensor_tensor(oh, oh, pos_e, ALU.mult))
                c.link(v.tensor_reduce(tmp2, oh, AX.X, ALU.add))
                c.link(v.tensor_copy(pos_i[:, k, :], tmp2))
            c.link(v.tensor_tensor(blk_cmp, n_excl[:, 1:NE].unsqueeze(1).broadcast_to([P, NBLK, NE - 1]),
                                   iota_f[:, 0:NBLK].unsqueeze(2).broadcast_to([P, NBLK, NE - 1]),
                                   ALU.is_le))
            c.link(v.tensor_reduce(blk_f, blk_cmp, AX.X, ALU.add))
            v.tensor_copy(blk_e, blk_f[0:1, :]).then_inc(pos_ready, 1)

            def pick_w1(j, u):
                e = v.value_load(blk_e[0:1, bass.ds(j, 1)], min_val=0, max_val=NE - 1)
                v.tensor_copy(w1_now[:, u, :, :].rearrange("p k h -> p (k h)"),
                              w1_all[:, bass.ds(e, 1), :].rearrange("p e w -> p (e w)"))\
                 .then_inc(w1_picked, 1)

            def turned_copy(j, u):
                v.wait_ge(xsT_done, j + 1)
                v.tensor_copy(xsT[:, u, :, :].rearrange("p k n -> p (k n)"), bank[u][:, :])\
                 .then_inc(xsT_copied, 1)

            def add_b2(j, u, n, first=False):
                e = v.value_load(blk_e[0:1, bass.ds(j, 1)], min_val=0, max_val=NE - 1)
                v.wait_ge(l2_done, j + 1)
                if not first:
                    v.wait_ge(y_stored[u], 16 * n)
                v.tensor_tensor(y_out[:, u, :, :], bank[6 + u][:, :].rearrange("p (m f) -> p m f", m=BM),
                                b2_bc[:, bass.ds(e, 1), :].broadcast_to([P, BM, F]), ALU.add)\
                 .then_inc(y_ready, 1)

            v.wait_ge(pos_ready, 1)
            v.wait_ge(w1_in, 16 * NE)
            pick_w1(0, 0)
            pick_w1(1, 1)
            turned_copy(0, 0)
            turned_copy(1, 1)
            v.wait_ge(l1_done, FC // 2)
            pick_w1(2, 0)
            turned_copy(2, 0)
            add_b2(0, 0, 0, first=True)
            v.wait_ge(l1_done, FC // 2 * 2)
            pick_w1(3, 1)
            turned_copy(3, 1)
            add_b2(1, 1, 0, first=True)
            with v.Fori(1, (NBLK - 2) // 2, 1) as i:
                v.wait_ge(l1_done, FC // 2 * (2 * i + 1))
                pick_w1(2 * i + 2, 0)
                turned_copy(2 * i + 2, 0)
                add_b2(2 * i, 0, i)
                v.wait_ge(l1_done, FC // 2 * (2 * i + 2))
                pick_w1(2 * i + 3, 1)
                turned_copy(2 * i + 3, 1)
                add_b2(2 * i + 1, 1, i)
            for j in range(2 * ((NBLK - 2) // 2), NBLK):
                if j + 2 < NBLK:
                    v.wait_ge(l1_done, FC // 2 * (j + 1))
                    pick_w1(j + 2, j % 2)
                    turned_copy(j + 2, j % 2)
                add_b2(j, j % 2, j // 2)
            def combine(b, u, n):
                row = x1[:, b, :]
                v.wait_ge(y_got[u], 16 * TOP * (n + 1))
                c.link(v.scalar_tensor_tensor(row, y_in[:, u, 0, :], w_a[:, b:b + 1], row,
                                              ALU.mult, ALU.add))
                v.scalar_tensor_tensor(row, y_in[:, u, 1, :], w_b[:, b:b + 1], row,
                                       ALU.mult, ALU.add).then_inc(combined, 1)

            for b in range(NB):
                combine(b, b % YS, b // YS)


_INS = ["x", "src", "dst", "L0_gnn_W", "L0_gnn_a_src", "L0_gnn_a_dst", "L0_ffn_gamma", "L0_ffn_beta",
        "L0_ffn_Wr", "L0_ffn_br", "L0_ffn_W1", "L0_ffn_b1", "L0_ffn_W2", "L0_ffn_b2"]


def kernel(**inputs):
    import numpy as _np
    import concourse.bacc as _bacc
    from concourse import mybir as _mybir
    from concourse.bass_utils import run_bass_kernel_spmd as _run

    nc = _bacc.Bacc("TRN2", target_bir_lowering=False, num_devices=1)
    arrays, args = {}, []
    for name in _INS:
        a = _np.ascontiguousarray(inputs[name])
        arrays[f"in_{name}"] = a
        args.append(nc.dram_tensor(f"in_{name}", a.shape, _mybir.dt.from_np(a.dtype), kind="ExternalInput").ap())
    x = inputs["x"]
    args.append(nc.dram_tensor("out", x.shape, _mybir.dt.from_np(_np.dtype("float32")), kind="ExternalOutput").ap())
    gat_moe_kernel(nc, *args)
    r = _run(nc, [arrays], core_ids=[0])
    return r.results[0]["out"]
```
